# Optimizing a Trainium2 kernel written in Bass

```python
import numpy as np
import jax
import jax.numpy as jnp

def _softmax(x, axis=-1):
    return jax.nn.softmax(x, axis=axis)

def _gelu(x):
    return jax.nn.gelu(x, approximate=True)

def _silu(x):
    return jax.nn.silu(x)

def _sigmoid(x):
    return jax.nn.sigmoid(x)

def _layernorm(x, axis=-1, eps=1e-05):
    m = jnp.mean(x, axis=axis, keepdims=True)
    v = jnp.var(x, axis=axis, keepdims=True)
    return (x - m) / jnp.sqrt(v + eps)

def _scatter_add(tgt, idx, src, axis=0):
    return tgt.at[idx].add(src)

def _segment_sum(src, seg, n):
    return jax.ops.segment_sum(src, seg, n)
kernel_name = 'mk_decoder_preln_d2_seqx_r8_998948'

def setup_inputs(seed: int=0):
    np.random.seed(seed)
    _w = jnp.asarray

    def _rec_inputs():
        import jax
        import jax.numpy as jnp
        _rk = jax.random.key(seed)
        x = -0.0002928 + 1 * jax.random.normal(jax.random.fold_in(_rk, 1), (8, 256, 128), jnp.float32)
        _lenS = 256 - jax.random.randint(jax.random.fold_in(_rk, 7), (8,), 0, max(1, 256 // 4) + 1, jnp.int32)
        _lenS2 = 256 - jax.random.randint(jax.random.fold_in(_rk, 8), (8,), 0, max(1, 256 // 4) + 1, jnp.int32)
        _ctx_1024P = jax.random.normal(jax.random.fold_in(_rk, 11), (8, 16, 128), jnp.float32)
        _ctx_1024c = jax.random.dirichlet(jax.random.fold_in(_rk, 511), 0.3 * jnp.ones((16,), jnp.float32), (8, 256))
        _ctx_1024t = jnp.einsum('bsk,bkd->bsd', _ctx_1024c, _ctx_1024P)
        _ctx_1024t = _ctx_1024t * jax.lax.rsqrt(jnp.mean(jnp.square(_ctx_1024t)) + 1e-12) * 0.953939
        ctx_1024 = -1.39393e-06 + 0.999914 * (_ctx_1024t + 0.3 * jax.random.normal(jax.random.fold_in(_rk, 611), (8, 256, 128), jnp.float32))
        _validS = jnp.arange(256)[None, :] < _lenS[:, None]
        _validS2 = jnp.arange(256)[None, :] < _lenS2[:, None]
        _causal = jnp.tril(jnp.ones((256, 256), dtype=bool))
        mask_BxS2_ik0 = jnp.where(jnp.broadcast_to(_validS2[:, :], (8, 256)), 0, 1).astype(jnp.int32)
        mask_BxSxS2_fk1 = jnp.where(jnp.broadcast_to(_validS2[:, None, :], (8, 256, 256)), 1.0, 0.0).astype(jnp.float32)
        return (x, ctx_1024, mask_BxS2_ik0, mask_BxSxS2_fk1)
    x, ctx_1024, mask_BxS2_ik0, mask_BxSxS2_fk1 = _rec_inputs()

    def _L0_attn_setup():
        import jax, jax.numpy as jnp
        import numpy as np
        MODEL_DIM = 128
        NUM_HEADS = 16
        HEAD_DIM = MODEL_DIM // NUM_HEADS
        EPS = 1e-12
        CHUNK = 128

        def _pos_elu(t):
            return jax.nn.elu(t) + 1.0

        def _linear_attention(q, k, v):
            b, h, l, d = q.shape
            nc = l // CHUNK
            qc = jnp.moveaxis(q.reshape(b, h, nc, CHUNK, d), 2, 0)
            kc = jnp.moveaxis(k.reshape(b, h, nc, CHUNK, d), 2, 0)
            vc = jnp.moveaxis(v.reshape(b, h, nc, CHUNK, d), 2, 0)
            mask = jnp.tril(jnp.ones((CHUNK, CHUNK), dtype=q.dtype))

            def step(carry, inp):
                S, z = carry
                qb, kb, vb = inp
                scores = jnp.einsum('bhcd,bhsd->bhcs', qb, kb) * mask
                num = jnp.einsum('bhcd,bhde->bhce', qb, S) + jnp.einsum('bhcs,bhse->bhce', scores, vb)
                den = jnp.einsum('bhcd,bhd->bhc', qb, z) + scores.sum(-1)
                out = num / den[..., None] + EPS
                S = S + jnp.einsum('bhsd,bhse->bhde', kb, vb)
                z = z + kb.sum(axis=2)
                return ((S, z), out)
            S0 = jnp.zeros((b, h, d, d), dtype=q.dtype)
            z0 = jnp.zeros((b, h, d), dtype=q.dtype)
            _, outs = jax.lax.scan(step, (S0, z0), (qc, kc, vc))
            return jnp.moveaxis(outs, 0, 1).transpose(0, 3, 1, 2, 4).reshape(b, h * 0 + l // l, 0, 0) if False else outs
        key = jax.random.key(seed)
        kx, kq, kk, kv, ko = jax.random.split(key, 5)
        b, l = (4, 512)
        x = jax.random.normal(kx, (b, l, MODEL_DIM), dtype=jnp.float32)
        Wq = 0.02 * jax.random.normal(kq, (MODEL_DIM, MODEL_DIM), dtype=jnp.float32)
        Wk = 0.02 * jax.random.normal(kk, (MODEL_DIM, MODEL_DIM), dtype=jnp.float32)
        Wv = 0.02 * jax.random.normal(kv, (MODEL_DIM, MODEL_DIM), dtype=jnp.float32)
        Wo = 0.02 * jax.random.normal(ko, (MODEL_DIM, MODEL_DIM), dtype=jnp.float32)
        return {'x': x, 'Wq': Wq, 'Wk': Wk, 'Wv': Wv, 'Wo': Wo}
    _L0_attn_all = _L0_attn_setup()
    _L0_attn_in = {k: v for k, v in _L0_attn_all.items() if k in ('Wq', 'Wk', 'Wv', 'Wo')}
    del _L0_attn_all

    def _L0_xattn_setup():
        import jax, jax.numpy as jnp
        import numpy as np
        E = 128
        H = 16
        D = E // H
        key = jax.random.key(seed)
        ks = jax.random.split(key, 8)
        B, Lq, Lkv = (2, 256, 256)
        scale = 1.0 / np.sqrt(E)
        return {'query': jax.random.normal(ks[0], (B, Lq, E), dtype=jnp.float32), 'key_value': jax.random.normal(ks[1], (B, Lkv, E), dtype=jnp.float32), 'mask': jax.random.randint(ks[2], (B, Lkv), 0, 2, dtype=jnp.int32), 'Wq': jax.random.normal(ks[3], (E, E), dtype=jnp.float32) * scale, 'bq': jnp.zeros((E,), dtype=jnp.float32), 'Wk': jax.random.normal(ks[4], (E, E), dtype=jnp.float32) * scale, 'bk': jnp.zeros((E,), dtype=jnp.float32), 'Wv': jax.random.normal(ks[5], (E, E), dtype=jnp.float32) * scale, 'bv': jnp.zeros((E,), dtype=jnp.float32), 'Wo': jax.random.normal(ks[6], (E, E), dtype=jnp.float32) * scale, 'bo': jnp.zeros((E,), dtype=jnp.float32)}
    _L0_xattn_all = _L0_xattn_setup()
    _L0_xattn_in = {k: v for k, v in _L0_xattn_all.items() if k in ('Wq', 'bq', 'Wk', 'bk', 'Wv', 'bv', 'Wo', 'bo')}
    del _L0_xattn_all

    def _L0_ffn_setup():
        import jax, jax.numpy as jnp
        import numpy as np
        HIDDEN = 128
        INNER = 512

        def _weight_quant(w):
            scale = 1.0 / jnp.clip(jnp.mean(jnp.abs(w)), 1e-05)
            wq = jnp.clip(jnp.round(w * scale), -1.0, 1.0) / scale
            return w + jax.lax.stop_gradient(wq - w)

        def _act_quant(x):
            scale = 127.0 / jnp.clip(jnp.max(jnp.abs(x), axis=-1, keepdims=True), 1e-05)
            xq = jnp.clip(jnp.round(x * scale), -128.0, 127.0) / scale
            return x + jax.lax.stop_gradient(xq - x)

        def _bitlinear(x, w):
            return jnp.einsum('bsi,oi->bso', _act_quant(x), _weight_quant(w))
        key = jax.random.key(seed)
        k0, k1, k2, k3 = jax.random.split(key, 4)
        x = jax.random.normal(k0, (4, 256, HIDDEN), dtype=jnp.float32)
        w_gate = jax.random.normal(k1, (INNER, HIDDEN), dtype=jnp.float32) / np.sqrt(HIDDEN)
        w_up = jax.random.normal(k2, (INNER, HIDDEN), dtype=jnp.float32) / np.sqrt(HIDDEN)
        w_down = jax.random.normal(k3, (HIDDEN, INNER), dtype=jnp.float32) / np.sqrt(INNER)
        return {'x': x, 'w_gate': w_gate, 'w_up': w_up, 'w_down': w_down}
    _L0_ffn_all = _L0_ffn_setup()
    _L0_ffn_in = {k: v for k, v in _L0_ffn_all.items() if k in ('w_gate', 'w_up', 'w_down')}
    del _L0_ffn_all

    def _L1_attn_setup():
        import jax, jax.numpy as jnp
        import numpy as np
        D_MODEL = 128
        N_BLOCKS = 4
        D_STATE = 16
        D_CONV = 4
        EXPAND = 2
        DT_RANK = 64
        D_INNER = EXPAND * D_MODEL
        BATCH = 2
        SEQLEN = 128

        def _layer_norm(x, w, b):
            m = jnp.mean(x, -1, keepdims=True)
            v = jnp.mean((x - m) ** 2, -1, keepdims=True)
            return (x - m) * jax.lax.rsqrt(v + 1e-05) * w + b

        def _selective_scan(u, dt, A, Bm, Cm, Dp):
            dA = jnp.exp(dt[..., None] * A)
            dBu = (dt * u)[..., None] * Bm[:, :, None, :]

            def step(h, inp):
                dA_t, dBu_t, C_t = inp
                h = dA_t * h + dBu_t
                y = jnp.einsum('ben,bn->be', h, C_t)
                return (h, y)
            h0 = jnp.zeros((u.shape[0], u.shape[2], A.shape[1]), u.dtype)
            xs = (jnp.moveaxis(dA, 1, 0), jnp.moveaxis(dBu, 1, 0), jnp.moveaxis(Cm, 1, 0))
            _, ys = jax.lax.scan(step, h0, xs)
            y = jnp.moveaxis(ys, 0, 1)
            return y + u * Dp

        def _mamba(x, in_w, cw, cb, xw, dtw, dtb, A_log, Dp, ow):
            L = x.shape[1]
            xz = x @ in_w
            u, z = jnp.split(xz, 2, axis=-1)
            K = cw.shape[1]
            up = jnp.pad(u, ((0, 0), (K - 1, 0), (0, 0)))
            conv = cb + sum((up[:, k:k + L, :] * cw[:, k] for k in range(K)))
            u = jax.nn.silu(conv)
            dbl = u @ xw
            dt = jax.nn.softplus(dbl[..., :DT_RANK] @ dtw + dtb)
            Bm = dbl[..., DT_RANK:DT_RANK + D_STATE]
            Cm = dbl[..., DT_RANK + D_STATE:]
            A = -jnp.exp(A_log)
            y = _selective_scan(u, dt, A, Bm, Cm, Dp)
            y = y * jax.nn.silu(z)
            return y @ ow

        def _forward(x, norm_w, norm_b, in_proj_w, conv_w, conv_b, xproj_w, dtproj_w, dtproj_b, A_log, skip_D, out_proj_w, fn_w, fn_b):
            for i in range(N_BLOCKS):
                h = _layer_norm(x, norm_w[i], norm_b[i])
                h = _mamba(h, in_proj_w[i], conv_w[i], conv_b[i], xproj_w[i], dtproj_w[i], dtproj_b[i], A_log[i], skip_D[i], out_proj_w[i])
                x = x + h
            return _layer_norm(x, fn_w, fn_b)
        key = jax.random.key(seed)
        ks = jax.random.split(key, 8)
        s = 0.02
        f = lambda k, sh: jax.random.normal(k, sh, dtype=jnp.float32) * s
        return {'x': jax.random.normal(ks[0], (BATCH, SEQLEN, D_MODEL), dtype=jnp.float32), 'norm_w': jnp.ones((N_BLOCKS, D_MODEL), jnp.float32), 'norm_b': jnp.zeros((N_BLOCKS, D_MODEL), jnp.float32), 'in_proj_w': f(ks[1], (N_BLOCKS, D_MODEL, 2 * D_INNER)), 'conv_w': f(ks[2], (N_BLOCKS, D_INNER, D_CONV)), 'conv_b': jnp.zeros((N_BLOCKS, D_INNER), jnp.float32), 'xproj_w': f(ks[3], (N_BLOCKS, D_INNER, DT_RANK + 2 * D_STATE)), 'dtproj_w': f(ks[4], (N_BLOCKS, DT_RANK, D_INNER)), 'dtproj_b': jnp.full((N_BLOCKS, D_INNER), -4.6, jnp.float32), 'A_log': jnp.tile(jnp.log(jnp.arange(1, D_STATE + 1, dtype=jnp.float32))[None, None, :], (N_BLOCKS, D_INNER, 1)), 'skip_D': jnp.ones((N_BLOCKS, D_INNER), jnp.float32), 'out_proj_w': f(ks[5], (N_BLOCKS, D_INNER, D_MODEL)), 'fn_w': jnp.ones((D_MODEL,), jnp.float32), 'fn_b': jnp.zeros((D_MODEL,), jnp.float32)}
    _L1_attn_all = _L1_attn_setup()
    _L1_attn_in = {k: v for k, v in _L1_attn_all.items() if k in ('norm_w', 'norm_b', 'in_proj_w', 'conv_w', 'conv_b', 'xproj_w', 'dtproj_w', 'dtproj_b', 'A_log', 'skip_D', 'out_proj_w', 'fn_w', 'fn_b')}
    del _L1_attn_all

    def _L1_xattn_setup():
        import jax, jax.numpy as jnp
        import numpy as np
        B, NQ, NK, E = (2, 256, 256, 128)
        NH, D = (16, 64)
        NEG = -100000000.0

        def _xavier(key, shape):
            std = np.sqrt(2.0 / (shape[-2] + shape[-1]))
            return jax.random.normal(key, shape, dtype=jnp.float32) * std
        key = jax.random.key(seed)
        ks = jax.random.split(key, 7)
        k_in = jax.random.normal(ks[0], (B, NK, E), dtype=jnp.float32)
        q_in = jax.random.normal(ks[1], (B, NQ, E), dtype=jnp.float32)
        mask = (jax.random.uniform(ks[2], (B, NQ, NK)) > 0.2).astype(jnp.float32)
        return {'key': k_in, 'query': q_in, 'mask': mask, 'w_q': _xavier(ks[3], (NH, E, D)), 'w_k': _xavier(ks[4], (NH, E, D)), 'w_v': _xavier(ks[5], (NH, E, D)), 'w_o': _xavier(ks[6], (NH, D, E))}
    _L1_xattn_all = _L1_xattn_setup()
    _L1_xattn_in = {k: v for k, v in _L1_xattn_all.items() if k in ('w_q', 'w_k', 'w_v', 'w_o')}
    del _L1_xattn_all

    def _L1_ffn_setup():
        import jax, jax.numpy as jnp
        import numpy as np
        TOP_K = 2
        key = jax.random.key(seed)
        ks = jax.random.split(key, 5)
        B, S, H, E = (2, 128, 128, 8)
        return {'hidden_states': jax.random.normal(ks[0], (B, S, H), dtype=jnp.float32), 'router_w': jax.random.normal(ks[1], (E, H), dtype=jnp.float32) * 0.02, 'router_b': jax.random.normal(ks[2], (E,), dtype=jnp.float32) * 0.02, 'expert_w': jax.random.normal(ks[3], (E, H, H), dtype=jnp.float32) * 0.02, 'expert_b': jax.random.normal(ks[4], (E, H), dtype=jnp.float32) * 0.02}
    _L1_ffn_all = _L1_ffn_setup()
    _L1_ffn_in = {k: v for k, v in _L1_ffn_all.items() if k in ('router_w', 'router_b', 'expert_w', 'expert_b')}
    del _L1_ffn_all
    return {'x': x, 'ctx_1024': ctx_1024, 'mask_BxS2_ik0': mask_BxS2_ik0, 'mask_BxSxS2_fk1': mask_BxSxS2_fk1, 'L0_attn_Wq': _L0_attn_in['Wq'], 'L0_attn_Wk': _L0_attn_in['Wk'], 'L0_attn_Wv': _L0_attn_in['Wv'], 'L0_attn_Wo': _L0_attn_in['Wo'], 'L0_xattn_Wq': _L0_xattn_in['Wq'], 'L0_xattn_bq': _L0_xattn_in['bq'], 'L0_xattn_Wk': _L0_xattn_in['Wk'], 'L0_xattn_bk': _L0_xattn_in['bk'], 'L0_xattn_Wv': _L0_xattn_in['Wv'], 'L0_xattn_bv': _L0_xattn_in['bv'], 'L0_xattn_Wo': _L0_xattn_in['Wo'], 'L0_xattn_bo': _L0_xattn_in['bo'], 'L0_ffn_w_gate': _L0_ffn_in['w_gate'], 'L0_ffn_w_up': _L0_ffn_in['w_up'], 'L0_ffn_w_down': _L0_ffn_in['w_down'], 'L1_attn_norm_w': _L1_attn_in['norm_w'], 'L1_attn_norm_b': _L1_attn_in['norm_b'], 'L1_attn_in_proj_w': _L1_attn_in['in_proj_w'], 'L1_attn_conv_w': _L1_attn_in['conv_w'], 'L1_attn_conv_b': _L1_attn_in['conv_b'], 'L1_attn_xproj_w': _L1_attn_in['xproj_w'], 'L1_attn_dtproj_w': _L1_attn_in['dtproj_w'], 'L1_attn_dtproj_b': _L1_attn_in['dtproj_b'], 'L1_attn_A_log': _L1_attn_in['A_log'], 'L1_attn_skip_D': _L1_attn_in['skip_D'], 'L1_attn_out_proj_w': _L1_attn_in['out_proj_w'], 'L1_attn_fn_w': _L1_attn_in['fn_w'], 'L1_attn_fn_b': _L1_attn_in['fn_b'], 'L1_xattn_w_q': _L1_xattn_in['w_q'], 'L1_xattn_w_k': _L1_xattn_in['w_k'], 'L1_xattn_w_v': _L1_xattn_in['w_v'], 'L1_xattn_w_o': _L1_xattn_in['w_o'], 'L1_ffn_router_w': _L1_ffn_in['router_w'], 'L1_ffn_router_b': _L1_ffn_in['router_b'], 'L1_ffn_expert_w': _L1_ffn_in['expert_w'], 'L1_ffn_expert_b': _L1_ffn_in['expert_b']}

def reference(x, ctx_1024, mask_BxS2_ik0, mask_BxSxS2_fk1, L0_attn_Wq, L0_attn_Wk, L0_attn_Wv, L0_attn_Wo, L0_xattn_Wq, L0_xattn_bq, L0_xattn_Wk, L0_xattn_bk, L0_xattn_Wv, L0_xattn_bv, L0_xattn_Wo, L0_xattn_bo, L0_ffn_w_gate, L0_ffn_w_up, L0_ffn_w_down, L1_attn_norm_w, L1_attn_norm_b, L1_attn_in_proj_w, L1_attn_conv_w, L1_attn_conv_b, L1_attn_xproj_w, L1_attn_dtproj_w, L1_attn_dtproj_b, L1_attn_A_log, L1_attn_skip_D, L1_attn_out_proj_w, L1_attn_fn_w, L1_attn_fn_b, L1_xattn_w_q, L1_xattn_w_k, L1_xattn_w_v, L1_xattn_w_o, L1_ffn_router_w, L1_ffn_router_b, L1_ffn_expert_w, L1_ffn_expert_b):
    import jax
    import jax.numpy as jnp

    def _L0_attn_ref(x, Wq, Wk, Wv, Wo):
        import jax, jax.numpy as jnp
        import numpy as np
        MODEL_DIM = 128
        NUM_HEADS = 16
        HEAD_DIM = MODEL_DIM // NUM_HEADS
        EPS = 1e-12
        CHUNK = 128

        def _pos_elu(t):
            return jax.nn.elu(t) + 1.0

        def _linear_attention(q, k, v):
            b, h, l, d = q.shape
            nc = l // CHUNK
            qc = jnp.moveaxis(q.reshape(b, h, nc, CHUNK, d), 2, 0)
            kc = jnp.moveaxis(k.reshape(b, h, nc, CHUNK, d), 2, 0)
            vc = jnp.moveaxis(v.reshape(b, h, nc, CHUNK, d), 2, 0)
            mask = jnp.tril(jnp.ones((CHUNK, CHUNK), dtype=q.dtype))

            def step(carry, inp):
                S, z = carry
                qb, kb, vb = inp
                scores = jnp.einsum('bhcd,bhsd->bhcs', qb, kb) * mask
                num = jnp.einsum('bhcd,bhde->bhce', qb, S) + jnp.einsum('bhcs,bhse->bhce', scores, vb)
                den = jnp.einsum('bhcd,bhd->bhc', qb, z) + scores.sum(-1)
                out = num / den[..., None] + EPS
                S = S + jnp.einsum('bhsd,bhse->bhde', kb, vb)
                z = z + kb.sum(axis=2)
                return ((S, z), out)
            S0 = jnp.zeros((b, h, d, d), dtype=q.dtype)
            z0 = jnp.zeros((b, h, d), dtype=q.dtype)
            _, outs = jax.lax.scan(step, (S0, z0), (qc, kc, vc))
            return jnp.moveaxis(outs, 0, 1).transpose(0, 3, 1, 2, 4).reshape(b, h * 0 + l // l, 0, 0) if False else outs
        b, l, D = x.shape
        h, d = (NUM_HEADS, HEAD_DIM)
        q = (x @ Wq.T).reshape(b, l, h, d).transpose(0, 2, 1, 3)
        k = (x @ Wk.T).reshape(b, l, h, d).transpose(0, 2, 1, 3)
        v = (x @ Wv.T).reshape(b, l, h, d).transpose(0, 2, 1, 3)
        q = _pos_elu(q)
        k = _pos_elu(k)
        outs = _linear_attention(q, k, v)
        nc = l // CHUNK
        attn = outs.transpose(1, 0, 3, 2, 4).reshape(b, l, D)
        return attn @ Wo.T

    def _L0_xattn_ref(query, key_value, mask, Wq, bq, Wk, bk, Wv, bv, Wo, bo):
        import jax, jax.numpy as jnp
        import numpy as np
        E = 128
        H = 16
        D = E // H
        B, Lq, _ = query.shape
        Lkv = key_value.shape[1]
        Q = (query @ Wq.T + bq).reshape(B, Lq, H, D)
        K = (key_value @ Wk.T + bk).reshape(B, Lkv, H, D)
        V = (key_value @ Wv.T + bv).reshape(B, Lkv, H, D)
        scores = jnp.einsum('bqhd,bkhd->bhqk', Q, K) / jnp.sqrt(jnp.float32(D))
        scores = jnp.where(mask[:, None, None, :] == 0, -jnp.inf, scores)
        probs = jax.nn.softmax(scores, axis=-1)
        context = jnp.einsum('bhqk,bkhd->bqhd', probs, V).reshape(B, Lq, E)
        return context @ Wo.T + bo

    def _L0_ffn_ref(x, w_gate, w_up, w_down):
        import jax, jax.numpy as jnp
        import numpy as np
        HIDDEN = 128
        INNER = 512

        def _weight_quant(w):
            scale = 1.0 / jnp.clip(jnp.mean(jnp.abs(w)), 1e-05)
            wq = jnp.clip(jnp.round(w * scale), -1.0, 1.0) / scale
            return w + jax.lax.stop_gradient(wq - w)

        def _act_quant(x):
            scale = 127.0 / jnp.clip(jnp.max(jnp.abs(x), axis=-1, keepdims=True), 1e-05)
            xq = jnp.clip(jnp.round(x * scale), -128.0, 127.0) / scale
            return x + jax.lax.stop_gradient(xq - x)

        def _bitlinear(x, w):
            return jnp.einsum('bsi,oi->bso', _act_quant(x), _weight_quant(w))
        gate = jax.nn.silu(_bitlinear(x, w_gate))
        up = _bitlinear(x, w_up)
        return _bitlinear(gate * up, w_down)

    def _L1_attn_ref(x, norm_w, norm_b, in_proj_w, conv_w, conv_b, xproj_w, dtproj_w, dtproj_b, A_log, skip_D, out_proj_w, fn_w, fn_b):
        import jax, jax.numpy as jnp
        import numpy as np
        D_MODEL = 128
        N_BLOCKS = 4
        D_STATE = 16
        D_CONV = 4
        EXPAND = 2
        DT_RANK = 64
        D_INNER = EXPAND * D_MODEL
        BATCH = 2
        SEQLEN = 128

        def _layer_norm(x, w, b):
            m = jnp.mean(x, -1, keepdims=True)
            v = jnp.mean((x - m) ** 2, -1, keepdims=True)
            return (x - m) * jax.lax.rsqrt(v + 1e-05) * w + b

        def _selective_scan(u, dt, A, Bm, Cm, Dp):
            dA = jnp.exp(dt[..., None] * A)
            dBu = (dt * u)[..., None] * Bm[:, :, None, :]

            def step(h, inp):
                dA_t, dBu_t, C_t = inp
                h = dA_t * h + dBu_t
                y = jnp.einsum('ben,bn->be', h, C_t)
                return (h, y)
            h0 = jnp.zeros((u.shape[0], u.shape[2], A.shape[1]), u.dtype)
            xs = (jnp.moveaxis(dA, 1, 0), jnp.moveaxis(dBu, 1, 0), jnp.moveaxis(Cm, 1, 0))
            _, ys = jax.lax.scan(step, h0, xs)
            y = jnp.moveaxis(ys, 0, 1)
            return y + u * Dp

        def _mamba(x, in_w, cw, cb, xw, dtw, dtb, A_log, Dp, ow):
            L = x.shape[1]
            xz = x @ in_w
            u, z = jnp.split(xz, 2, axis=-1)
            K = cw.shape[1]
            up = jnp.pad(u, ((0, 0), (K - 1, 0), (0, 0)))
            conv = cb + sum((up[:, k:k + L, :] * cw[:, k] for k in range(K)))
            u = jax.nn.silu(conv)
            dbl = u @ xw
            dt = jax.nn.softplus(dbl[..., :DT_RANK] @ dtw + dtb)
            Bm = dbl[..., DT_RANK:DT_RANK + D_STATE]
            Cm = dbl[..., DT_RANK + D_STATE:]
            A = -jnp.exp(A_log)
            y = _selective_scan(u, dt, A, Bm, Cm, Dp)
            y = y * jax.nn.silu(z)
            return y @ ow

        def _forward(x, norm_w, norm_b, in_proj_w, conv_w, conv_b, xproj_w, dtproj_w, dtproj_b, A_log, skip_D, out_proj_w, fn_w, fn_b):
            for i in range(N_BLOCKS):
                h = _layer_norm(x, norm_w[i], norm_b[i])
                h = _mamba(h, in_proj_w[i], conv_w[i], conv_b[i], xproj_w[i], dtproj_w[i], dtproj_b[i], A_log[i], skip_D[i], out_proj_w[i])
                x = x + h
            return _layer_norm(x, fn_w, fn_b)
        return _forward(x, norm_w, norm_b, in_proj_w, conv_w, conv_b, xproj_w, dtproj_w, dtproj_b, A_log, skip_D, out_proj_w, fn_w, fn_b)

    def _L1_xattn_ref(key, query, mask, w_q, w_k, w_v, w_o):
        import jax, jax.numpy as jnp
        import numpy as np
        B, NQ, NK, E = (2, 256, 256, 128)
        NH, D = (16, 64)
        NEG = -100000000.0

        def _xavier(key, shape):
            std = np.sqrt(2.0 / (shape[-2] + shape[-1]))
            return jax.random.normal(key, shape, dtype=jnp.float32) * std
        sqrt_d = jnp.sqrt(jnp.float32(D))
        q = jnp.einsum('blj,njd->bnld', query, w_q)
        k = jnp.einsum('blj,njd->bnld', key, w_k)
        v = jnp.einsum('blj,njd->bnld', key, w_v)
        score = jnp.einsum('bnid,bnkd->bnik', q, k) / sqrt_d
        m = mask[:, None]
        score = score * m + NEG * (1.0 - m)
        attn = jax.nn.softmax(score, axis=-1)
        out = jnp.einsum('bnij,bnjk->bnik', attn, v)
        out = jnp.einsum('bnlj,njk->blk', out, w_o)
        return out

    def _L1_ffn_ref(hidden_states, router_w, router_b, expert_w, expert_b):
        import jax, jax.numpy as jnp
        import numpy as np
        TOP_K = 2
        logits = jnp.einsum('bsh,eh->bse', hidden_states, router_w) + router_b
        routing_weights = jax.nn.softmax(logits, axis=-1)
        _, top_k_indices = jax.lax.top_k(routing_weights, TOP_K)
        E = router_w.shape[0]
        mask = jax.nn.one_hot(top_k_indices, E, dtype=hidden_states.dtype).sum(axis=-2)
        out = jnp.einsum('bse,ehd,bsd->bsh', mask, expert_w, hidden_states)
        out = out + jnp.einsum('bse,eh->bsh', mask, expert_b)
        return out
    x = x + _L0_attn_ref(_layernorm(x, axis=-1), L0_attn_Wq, L0_attn_Wk, L0_attn_Wv, L0_attn_Wo)
    x = x + _L0_xattn_ref(_layernorm(x, axis=-1), ctx_1024, mask_BxS2_ik0, L0_xattn_Wq, L0_xattn_bq, L0_xattn_Wk, L0_xattn_bk, L0_xattn_Wv, L0_xattn_bv, L0_xattn_Wo, L0_xattn_bo)
    x = x + _L0_ffn_ref(_layernorm(x, axis=-1), L0_ffn_w_gate, L0_ffn_w_up, L0_ffn_w_down)
    x = x + _L1_attn_ref(_layernorm(x, axis=-1), L1_attn_norm_w, L1_attn_norm_b, L1_attn_in_proj_w, L1_attn_conv_w, L1_attn_conv_b, L1_attn_xproj_w, L1_attn_dtproj_w, L1_attn_dtproj_b, L1_attn_A_log, L1_attn_skip_D, L1_attn_out_proj_w, L1_attn_fn_w, L1_attn_fn_b)
    x = x + _L1_xattn_ref(ctx_1024, _layernorm(x, axis=-1), mask_BxSxS2_fk1, L1_xattn_w_q, L1_xattn_w_k, L1_xattn_w_v, L1_xattn_w_o)
    x = x + _L1_ffn_ref(_layernorm(x, axis=-1), L1_ffn_router_w, L1_ffn_router_b, L1_ffn_expert_w, L1_ffn_expert_b)
    return x

_drawn_inputs = setup_inputs


def setup_inputs(seed=0):
    import zlib

    import numpy as np

    out = dict(_drawn_inputs(seed))
    spreads = {'L0_xattn_bq': (0.0, 0.297),
     'L0_xattn_bk': (0.0, 0.8),
     'L0_xattn_bv': (0.0, 0.1),
     'L0_xattn_bo': (0.0, 0.1),
     'L1_attn_norm_w': (1.0, 0.6),
     'L1_attn_norm_b': (0.0, 0.8),
     'L1_attn_conv_b': (0.0, 0.8),
     'L1_attn_dtproj_b': (-4.599999904632568, 0.6),
     'L1_attn_skip_D': (1.0, 0.6),
     'L1_attn_fn_w': (1.0, 0.2),
     'L1_attn_fn_b': (0.0, 0.1)}
    factors = {'L0_attn_Wq': 8.0,
     'L0_attn_Wk': 8.0,
     'L0_attn_Wv': 5.856,
     'L0_attn_Wo': 5.942,
     'L1_attn_in_proj_w': 8.0,
     'L1_attn_conv_w': 8.0,
     'L1_attn_xproj_w': 8.0,
     'L1_attn_dtproj_w': 8.0,
     'L1_attn_A_log': 8.0,
     'L1_attn_out_proj_w': 8.0,
     'L1_ffn_expert_b': 6.352}
    for name, (base, spread) in spreads.items():
        noise = np.random.default_rng([zlib.crc32(name.encode()), seed]).standard_normal(out[name].shape)
        drawn = base * np.exp(spread * noise) if base else spread * noise
        out[name] = jnp.asarray(drawn.astype(out[name].dtype))
    for name, factor in factors.items():
        out[name] = (out[name] * factor).astype(out[name].dtype)
    return out
```

```python
from contextlib import ExitStack

import concourse.bass as bass
from concourse import mybir

ALU = mybir.AluOpType
ACT = mybir.ActivationFunctionType
AX = mybir.AxisListType
F32 = mybir.dt.float32
BF16 = mybir.dt.bfloat16
I32 = mybir.dt.int32
ds = bass.ds

P = 128
B = 8
L = 256
T = B * L
NT = T // P
CH = 512
HALF = 1024
HB = HALF // L
NH = 16
ROUND = 12582912.0
MASKED = -1.0e30
F = 512
DI = 256
NS = 16
RANK = 64
TAPS = 4
NBLK = 4
NE = 8


class Chip:

    def __init__(self, nc, ctx):
        self.nc = nc
        self.ctx = ctx
        self.whole = ctx
        self.made = []

    def sb(self, name, shape, dt=F32):
        return self.ctx.enter_context(self.nc.sbuf_tensor(name, shape, dt))

    def psb(self, bank):
        return self.ps[:, bank, :].bitcast(BF16)


class Stage:

    def __init__(self, chip, name):
        self.nc, self.name, self.ctx = chip.nc, name, ExitStack()
        self.whole, self.made = chip.whole, chip.made

    def __enter__(self):
        self.ctx.__enter__()
        return self

    def __exit__(self, *a):
        return self.ctx.__exit__(*a)

    def sb(self, name, shape, dt=F32):
        return self.ctx.enter_context(self.nc.sbuf_tensor(f"{self.name}_{name}", shape, dt))

    def sem(self, name):
        made = self.whole.enter_context(self.nc.semaphore(f"{self.name}_{name}"))
        self.made.append(made)
        return made


def clear_semaphores(c):
    with c.nc.Block() as block:
        @block.gpsimd
        def _(pool):
            for made in c.made:
                pool.sem_clear(made)
    c.made = []


def constants(c):
    nc = c.nc
    c.ident = c.sb("ident", [P, P])
    c.identb = c.sb("identb", [P, P], BF16)
    c.centre = c.sb("centre", [P, P])
    c.average = c.sb("average", [P, P])
    c.ones_row = c.sb("ones_row", [P, P], BF16)
    c.ones_sq = c.sb("ones_sq", [P, P])
    c.eps = c.sb("eps", [P, 1])
    c.one = c.sb("one", [P, 1])
    with Stage(c, "const") as s:
        made = s.sem("made")
        with nc.Block() as block:
            @block.gpsimd
            def _(pool):
                pool.memset(c.ident[:, :], 0.0).then_inc(made, 1)
                pool.memset(c.average[:, :], 1.0 / P).then_inc(made, 1)
                pool.memset(c.centre[:, :], -1.0 / P).then_inc(made, 1)
                pool.memset(c.ones_row[:, :], 1.0).then_inc(made, 1)
                pool.memset(c.ones_sq[:, :], 1.0).then_inc(made, 1)
                pool.memset(c.eps[:, :], 1e-5).then_inc(made, 1)
                pool.memset(c.one[:, :], 1.0).then_inc(made, 1)
                pool.wait_ge(made, 7)
                pool.affine_select(out=c.ident[:, :], in_=c.ident[:, :], compare_op=ALU.not_equal, fill=1.0,
                                   base=0, pattern=[[-1, P]], channel_multiplier=1).then_inc(made, 1)
                pool.affine_select(out=c.centre[:, :], in_=c.centre[:, :], compare_op=ALU.not_equal,
                                   fill=1.0 - 1.0 / P, base=0, pattern=[[-1, P]],
                                   channel_multiplier=1).then_inc(made, 1)
                pool.wait_ge(made, 9)
                pool.tensor_copy(c.identb[:, :], c.ident[:, :]).then_inc(made, 1)
                pool.wait_ge(made, 10)


def load_stage(c, g):
    nc = c.nc
    with Stage(c, "load") as s:
        xt = s.sb("xt", [P, NT, P])
        ct = s.sb("ct", [P, NT, P])
        wa = s.sb("wa", [P, 8, P])
        wg = s.sb("wg", [P, 8, P])
        wd = s.sb("wd", [P, F])
        we = s.sb("we", [P, NE, P])
        wr = s.sb("wr", [NE, P])
        wq = s.sb("wq", [P, 3, 2 * F])
        part = s.sb("part", [P, 3])
        mean = s.sb("mean", [P, 3])
        wscale = s.sb("wscale", [P, 3])
        wgq = s.sb("wgq", [P, 8, P], BF16)
        wdq = s.sb("wdq", [P, F], BF16)

        acts_in, weights_in, small_in = s.sem("acts_in"), s.sem("weights_in"), s.sem("small_in")
        turned = s.sem("turned")
        copied_act, copied_dve = s.sem("copied_act"), s.sem("copied_dve")
        sums, mean_done, step, ternary = s.sem("sums"), s.sem("mean_done"), s.sem("step"), s.sem("ternary")
        padded, mask_read, mask_done = s.sem("padded"), s.sem("mask_read"), s.sem("mask_done")
        qturned, qcopied = s.sem("qturned"), s.sem("qcopied")
        mi = s.sb("mi", [P, B, L], I32)
        mcol = s.sb("mcol", [P, NT], I32)

        jobs = [(ct[:, t, :], P) for t in range(NT)] + [(xt[:, t, :], P) for t in range(NT)]
        jobs += [(wa[:, i, :], P) for i in range(8)] + [(we[:, e, :], P) for e in range(NE)] + [(wr[:, :], NE)]
        banks = [jobs[i:i + 4] for i in range(0, len(jobs), 4)]

        with nc.Block() as block:
            @block.sync
            def _(sp):
                sp.dma_start(ct[:, :, :], g["ctx"].rearrange("b (t p) d -> p (b t) d", p=P)).then_inc(acts_in, 16)
                sp.dma_start(xt[:, :, :], g["x"].rearrange("b (t p) d -> p (b t) d", p=P)).then_inc(acts_in, 16)
                sp.dma_start(we[:, :, :], g["ew"].rearrange("e h d -> h e d")).then_inc(weights_in, 16)
                sp.dma_start(wr[:, :], g["rw"]).then_inc(weights_in, 16)

            @block.scalar
            def _(act):
                for i, n in enumerate(("aq", "ak", "av", "ao", "xq", "xk", "xv", "xo")):
                    act.dma_start(wa[:, i, :], g[n]).then_inc(weights_in, 16)
                act.dma_start(wg[:, 0:4, :], g["wg"].rearrange("(t p) d -> p t d", p=P)).then_inc(weights_in, 16)
                act.dma_start(wg[:, 4:8, :], g["wu"].rearrange("(t p) d -> p t d", p=P)).then_inc(weights_in, 16)
                act.dma_start(wd[:, :], g["wd"]).then_inc(weights_in, 16)
                act.dma_start(mi[:, :, :], g["m0"].rearrange("(a b) k -> a b k", a=1).broadcast_to([P, B, L])
                              ).then_inc(mask_read, 16)
                act.dma_start(mcol[:, :], g["m0"].rearrange("b (t p) -> p (b t)", p=P),
                              allow_slow_non_contiguous=True).then_inc(mask_read, 16)
                for n in range(1, 8, 2):
                    act.wait_ge(turned, n + 1)
                    dst = c.cT if n < 4 else c.xT
                    act.activation(dst[:, (n % 4) * CH:(n % 4 + 1) * CH], c.ps[:, n % 4, :], ACT.Copy).then_inc(copied_act, 1)

            @block.gpsimd
            def _(pool):
                pool.memset(c.bqp[:, :, :], 0.0).then_inc(padded, 1)
                pool.wait_ge(padded, 1)
                for k, n in enumerate(("xbq", "xbk")):
                    for i in range(4):
                        pool.dma_start(c.bqp[32 * i:32 * i + 8, k, :],
                                       g[n].rearrange("(j i d) -> i d j", i=4, d=8)[i],
                                       allow_slow_non_contiguous=True).then_inc(small_in, 16)
                pool.dma_start(c.bv[:, :], g["xbv"].rearrange("(p a) -> p a", a=1)).then_inc(small_in, 16)
                pool.dma_start(c.bo[:, :], g["xbo"].rearrange("(p a) -> p a", a=1)).then_inc(small_in, 16)
                pool.dma_start(c.rb[:, :], g["rb"].rearrange("(a n) -> a n", a=1)).then_inc(small_in, 16)
                pool.dma_start(c.eb[:, :], g["eb"]).then_inc(small_in, 16)
                pool.memset(c.ones_f[:, :], 1.0).then_inc(padded, 1)
                pool.wait_ge(small_in, 16 * 12)

            @block.tensor
            def _(pe):
                pe.wait_ge(acts_in, 32)
                for n, bank in enumerate(banks):
                    if n == 8:
                        pe.wait_ge(weights_in, 16 * 13)
                    if n >= 4 and n < 12 and n % 2 == 1:
                        pe.wait_ge(copied_act, (n - 4) // 2 + 1)
                    elif 4 <= n < 12:
                        pe.wait_ge(copied_dve, (n - 4) // 2 + 1)
                    elif n >= 12:
                        pe.wait_ge(copied_dve, 4 + n - 11)
                    for k, (src, rows) in enumerate(bank):
                        mm = pe.transpose(c.ps[:, n % 4, k * P:k * P + rows], src, c.ident[0:rows, 0:rows])
                    mm.then_inc(turned, 1)
                pe.wait_ge(sums, 3)
                pe.matmul(c.ps[:, 4, 0:3], c.ones_sq[:, :], part[:, :], start=True, stop=True).then_inc(mean_done, 1)
                pe.wait_ge(ternary, 3)
                for n in range(8):
                    pe.transpose(c.psb(5)[:, n * P:(n + 1) * P], wgq[:, n, :], c.identb[:, :])
                for n in range(4):
                    mm = pe.transpose(c.psb(6)[:, n * P:(n + 1) * P], wdq[:, n * P:(n + 1) * P], c.identb[:, :])
                mm.then_inc(qturned, 1)

            @block.vector
            def _(dve):
                dve.memset(c.wpad[:, :, :], 0.0).then_inc(step, 1)
                for n in range(0, 8, 2):
                    dve.wait_ge(turned, n + 1)
                    dst = c.cT if n < 4 else c.xT
                    dve.tensor_copy(dst[:, (n % 4) * CH:(n % 4 + 1) * CH], c.ps[:, n % 4, :]).then_inc(copied_dve, 1)
                dve.wait_ge(mask_read, 32)
                dve.tensor_scalar(c.maskrow[:, :, :], mi[:, :, :], 0.0, MASKED, ALU.is_equal, ALU.mult).then_inc(mask_done, 1)
                dve.tensor_scalar(c.maskcol[:, :], mcol[:, :], 0.0, None, ALU.not_equal).then_inc(mask_done, 1)
                dve.wait_ge(step, 1)
                for n in (8, 9):
                    a = n - 8
                    dve.wait_ge(turned, n + 1)
                    for k in range(2):
                        dst = c.wpad[:, 2 * a + k, :].rearrange("p (j i d) -> p j i d", j=4, i=4)[:, :, :, 0:8]
                        src = c.ps[:, n % 4, k * P:(k + 1) * P].rearrange("p (j i d) -> p j i d", j=4, i=4)
                        dve.tensor_copy(dst, src).then_inc(step, 1)
                    dve.tensor_copy(c.wvo[:, 2 * a:2 * a + 2, :], c.ps[:, n % 4, 2 * P:4 * P]
                                    .rearrange("p (a d) -> p a d", a=2)).then_inc(copied_dve, 1)
                for n in (10, 11):
                    dve.wait_ge(turned, n + 1)
                    dve.tensor_copy(c.ewT[:, 4 * (n - 10):4 * (n - 10) + 4, :], c.ps[:, n % 4, :]
                                    .rearrange("p (a d) -> p a d", a=4)).then_inc(copied_dve, 1)
                dve.wait_ge(turned, 13)
                dve.tensor_copy(c.rwT[:, :], c.ps[:, 0, 0:NE]).then_inc(copied_dve, 1)
                dve.wait_ge(weights_in, 16 * 13)
                for k, src in enumerate((wg[:, 0:4, :], wg[:, 4:8, :], wd[:, :])):
                    dve.tensor_reduce(part[:, k:k + 1], src, AX.XY if k < 2 else AX.X, ALU.add,
                                      apply_absolute_value=True).then_inc(sums, 1)
                dve.wait_ge(mean_done, 1)
                dve.tensor_scalar(c.wmean[:, :], c.ps[:, 4, 0:3], 1.0 / (F * P), 1e-5, ALU.mult, ALU.max).then_inc(step, 1)
                dve.wait_ge(step, 6)
                dve.reciprocal(wscale[:, :], c.wmean[:, :]).then_inc(step, 1)
                dve.wait_ge(step, 7)
                for k, src in enumerate((wg[:, 0:4, :], wg[:, 4:8, :], wd[:, :])):
                    w = wq[:, k, 0:F]
                    if k < 2:
                        w = w.rearrange("p (t d) -> p t d", t=4)
                    dve.tensor_scalar(w, src, wscale[:, k:k + 1], ROUND, ALU.mult, ALU.add).then_inc(step, 1)
                dve.wait_ge(step, 10)
                dve.tensor_scalar(wq[:, :, F:2 * F], wq[:, :, 0:F], ROUND, 1.0, ALU.subtract, ALU.min).then_inc(step, 1)
                dve.wait_ge(step, 11)
                for k, dst in enumerate((wgq[:, 0:4, :], wgq[:, 4:8, :], wdq[:, :])):
                    w = wq[:, k, F:2 * F]
                    if k < 2:
                        w = w.rearrange("p (t d) -> p t d", t=4)
                    dve.tensor_scalar(dst, w, -1.0, None, ALU.max).then_inc(ternary, 1)
                dve.wait_ge(qturned, 1)
                dve.tensor_copy(c.wguT[:, :], c.psb(5)[:, 0:8 * P]).then_inc(qcopied, 1)
                dve.tensor_copy(c.wdT[:, :, :], c.psb(6)[:, 0:4 * P].rearrange("p (t d) -> p t d", t=4)).then_inc(qcopied, 1)
                dve.wait_ge(small_in, 16 * 12)
                dve.tensor_scalar(c.bqs[:, :], c.bqp[:, 0, :], 8.0 ** -0.5, None, ALU.mult).then_inc(qcopied, 1)


def norm_stage(c, name, src, dst, gain=None, bias=None, add_to=None):
    nc = c.nc
    with Stage(c, name) as s:
        sq = s.sb("sq", [P, T])
        lnv = s.sb("lnv", [P, T])
        rstd = s.sb("rstd", [P, T])
        centred, squared, var_done, lnv_done, rstd_done, scaled, done = c.norm_sems
        base = 4 * c.norms
        c.norms += 1
        with nc.Block() as block:
            @block.tensor
            def _(pe):
                for h in range(4):
                    pe.matmul(c.ps[:, h, :], c.centre[:, :], src[:, h * CH:(h + 1) * CH],
                              start=True, stop=True).then_inc(centred, 1)
                for h in range(4):
                    pe.wait_ge(squared, base + h + 1)
                    pe.matmul(c.ps[:, 4 + h, :], c.average[:, :], sq[:, h * CH:(h + 1) * CH],
                              start=True, stop=True).then_inc(var_done, 1)

            @block.scalar
            def _(act):
                for h in range(4):
                    act.wait_ge(centred, base + h + 1)
                    act.activation(sq[:, h * CH:(h + 1) * CH], c.ps[:, h, :], ACT.Square).then_inc(squared, 1)
                for h in range(4):
                    act.wait_ge(var_done, base + h + 1)
                    act.activation(lnv[:, h * CH:(h + 1) * CH], c.ps[:, 4 + h, :], ACT.Ln,
                                   bias=c.eps[:, 0:1]).then_inc(lnv_done, 1)
                    act.wait_ge(lnv_done, base + h + 1)
                    act.activation(rstd[:, h * CH:(h + 1) * CH], lnv[:, h * CH:(h + 1) * CH], ACT.Exp,
                                   scale=-0.5).then_inc(rstd_done, 1)

            @block.vector
            def _(dve):
                for h in range(4):
                    cols = slice(h * CH, (h + 1) * CH)
                    dve.wait_ge(rstd_done, base + h + 1)
                    if add_to is None and gain is None:
                        dve.tensor_tensor(dst[:, cols], c.ps[:, h, :], rstd[:, cols], ALU.mult).then_inc(done, 1)
                        continue
                    dve.tensor_tensor(sq[:, cols], c.ps[:, h, :], rstd[:, cols], ALU.mult).then_inc(scaled, 1)
                    dve.wait_ge(scaled, 2 * h + 1)
                    dve.tensor_scalar(lnv[:, cols], sq[:, cols], gain, bias, ALU.mult, ALU.add).then_inc(scaled, 1)
                    dve.wait_ge(scaled, 2 * h + 2)
                    dve.tensor_tensor(add_to[:, cols], add_to[:, cols], lnv[:, cols], ALU.add).then_inc(done, 1)


def linear_attention_stage(c):
    nc = c.nc
    D = P // NH
    with Stage(c, "la") as s:
        xb = s.sb("xb", [P, L])
        low = s.sb("low", [P, 2, 4, L])
        qk = s.sb("qk", [P, 2, 4, L])
        v = s.sb("v", [P, 2, NH, D + 1])
        sc = s.sb("sc", [P, 2, 3, P])
        tri = s.sb("tri", [P, 3, P])
        rec = s.sb("rec", [P, 2, NH])
        on = s.sb("on", [P, 2, NH, D])
        oT = s.sb("oT", [P, L])
        names = ("x_in proj v_proj low_done exp_done feat v_done scores sc_done pv rec_done on_done "
                 "turned oT_done out_done x_done ready tri_made").split()
        (x_in, proj, v_proj, low_done, exp_done, feat, v_done, scores, sc_done, pv, rec_done, on_done,
         turned, oT_done, out_done, x_done, ready, tri_made) = (s.sem(n) for n in names)
        with nc.Block() as block:
            @block.gpsimd
            def _(pool):
                pool.memset(tri[:, :, :], 1.0).then_inc(tri_made, 1)
                pool.memset(v[:, :, :, :], 1.0).then_inc(tri_made, 1)
                pool.wait_ge(tri_made, 2)
                for k in (0, 2):
                    pool.affine_select(out=tri[:, k, :], in_=tri[:, k, :], compare_op=ALU.is_ge, fill=0.0,
                                       base=0, pattern=[[1, P]], channel_multiplier=-1).then_inc(tri_made, 1)

            @block.scalar
            def _(act):
                act.sem_inc(x_done, 1)
                act.wait_ge(tri_made, 4)
                with act.Fori(0, B) as b:
                    act.wait_ge(x_done, b + 1)
                    act.activation(xb[:, :], c.xn[:, ds(b * L, L)], ACT.Copy).then_inc(x_in, 1)
                    for k in range(2):
                        act.wait_ge(low_done, b * 2 + k + 1)
                        act.activation(low[:, k, :, :], low[:, k, :, :], ACT.Exp).then_inc(exp_done, 1)
                    act.wait_ge(v_proj, b + 1)
                    act.activation(v[:, :, :, 0:D], c.ps[:, 4, 0:L].rearrange("p (t h d) -> p t h d", t=2, d=D),
                                   ACT.Copy).then_inc(v_done, 1)
                    act.wait_ge(turned, b + 1)
                    act.activation(oT[:, :], c.ps[:, 6, 0:L], ACT.Copy, ).then_inc(oT_done, 1)

            @block.tensor
            def _(pe):
                with pe.Fori(0, B) as b:
                    pe.wait_ge(x_in, b + 1)
                    for k in range(2):
                        for j in range(4):
                            mm = pe.matmul(c.ps[:, 2 * k + j // 2, (j % 2) * L:(j % 2 + 1) * L],
                                           c.wpad[:, k, j * P:(j + 1) * P], xb[:, :], start=True, stop=True)
                        mm.then_inc(proj, 1)
                    for t in range(2):
                        mm = pe.matmul(c.ps[:, 4, t * P:(t + 1) * P], xb[:, t * P:(t + 1) * P], c.wvo[:, 0, :],
                                       start=True, stop=True)
                    mm.then_inc(v_proj, 1)
                    pe.wait_ge(feat, b * 2 + 2)

                    def score(h):
                        j, r = divmod(h, 4)
                        bank = h % 2
                        if h >= 2:
                            pe.wait_ge(sc_done, b * NH + h - 1)
                        row = slice(32 * r, 32 * r + D)
                        pe.matmul(c.ps[:, bank, 0:L], qk[row, 1, j, 0:P], qk[row, 0, j, :], start=True, stop=True)
                        pe.matmul(c.ps[:, bank, L:L + P], qk[row, 1, j, P:L], qk[row, 0, j, P:L],
                                  start=True, stop=True).then_inc(scores, 1)

                    def outs(h):
                        if h == 0:
                            pe.wait_ge(v_done, b + 1)
                        pe.wait_ge(sc_done, b * NH + h + 1)
                        o = c.ps[:, 5, 0:2 * NH * (D + 1)].rearrange("p (t h d) -> p t h d", t=2, h=NH)
                        pe.matmul(o[:, 0, h, :], sc[:, h % 2, 0, :], v[:, 0, h, :], start=True, stop=True)
                        pe.matmul(o[:, 1, h, :], sc[:, h % 2, 1, :], v[:, 0, h, :], start=True, stop=False)
                        pe.matmul(o[:, 1, h, :], sc[:, h % 2, 2, :], v[:, 1, h, :],
                                  start=False, stop=True).then_inc(pv, 1)

                    score(0)
                    for h in range(NH):
                        if h + 1 < NH:
                            score(h + 1)
                        outs(h)
                    pe.wait_ge(on_done, b + 1)
                    for t in range(2):
                        mm = pe.transpose(c.ps[:, 6, t * P:(t + 1) * P], on[:, t, :, :].rearrange("p h d -> p (h d)"),
                                          c.ident[:, :])
                    mm.then_inc(turned, 1)
                    pe.wait_ge(oT_done, b + 1)
                    pe.matmul(c.ps[:, 7, 0:L], c.wvo[:, 1, :], oT[:, :], start=True, stop=True).then_inc(out_done, 1)

            @block.vector
            def _(dve):
                dve.wait_ge(tri_made, 4)
                with dve.Fori(0, B) as b:
                    for k in range(2):
                        dve.wait_ge(proj, b * 2 + k + 1)
                        bank = c.ps[:, 2 * k:2 * k + 2, :].rearrange("p a (j l) -> p (a j) l", j=2)
                        dve.tensor_scalar(low[:, k, :, :], bank, 0.0, None, ALU.min).then_inc(low_done, 1)
                    for k in range(2):
                        bank = c.ps[:, 2 * k:2 * k + 2, :].rearrange("p a (j l) -> p (a j) l", j=2)
                        dve.wait_ge(exp_done, b * 2 + k + 1)
                        dve.scalar_tensor_tensor(out=qk[:, k, :, :], in0=bank, scalar=0.0, in1=low[:, k, :, :],
                                                 op0=ALU.max, op1=ALU.add).then_inc(feat, 1)
                    for h in range(NH):
                        dve.wait_ge(scores, b * NH + h + 1)
                        if h >= 2:
                            dve.wait_ge(pv, b * NH + h - 1)
                        dve.tensor_tensor(sc[:, h % 2, :, :], c.ps[:, h % 2, 0:3 * P].rearrange("p (a q) -> p a q", a=3),
                                          tri[:, :, :], ALU.mult).then_inc(sc_done, 1)
                    dve.wait_ge(pv, b * NH + NH)
                    o = c.ps[:, 5, 0:2 * NH * (D + 1)].rearrange("p (t h d) -> p t h d", t=2, h=NH)
                    dve.reciprocal(rec[:, :, :], o[:, :, :, D]).then_inc(rec_done, 1)
                    dve.wait_ge(rec_done, b * 2 + 1)
                    dve.tensor_tensor(on[:, :, :, :], o[:, :, :, 0:D],
                                      rec[:, :, :].unsqueeze(3).broadcast_to([P, 2, NH, D]), ALU.mult).then_inc(rec_done, 1)
                    dve.wait_ge(rec_done, b * 2 + 2)
                    dve.tensor_scalar(on[:, :, :, :], on[:, :, :, :], 1e-12, None, ALU.add).then_inc(on_done, 1)
                    dve.wait_ge(out_done, b + 1)
                    dve.tensor_tensor(c.xT[:, ds(b * L, L)], c.xT[:, ds(b * L, L)], c.ps[:, 7, 0:L],
                                      ALU.add).then_inc(x_done, 1)


def cross_attention_stage(c, name, D, masked_rows, weights):
    nc = c.nc
    HPG = 2 if D == 64 else 4
    G = NH // HPG
    HS = P // HPG
    W = NH * D
    OG = W // P
    NI = 2 * NH // 2
    NU = NI // 2
    QB, VB = G // 2, max(1, 2 * W // CH)
    NP = 2 * QB + VB
    SCALE = float(D) ** -0.5
    if not masked_rows:
        wq, wk, wv, wo = weights
    with Stage(c, name) as s:
        xb = s.sb("xb", [P, 2, L])
        q = s.sb("q", [P, G, L])
        k = s.sb("k", [P, G, L])
        v = s.sb("v", [P, 2, NH, D + 1])
        mx = s.sb("mx", [P, 2, 2])
        pr = s.sb("pr", [P, 2, 2, L])
        pT = s.sb("pT", [P, 2, 2, 2, P])
        rec = s.sb("rec", [P, 2, 4])
        on = s.sb("on", [P, 2, W])
        oT = s.sb("oT", [P, OG, P])
        if masked_rows:
            m = s.sb("m", [P, 2, L])
            neg = s.sb("neg", [P, 2, L])
            sm = s.sb("sm", [P, 2, 2, L])
        else:
            mr = s.sb("mr", [P, L], BF16)
            mc = s.sb("mc", [P, 2])
        sems = ("x_in proj evac ones_set mask_in neg_done scores s_free times shifted max_done exp_done turned "
                "pT_done pv rec_done o_norm o_turned oT_done out_done x_done mcol_in").split()
        (x_in, proj, evac, ones_set, mask_in, neg_done, scores, s_free, times, shifted, max_done, exp_done,
         turned, pT_done, pv, rec_done, o_norm, o_turned, oT_done, out_done, x_done, mcol_in) = (
            s.sem(n) for n in sems)
        def heads(n):
            pair = n % (NH // 2)
            gp, r = divmod(pair, HPG)
            return [(HPG * (2 * gp + j) + r, 2 * gp + j, HS * r) for j in range(2)]

        if masked_rows:
            w_in = s.sem("w_in")
            wq, wk, wv = (s.sb(x, [P, W]) for x in ("wq", "wk", "wv"))
            wo = s.sb("wo", [P, W])
        with nc.Block() as block:
            if masked_rows:
                @block.sync
                def _(sp):
                    for w, src in zip((wq, wk, wv), weights[0:3]):
                        sp.dma_start(w[:, :].rearrange("e (n d) -> e n d", d=D),
                                     src.rearrange("n e d -> e n d")).then_inc(w_in, 16)
                    sp.dma_start(wo[:, :].rearrange("p (g e) -> p g e", e=P),
                                 weights[3].rearrange("(g a) d e -> (a d) g e", a=2)).then_inc(w_in, 16)
                    for q_ in range(2):
                        sp.dma_start(m[:, q_, :], c.mask1[0, q_ * P:(q_ + 1) * P, :]).then_inc(mask_in, 16)
                    with sp.Fori(1, B) as b:
                        sp.wait_ge(x_done, b * 2 + 2)
                        for q_ in range(2):
                            sp.dma_start(m[:, q_, :], c.mask1[ds(b, 1), q_ * P:(q_ + 1) * P, :]
                                         .rearrange("a p k -> (a p) k")).then_inc(mask_in, 16)

            @block.gpsimd
            def _(pool):
                pool.memset(v[:, :, :, D:D + 1], 1.0).then_inc(ones_set, 1)
                pool.memset(xb[:, :, 0:1], 0.0).then_inc(x_done, 1)
                pool.memset(xb[:, :, 1:2], 0.0).then_inc(x_done, 1)
                with pool.Fori(0, B) as b:
                    pool.wait_ge(x_done, b * 2 + 2)
                    pool.wait_ge(ones_set, 1)
                    pool.tensor_copy(xb[:, 0, :], c.xn[:, ds(b * L, L)]).then_inc(x_in, 1)
                    pool.tensor_copy(xb[:, 1, :], c.cT[:, ds(b * L, L)]).then_inc(x_in, 1)
                    if not masked_rows:
                        pool.tensor_copy(mr[:, :], c.maskrow[:, ds(b, 1), :].rearrange("p a k -> p (a k)")).then_inc(neg_done, 1)
                        pool.tensor_copy(mc[:, :], c.maskcol[:, ds(b * 2, 2)]).then_inc(mcol_in, 1)

            @block.tensor
            def _(pe):
                if masked_rows:
                    pe.wait_ge(w_in, 64)
                with pe.Fori(0, B) as b:
                    pe.wait_ge(x_in, b * 2 + 2)

                    for n in range(NP):
                        bank = c.ps[:, 6 + n % 2, :]
                        if n >= 2:
                            pe.wait_ge(evac, b * NP + n - 1)
                        if n < 2 * QB:
                            w = wq if n < QB else wk
                            for j in range(2):
                                gr = 2 * (n % QB) + j
                                mm = pe.matmul(bank[:, j * L:(j + 1) * L], w[:, gr * P:(gr + 1) * P],
                                               xb[:, 0 if n < QB else 1, :], start=True, stop=True)
                        elif W == P:
                            for t in range(2):
                                mm = pe.matmul(bank[:, t * P:(t + 1) * P], xb[:, 1, t * P:(t + 1) * P], wv,
                                               start=True, stop=True)
                        else:
                            t, half = divmod(n - 2 * QB, 2)
                            mm = pe.matmul(bank, xb[:, 1, t * P:(t + 1) * P], wv[:, half * CH:(half + 1) * CH],
                                           start=True, stop=True)
                        mm.then_inc(proj, 1)
                    pe.wait_ge(evac, b * NP + NP)
                    if not masked_rows:
                        pe.wait_ge(neg_done, b + 1)

                    def score(n):
                        qt = n // (NH // 2)
                        bank = c.ps[:, n % 2, :]
                        if n >= 2:
                            if masked_rows:
                                pe.wait_ge(s_free, b * NI + n - 1)
                            else:
                                pe.wait_ge(exp_done, b * 2 * NI + 2 * n - 2)
                        for j, (h, gr, row) in enumerate(heads(n)):
                            cols = bank[:, j * L:(j + 1) * L]
                            if not masked_rows:
                                pe.matmul(cols, c.ones_row[row:row + 1, :], mr[row:row + 1, :], start=True, stop=False)
                            mm = pe.matmul(cols, q[row:row + D, gr, qt * P:(qt + 1) * P], k[row:row + D, gr, :],
                                           start=masked_rows, stop=True)
                        mm.then_inc(scores, 1)

                    def turn(n):
                        pe.wait_ge(exp_done, b * 2 * NI + 2 * n + 2)
                        if n >= 2:
                            pe.wait_ge(pT_done, b * NI + n - 1)
                        for j in range(2):
                            for t in range(2):
                                mm = pe.transpose(c.ps[:, 2 + n % 2, (2 * j + t) * P:(2 * j + t + 1) * P],
                                                  pr[:, n % 2, j, t * P:(t + 1) * P], c.ident[:, :])
                        mm.then_inc(turned, 1)

                    def outs(n):
                        u = n // 2
                        if n % 2 == 0 and u >= 2:
                            pe.wait_ge(o_norm, b * NU + u - 1)
                        pe.wait_ge(pT_done, b * NI + n + 1)
                        for j, (h, gr, row) in enumerate(heads(n)):
                            at = (2 * (n % 2) + j) * (D + 1)
                            for t in range(2):
                                mm = pe.matmul(c.ps[:, 4 + u % 2, at:at + D + 1], pT[:, n % 2, j, t, :],
                                               v[:, t, h, :], start=(t == 0), stop=(t == 1))
                        mm.then_inc(pv, 1)

                    def project(qt):
                        pe.wait_ge(o_norm, b * NU + (qt + 1) * (NU // 2))
                        for gr in range(OG):
                            bank = 6 + (gr // 4) % 2
                            if OG > 4 and gr == 4:
                                mm.then_inc(o_turned, 1)
                            if gr == 0 and qt == 1:
                                pe.wait_ge(x_done, b * 2 + 3)
                            mm = pe.transpose(c.ps[:, bank, (gr % 4) * P:(gr % 4 + 1) * P],
                                              on[:, qt, gr * P:(gr + 1) * P], c.ident[:, :])
                        mm.then_inc(o_turned, 1)
                        nb = max(1, OG // 4)
                        pe.wait_ge(oT_done, b * 2 * nb + (qt + 1) * nb)
                        for gr in range(OG):
                            mm = pe.matmul(c.ps[:, 6, 0:P] if OG > 1 else c.ps[:, 7, 0:P],
                                           wo[:, gr * P:(gr + 1) * P], oT[:, gr, :],
                                           start=(gr == 0), stop=(gr == OG - 1))
                        mm.then_inc(out_done, 1)

                    for n in range(NI + 2):
                        if n < NI:
                            score(n)
                        if 1 <= n <= NI:
                            turn(n - 1)
                        if n >= 2:
                            outs(n - 2)
                            if n - 2 == NI // 2 + 1:
                                project(0)
                    project(1)

            def evacuate_turned(eng, b, n):
                eng.wait_ge(turned, b * NI + n + 1)
                if n >= 2:
                    eng.wait_ge(pv, b * NI + n - 1)
                src = c.ps[:, 2 + n % 2, :]
                dst = pT[:, n % 2, :, :, :].rearrange("p j t q -> p (j t q)")
                if masked_rows:
                    eng.activation(dst, src, ACT.Copy).then_inc(pT_done, 1)
                else:
                    eng.tensor_copy(dst, src).then_inc(pT_done, 1)

            @block.scalar
            def _(act):
                act.wait_ge(ones_set, 1)
                with act.Fori(0, B) as b:
                    for n in range(NP):
                        act.wait_ge(proj, b * NP + n + 1)
                        bank = c.ps[:, 6 + n % 2, :]
                        if n < 2 * QB:
                            gr = 2 * (n % QB)
                            if masked_rows:
                                dst = (q if n < QB else k)[:, gr:gr + 2, :].rearrange("p j l -> p (j l)")
                                act.activation(dst, bank, ACT.Copy, scale=SCALE if n < QB else 1.0).then_inc(evac, 1)
                            else:
                                dst = q if n < QB else k
                                bias = c.bqs if n < QB else c.bqp[:, 1, :]
                                for j in range(2):
                                    a = act.activation(dst[:, gr + j, :], bank[:, j * L:(j + 1) * L], ACT.Identity,
                                                       bias=bias[:, gr + j:gr + j + 1],
                                                       scale=SCALE if n < QB else 1.0)
                                a.then_inc(evac, 1)
                        elif masked_rows:
                            t, half = divmod(n - 2 * QB, 2)
                            act.activation(v[:, t, half * 8:half * 8 + 8, 0:D],
                                           bank.rearrange("p (h d) -> p h d", d=D), ACT.Copy).then_inc(evac, 1)
                        else:
                            act.wait_ge(mcol_in, b + 1)
                            for t in range(2):
                                act.activation(v[:, t, :, 0:D], bank[:, t * P:(t + 1) * P]
                                               .rearrange("p (h d) -> p h d", d=D), ACT.Copy, scale=mc[:, t:t + 1])
                                a = act.activation(v[:, t, :, D], c.ones_f[:, 0:NH], ACT.Copy, scale=mc[:, t:t + 1])
                            a.then_inc(evac, 1)
                    for n in range(NI):
                        if n >= 2:
                            act.wait_ge(turned, b * NI + n - 1)
                        act.wait_ge(max_done, b * NI + n + 1)
                        for j in range(2):
                            src = sm[:, n % 2, j, :] if masked_rows else c.ps[:, n % 2, j * L:(j + 1) * L]
                            act.activation(pr[:, n % 2, j, :], src, ACT.Exp,
                                           bias=mx[:, n % 2, j:j + 1]).then_inc(exp_done, 1)
                        if n >= 1 and masked_rows:
                            evacuate_turned(act, b, n - 1)
                    if masked_rows:
                        evacuate_turned(act, b, NI - 1)

            @block.vector
            def _(dve):
                def maximum(b, n):
                    qt = n // (NH // 2)
                    dve.wait_ge(scores, b * NI + n + 1)
                    bank = c.ps[:, n % 2, :].rearrange("p (j k) -> p j k", j=2)
                    if masked_rows:
                        if n >= 2:
                            dve.wait_ge(exp_done, b * 2 * NI + 2 * n - 2)
                        dve.tensor_tensor(sm[:, n % 2, :, :], bank,
                                          m[:, qt, :].unsqueeze(1).broadcast_to([P, 2, L]), ALU.mult).then_inc(s_free, 1)
                        dve.wait_ge(s_free, b * NI + n + 1)
                        dve.tensor_tensor(sm[:, n % 2, :, :], sm[:, n % 2, :, :],
                                          neg[:, qt, :].unsqueeze(1).broadcast_to([P, 2, L]), ALU.add).then_inc(shifted, 1)
                        dve.wait_ge(shifted, b * NI + n + 1)
                        dve.tensor_reduce(mx[:, n % 2, :], sm[:, n % 2, :, :], AX.X, ALU.max,
                                          negate=True).then_inc(max_done, 1)
                    else:
                        if n >= 2:
                            dve.wait_ge(exp_done, b * 2 * NI + 2 * n - 2)
                        dve.tensor_reduce(mx[:, n % 2, :], bank, AX.X, ALU.max, negate=True).then_inc(max_done, 1)

                def normalise(b, u):
                    dve.wait_ge(pv, b * NI + 2 * u + 2)
                    if u == 0:
                        dve.wait_ge(x_done, b * 2 + 2)
                    o = c.ps[:, 4 + u % 2, 0:4 * (D + 1)].rearrange("p (r j d) -> p r j d", r=2, j=2)
                    dve.reciprocal(rec[:, u % 2, :].rearrange("p (r j) -> p r j", r=2), o[:, :, :, D]).then_inc(rec_done, 1)
                    dve.wait_ge(rec_done, b * NU + u + 1)
                    qt, pair = divmod(2 * u, NH // 2)
                    gp, r = divmod(pair, HPG)
                    base = HPG * 2 * gp * D
                    dst = on[:, qt, base:base + 2 * HPG * D].rearrange("p (j r d) -> p r j d", j=2, r=HPG)[:, r:r + 2]
                    dve.tensor_tensor(dst, o[:, :, :, 0:D],
                                      rec[:, u % 2, :].rearrange("p (r j) -> p r j", r=2).unsqueeze(3)
                                      .broadcast_to([P, 2, 2, D]), ALU.mult).then_inc(o_norm, 1)

                def finish(b, qt):
                    nb = max(1, OG // 4)
                    for a in range(nb):
                        dve.wait_ge(o_turned, b * 2 * nb + qt * nb + a + 1)
                        if OG > 1:
                            dve.tensor_copy(oT[:, 4 * a:4 * a + 4, :],
                                            c.ps[:, 6 + a, :].rearrange("p (g q) -> p g q", g=4)).then_inc(oT_done, 1)
                        else:
                            dve.tensor_scalar(oT[:, 0, :], c.ps[:, 6, 0:P], c.bv[:, 0:1], None, ALU.add).then_inc(oT_done, 1)
                    dve.wait_ge(out_done, b * 2 + qt + 1)
                    cols = c.xT[:, ds(b * L + qt * P, P)]
                    if OG > 1:
                        dve.tensor_tensor(cols, cols, c.ps[:, 6, 0:P], ALU.add).then_inc(x_done, 1)
                    else:
                        dve.scalar_tensor_tensor(out=cols, in0=c.ps[:, 7, 0:P], scalar=c.bo[:, 0:1], in1=cols,
                                                 op0=ALU.add, op1=ALU.add).then_inc(x_done, 1)

                with dve.Fori(0, B) as b:
                    if masked_rows:
                        dve.wait_ge(mask_in, b * 32 + 32)
                        dve.tensor_scalar(neg[:, :, :], m[:, :, :], -1.0, 1.0, ALU.mult, ALU.add).then_inc(neg_done, 1)
                        dve.wait_ge(neg_done, b * 2 + 1)
                        dve.tensor_scalar(neg[:, :, :], neg[:, :, :], -1.0e8, None, ALU.mult).then_inc(neg_done, 1)
                        dve.wait_ge(neg_done, b * 2 + 2)
                    for n in range(NI):
                        if n == NI // 2 + 4:
                            finish(b, 0)
                        maximum(b, n)
                        if not masked_rows and n >= 1:
                            evacuate_turned(dve, b, n - 1)
                        if n >= 4 and n % 2 == 0:
                            normalise(b, n // 2 - 2)
                    if not masked_rows:
                        evacuate_turned(dve, b, NI - 1)
                    normalise(b, NU - 2)
                    normalise(b, NU - 1)
                    finish(b, 1)


def ffn_stage(c):
    nc = c.nc
    with Stage(c, "ffn") as s:
        xb = s.sb("xb", [P, P])
        ab = s.sb("ab", [P, 8])
        xr = s.sb("xr", [P, P])
        xq = s.sb("xq", [P, P], BF16)
        xqT = s.sb("xqT", [P, P], BF16)
        gate = s.sb("gate", [P, F])
        hid = s.sb("hid", [P, F])
        hr = s.sb("hr", [P, F])
        hq = s.sb("hq", [P, F], BF16)
        hqT = s.sb("hqT", [P, 4, P], BF16)
        y = s.sb("y", [P, P])
        names = "x_in turned st xq_done xqT_t xqT_done gu gate_done hq_done hqT_t hqT_done down y_done y_t x_done s_w".split()
        (x_in, turned, st, xq_done, xqT_t, xqT_done, gu, gate_done, hq_done, hqT_t, hqT_done, down, y_done, y_t,
         x_done, s_w) = (s.sem(n) for n in names)
        hq_step = s.sem("hq_step")
        with nc.Block() as block:
            @block.gpsimd
            def _(pool):
                pool.memset(xb[:, 0:1], 0.0).then_inc(x_done, 1)
                with pool.Fori(0, NT) as t:
                    pool.wait_ge(x_done, t + 1)
                    pool.wait_ge(x_done, 1)
                    pool.tensor_copy(xb[:, :], c.xn[:, ds(t * P, P)]).then_inc(x_in, 1)

            @block.tensor
            def _(pe):
                with pe.Fori(0, NT) as t:
                    pe.wait_ge(x_in, t + 1)
                    pe.transpose(c.ps[:, 0, 0:P], xb[:, :], c.ident[:, :]).then_inc(turned, 1)
                    pe.wait_ge(xq_done, t + 1)
                    pe.transpose(c.psb(1)[:, 0:P], xq[:, :], c.identb[:, :]).then_inc(xqT_t, 1)
                    pe.wait_ge(xqT_done, t + 1)
                    pe.matmul(c.ps[:, 2, :], xqT[:, :], c.wguT[:, 0:F], start=True, stop=True).then_inc(gu, 1)
                    pe.matmul(c.ps[:, 3, :], xqT[:, :], c.wguT[:, F:2 * F], start=True, stop=True).then_inc(gu, 1)
                    pe.wait_ge(hq_done, t + 1)
                    for k in range(4):
                        mm = pe.transpose(c.psb(4)[:, k * P:(k + 1) * P], hq[:, k * P:(k + 1) * P], c.identb[:, :])
                    mm.then_inc(hqT_t, 1)
                    pe.wait_ge(hqT_done, t + 1)
                    for k in range(4):
                        mm = pe.matmul(c.ps[:, 5, 0:P], hqT[:, k, :], c.wdT[:, k, :], start=(k == 0), stop=(k == 3))
                    mm.then_inc(down, 1)
                    pe.wait_ge(y_done, t + 1)
                    pe.transpose(c.ps[:, 6, 0:P], y[:, :], c.ident[:, :]).then_inc(y_t, 1)

            @block.scalar
            def _(act):
                with act.Fori(0, NT) as t:
                    act.wait_ge(xqT_t, t + 1)
                    act.activation(xqT[:, :], c.psb(1)[:, 0:P], ACT.Copy).then_inc(xqT_done, 1)
                    act.wait_ge(gu, 2 * t + 1)
                    act.wait_ge(s_w, t + 1)
                    act.activation(gate[:, :], c.ps[:, 2, :], ACT.Silu, scale=ab[:, 3:4]).then_inc(gate_done, 1)
                    act.wait_ge(hqT_t, t + 1)
                    act.activation(hqT[:, :, :].rearrange("p k q -> p (k q)"), c.psb(4)[:, 0:F], ACT.Copy).then_inc(hqT_done, 1)

            @block.vector
            def _(dve):
                STEPS = 7
                with dve.Fori(0, NT) as t:
                    dve.wait_ge(turned, t + 1)
                    dve.tensor_reduce(ab[:, 0:1], c.ps[:, 0, 0:P], AX.X, ALU.max, apply_absolute_value=True).then_inc(st, 1)
                    dve.wait_ge(st, t * STEPS + 1)
                    dve.tensor_scalar(ab[:, 1:2], ab[:, 0:1], 1e-5, 1.0 / 127.0, ALU.max, ALU.mult).then_inc(st, 1)
                    dve.wait_ge(st, t * STEPS + 2)
                    dve.reciprocal(ab[:, 2:3], ab[:, 1:2]).then_inc(st, 1)
                    dve.wait_ge(st, t * STEPS + 3)
                    dve.tensor_scalar(xr[:, :], c.ps[:, 0, 0:P], ab[:, 2:3], ROUND, ALU.mult, ALU.add).then_inc(st, 1)
                    dve.wait_ge(st, t * STEPS + 4)
                    dve.tensor_scalar(xq[:, :], xr[:, :], ROUND, None, ALU.subtract).then_inc(xq_done, 1)
                    dve.tensor_scalar(ab[:, 3:5], c.wmean[:, 0:2], ab[:, 1:2], None, ALU.mult).then_inc(s_w, 1)
                    dve.wait_ge(s_w, t + 1)
                    dve.wait_ge(gate_done, t + 1)
                    dve.wait_ge(gu, 2 * t + 2)
                    dve.scalar_tensor_tensor(out=hid[:, :], in0=c.ps[:, 3, :], scalar=ab[:, 4:5], in1=gate[:, :],
                                             op0=ALU.mult, op1=ALU.mult).then_inc(st, 1)
                    dve.wait_ge(st, t * STEPS + 5)
                    dve.tensor_reduce(ab[:, 5:6], hid[:, :], AX.X, ALU.max, apply_absolute_value=True).then_inc(st, 1)
                    dve.wait_ge(st, t * STEPS + 6)
                    dve.tensor_scalar(ab[:, 6:7], ab[:, 5:6], 1e-5, 1.0 / 127.0, ALU.max, ALU.mult).then_inc(st, 1)
                    dve.wait_ge(st, t * STEPS + 7)
                    dve.reciprocal(ab[:, 7:8], ab[:, 6:7]).then_inc(hq_step, 1)
                    dve.wait_ge(hq_step, 2 * t + 1)
                    dve.tensor_scalar(hr[:, :], hid[:, :], ab[:, 7:8], ROUND, ALU.mult, ALU.add).then_inc(hq_step, 1)
                    dve.wait_ge(hq_step, 2 * t + 2)
                    dve.tensor_scalar(hq[:, :], hr[:, :], ROUND, None, ALU.subtract).then_inc(hq_done, 1)
                    dve.wait_ge(down, t + 1)
                    dve.tensor_scalar(y[:, :], c.ps[:, 5, 0:P], ab[:, 6:7], c.wmean[:, 2:3], ALU.mult, ALU.mult).then_inc(y_done, 1)
                    dve.wait_ge(y_t, t + 1)
                    cols = c.xT[:, ds(t * P, P)]
                    dve.tensor_tensor(cols, cols, c.ps[:, 6, 0:P], ALU.add).then_inc(x_done, 1)



def mamba_stage(c, g):
    nc = c.nc
    PAD = TAPS - 1
    R = 4
    xm = c.xn
    with Stage(c, "ma") as s:
        w_in = s.sb("w_in", [P, 2 * DI])
        cw = s.sb("cw", [P, DI, TAPS])
        w_tap = s.sb("w_tap", [P, TAPS, DI])
        cb = s.sb("cb", [P, 2])
        w_x = s.sb("w_x", [P, 2, RANK + 2 * NS])
        w_bc = s.sb("w_bc", [P, 2, 3, 2 * NS])
        w_dt = s.sb("w_dt", [RANK, DI])
        dtb = s.sb("dtb", [P, 2])
        A = s.sb("A", [P, 2, NS])
        Al = s.sb("Al", [P, 2, NS])
        Dp = s.sb("Dp", [P, 2])
        dD = s.sb("dD", [P, 2, P])
        w_out = s.sb("w_out", [P, 2, P])
        nw = s.sb("nw", [P, 2])
        sel = s.sb("sel", [3 * 2 * NS, 2 * NS, P], BF16)
        hn = s.sb("hn", [P, B, PAD + L])
        u = s.sb("u", [P, 2, T])
        z = s.sb("z", [P, 2, T])
        bc = s.sb("bc", [3 * 2 * NS, T], BF16)
        dt = s.sb("dt", [P, 2, T])
        dtu = s.sb("dtu", [P, 2, T])
        dA = s.sb("dA", [P, R, HALF])
        hs = s.sb("hs", [P, R, HALF])
        Bs = s.sb("Bs", [P, 2, HALF])
        sq = hs[:, 0:2, :].rearrange("p a l -> p (a l)")
        rstd = hs[:, 2:4, :].rearrange("p a l -> p (a l)")
        dtr = hs[0:RANK, 0:2, :].rearrange("p a l -> p (a l)")
        bcr = hs[0:96, 2:4, :].rearrange("p a l -> p (a l)")

        names = ("early_in mid_in late_in consts tap_done dd_done a_step a_done xm_ready centred squared "
                 "var_done lnv_done rstd_done scaled hn_ready proj silu_done bc_ps dtr_ps bc_p1 bc_r bc_p2 bc_r2 "
                 "bc_done dtr_done dt_ps abs_done relu_done exp_done ln_done dt_done dtu_done b_ready bs_done "
                 "c_ready da_done dbu_done scan_done hc_done y_acc gated out_ps").split()
        (early_in, mid_in, late_in, consts, tap_done, dd_done, a_step, a_done, xm_ready, centred, squared,
         var_done, lnv_done, rstd_done, scaled, hn_ready, proj, silu_done, bc_ps, dtr_ps, bc_p1, bc_r, bc_p2, bc_r2,
         bc_done, dtr_done, dt_ps, abs_done, relu_done, exp_done, ln_done, dt_done, dtu_done, b_ready, bs_done,
         c_ready, da_done, dbu_done, scan_done, hc_done, y_acc, gated, out_ps) = (s.sem(n) for n in names)
        EARLY, MID, LATE = 5 * 16, 6 * 16, 3 * 16
        XM0, BS0, DBU0, HC0, SCAN0, Y0, DT0 = 2, 1, 4, 2, 4, 4, 2

        def pair(k, rows=P):
            return c.ps[0:rows, 2 * k:2 * k + 2, :].rearrange("p a l -> p (a l)")

        def half(gt):
            return slice(gt * HALF, (gt + 1) * HALF)

        def load_early(sp, i):
            sp.dma_start(w_in[:, :], g["m_in"][ds(i, 1)].rearrange("a p n -> (a p) n")).then_inc(early_in, 16)
            sp.dma_start(cw[:, :, :], g["m_cw"][ds(i, 1)].broadcast_to([P, DI, TAPS])).then_inc(early_in, 16)
            sp.dma_start(cb[:, :], g["m_cb"][ds(i, 1)].rearrange("a (h p) -> (a p) h", p=P),
                         allow_slow_non_contiguous=True).then_inc(early_in, 16)
            for k, n in enumerate(("m_nw", "m_nb")):
                sp.dma_start(nw[:, k:k + 1], g[n][ds(i, 1)].rearrange("a p -> p a"),
                             allow_slow_non_contiguous=True).then_inc(early_in, 16)

        def load_mid(sp, i):
            sp.dma_start(w_x[:, :, :], g["m_xw"][ds(i, 1)].rearrange("a (h p) n -> (a p) h n", p=P)).then_inc(mid_in, 16)
            for part in range(3):
                sp.dma_start(w_bc[:, :, part, :], g["m_xw"][ds(i, 1), :, RANK:RANK + 2 * NS]
                             .rearrange("a (h p) n -> (a p) h n", p=P)).then_inc(mid_in, 16)
            sp.dma_start(w_dt[:, :], g["m_dw"][ds(i, 1)].rearrange("a p n -> (a p) n")).then_inc(mid_in, 16)
            sp.dma_start(dtb[:, :], g["m_db"][ds(i, 1)].rearrange("a (h p) -> (a p) h", p=P),
                         allow_slow_non_contiguous=True).then_inc(mid_in, 16)

        def load_late(sp, i):
            sp.dma_start(Al[:, :, :], g["m_al"][ds(i, 1)].rearrange("a (h p) n -> (a p) h n", p=P)).then_inc(late_in, 16)
            sp.dma_start(Dp[:, :], g["m_D"][ds(i, 1)].rearrange("a (h p) -> (a p) h", p=P),
                         allow_slow_non_contiguous=True).then_inc(late_in, 16)
            sp.dma_start(w_out[:, :, :], g["m_ow"][ds(i, 1)].rearrange("a (h p) n -> (a p) h n", p=P)).then_inc(late_in, 16)

        with nc.Block() as block:
            @block.sync
            def _(sp):
                load_early(sp, 0)
                load_mid(sp, 0)
                load_late(sp, 0)
                with sp.Fori(1, NBLK) as i:
                    sp.wait_ge(silu_done, i * 8)
                    load_early(sp, i)
                    sp.wait_ge(dt_done, i * 4 + DT0)
                    load_mid(sp, i)
                    sp.wait_ge(xm_ready, i * 2 + XM0)
                    load_late(sp, i)

            @block.gpsimd
            def _(pool):
                pool.memset(hn[:, :, 0:PAD], 0.0).then_inc(consts, 1)
                pool.memset(dA[:, :, :], 0.0).then_inc(consts, 1)
                pool.memset(sel[:, :, :], 0.0).then_inc(consts, 1)
                for part in range(3):
                    pool.wait_ge(consts, 3 + part)
                    pool.affine_select(out=sel[:, :, :], in_=sel[:, :, :], compare_op=ALU.not_equal, fill=1.0,
                                       base=-2 * NS * part, pattern=[[-1, 2 * NS], [0, P]],
                                       channel_multiplier=1).then_inc(consts, 1)
                pool.sem_inc(dbu_done, DBU0)
                with pool.Fori(0, NBLK) as i:
                    pool.wait_ge(early_in, i * EARLY + EARLY)
                    for k in range(TAPS):
                        pool.tensor_tensor(w_tap[:, k, :], w_in[:, 0:DI], cw[:, :, k], ALU.mult).then_inc(tap_done, 1)
                    for gt in range(2):
                        with pool.Fori(0, NS // 2) as t:
                            for k in range(4):
                                if k % 2 == 0:
                                    pool.wait_ge(bs_done, i * 2 * NS + t * 2 + gt * NS + k // 2 + 1 + BS0)
                                pool.wait_ge(y_acc, i * 4 * NS + t * 4 + gt * 2 * NS + k + 1)
                                pool.tensor_tensor(hs[:, k, :], dtu[:, k % 2, half(gt)], Bs[:, k // 2, :],
                                                   ALU.mult).then_inc(dbu_done, 1)

            @block.tensor
            def _(pe):
                pe.sem_inc(y_acc, Y0)
                pe.wait_ge(consts, 6)
                with pe.Fori(0, NBLK) as i:
                    pe.wait_ge(xm_ready, i * 2 + XM0)
                    for h in range(4):
                        pe.matmul(c.ps[:, h, :], c.centre[:, :], xm[:, h * CH:(h + 1) * CH],
                                  start=True, stop=True).then_inc(centred, 1)
                    for h in range(4):
                        pe.wait_ge(squared, i * 4 + h + 1)
                        pe.matmul(c.ps[:, 4 + h, :], c.average[:, :], sq[:, h * CH:(h + 1) * CH],
                                  start=True, stop=True).then_inc(var_done, 1)
                    pe.wait_ge(hn_ready, i * 4 + 4)
                    pe.wait_ge(tap_done, i * TAPS + TAPS)
                    for k in range(8):
                        gt, m = divmod(k, 4)
                        if k >= 4:
                            pe.wait_ge(silu_done, i * 8 + k - 3)
                        for a in range(2):
                            b0 = gt * HB + a * 2
                            out = c.ps[:, 2 * m + a, :]
                            if m < 2:
                                mm = pe.matmul(out, w_in[:, DI + m * P:DI + (m + 1) * P], hn[:, b0:b0 + 2, PAD:PAD + L],
                                               start=True, stop=True)
                            else:
                                for t in range(TAPS):
                                    mm = pe.matmul(out, w_tap[:, t, (m - 2) * P:(m - 1) * P], hn[:, b0:b0 + 2, t:t + L],
                                                   start=(t == 0), stop=(t == TAPS - 1))
                        mm.then_inc(proj, 1)
                    pe.wait_ge(silu_done, i * 8 + 8)
                    pe.wait_ge(mid_in, i * MID + MID)
                    for gt in range(2):
                        for a in range(2):
                            cols = slice(gt * HALF + a * CH, gt * HALF + (a + 1) * CH)
                            for h in range(2):
                                mm = pe.matmul(c.ps[0:96, 2 * gt + a, :], w_bc[:, h, :, :].rearrange("p a n -> p (a n)"),
                                               u[:, h, cols], start=(h == 0), stop=(h == 1))
                        mm.then_inc(bc_ps, 1)
                        for a in range(2):
                            cols = slice(gt * HALF + a * CH, gt * HALF + (a + 1) * CH)
                            for h in range(2):
                                mm = pe.matmul(c.ps[0:RANK, 4 + 2 * gt + a, :], w_x[:, h, 0:RANK],
                                               u[:, h, cols], start=(h == 0), stop=(h == 1))
                        mm.then_inc(dtr_ps, 1)
                    pe.wait_ge(dtr_done, i * 2 + 2)
                    for gt in range(2):
                        if gt == 1:
                            pe.wait_ge(bc_r, i * 2 + 2)
                        for h in range(2):
                            for a in range(2):
                                cols = slice(gt * HALF + a * CH, gt * HALF + (a + 1) * CH)
                                mm = pe.matmul(c.ps[:, 4 - 4 * gt + 2 * h + a, :], w_dt[:, h * P:(h + 1) * P],
                                               dtr[:, cols], start=True, stop=True)
                            mm.then_inc(dt_ps, 1)
                    pe.wait_ge(relu_done, i * 4 + 4)
                    pe.wait_ge(bc_done, i * 2 + 2)
                    pe.wait_ge(dd_done, i * 2 + 2)
                    for gt in range(2):
                        if gt == 1:
                            pe.wait_ge(gated, i * 4 + 2)
                        for h in range(2):
                            for a in range(2):
                                cols = slice(gt * HALF + a * CH, gt * HALF + (a + 1) * CH)
                                pe.matmul(c.ps[:, 4 + 2 * h + a, :], dD[:, h, :], u[:, h, cols], start=True, stop=False,
                                          skip_group_check=True)

                        def spread(k, a, done):
                            for q in range(2):
                                mm = pe.matmul(c.ps[:, 2 * a + q, :], k,
                                               bc[:, gt * HALF + q * CH:gt * HALF + (q + 1) * CH],
                                               start=True, stop=True)
                            mm.then_inc(done, 1)

                        def spread_b(n, state):
                            pe.wait_ge(bs_done, state + BS0)
                            spread(sel[:, ds(n, 1), :].rearrange("p a q -> p (a q)"), 0, b_ready)

                        def spread_c(n, state):
                            pe.wait_ge(hc_done, state * 2 + HC0)
                            spread(sel[:, ds(n + NS, 1), :].rearrange("p a q -> p (a q)"), 1, c_ready)

                        def sum_y(slot, item):
                            pe.wait_ge(hc_done, item + 1 + HC0)
                            for q in range(2):
                                mm = pe.matmul(c.ps[:, 4 + 2 * (slot % 2) + q, :], c.ident[:, :],
                                               hs[:, slot, q * CH:(q + 1) * CH], start=False, stop=False,
                                               skip_group_check=True)
                            mm.then_inc(y_acc, 1)

                        first = i * 2 * NS + gt * NS
                        spread_b(0, first)
                        spread_b(1, first + 1)
                        spread_c(0, first)
                        with pe.Fori(0, NS // 2 - 1) as t:
                            for p in range(2):
                                state = i * 2 * NS + t * 2 + gt * NS + 1 + p
                                slot = 2 * p
                                spread_b(t * 2 + 2 + p, state + 1)
                                sum_y(slot, i * 4 * NS + t * 4 + gt * 2 * NS + 2 * p)
                                spread_c(t * 2 + 1 + p, state)
                                sum_y(slot + 1, i * 4 * NS + t * 4 + gt * 2 * NS + 2 * p + 1)
                        item = i * 4 * NS + gt * 2 * NS + 2 * (NS - 2)
                        sum_y(0, item)
                        spread_c(NS - 1, first + NS - 1)
                        sum_y(1, item + 1)
                        sum_y(2, item + 2)
                        sum_y(3, item + 3)
                    pe.wait_ge(gated, i * 4 + 4)
                    for gt in range(2):
                        for a in range(2):
                            cols = slice(gt * HALF + a * CH, gt * HALF + (a + 1) * CH)
                            for h in range(2):
                                mm = pe.matmul(c.ps[:, 2 * gt + a, :], w_out[:, h, :], z[:, h, cols],
                                               start=(h == 0), stop=(h == 1))
                        mm.then_inc(out_ps, 1)

            @block.scalar
            def _(act):
                act.sem_inc(bs_done, BS0)
                act.wait_ge(consts, 6)
                with act.Fori(0, NBLK) as i:
                    for h in range(4):
                        act.wait_ge(centred, i * 4 + h + 1)
                        act.activation(sq[:, h * CH:(h + 1) * CH], c.ps[:, h, :], ACT.Square).then_inc(squared, 1)
                    for h in range(4):
                        r = rstd[:, h * CH:(h + 1) * CH]
                        act.wait_ge(var_done, i * 4 + h + 1)
                        act.activation(r, c.ps[:, 4 + h, :], ACT.Ln, bias=c.eps[:, 0:1]).then_inc(lnv_done, 1)
                        act.wait_ge(lnv_done, i * 4 + h + 1)
                        act.activation(r, r, ACT.Exp, scale=-0.5).then_inc(rstd_done, 1)
                    act.wait_ge(late_in, i * LATE + LATE)
                    act.activation(A[:, :, :], Al[:, :, :], ACT.Exp).then_inc(a_step, 1)
                    act.wait_ge(a_step, i + 1)
                    act.activation(A[:, :, :], A[:, :, :], ACT.Copy, scale=-1.0).then_inc(a_done, 1)
                    for k in range(8):
                        gt, m = divmod(k, 4)
                        act.wait_ge(proj, i * 8 + k + 1)
                        if m < 2:
                            act.activation(z[:, m, half(gt)], pair(m), ACT.Silu).then_inc(silu_done, 1)
                        else:
                            act.activation(u[:, m - 2, half(gt)], pair(m), ACT.Silu,
                                           bias=cb[:, m - 2:m - 1]).then_inc(silu_done, 1)
                    for gt in range(2):
                        act.wait_ge(bc_ps, i * 2 + gt + 1)
                        act.activation(bc[:, half(gt)], pair(gt, 96), ACT.Copy).then_inc(bc_p1, 1)
                        act.wait_ge(dtr_ps, i * 2 + gt + 1)
                        act.activation(dtr[:, half(gt)], pair(2 + gt, RANK), ACT.Copy).then_inc(dtr_done, 1)
                    for gt in range(2):
                        act.wait_ge(bc_r, i * 2 + gt + 1)
                        act.activation(bc[32:64, half(gt)], bcr[32:64, half(gt)], ACT.Copy)
                        act.activation(bc[64:96, half(gt)], bcr[64:96, half(gt)], ACT.Copy).then_inc(bc_p2, 1)
                    for gt in range(2):
                        act.wait_ge(bc_r2, i * 2 + gt + 1)
                        act.activation(bc[64:96, half(gt)], bcr[64:96, half(gt)], ACT.Copy).then_inc(bc_done, 1)
                    for k in range(4):
                        gt, h = divmod(k, 2)
                        l = Bs[:, k % 2, :]
                        act.wait_ge(dt_ps, i * 4 + k + 1)
                        act.wait_ge(dt_done, i * 4 + k + 1)
                        act.activation(l, pair(2 - 2 * gt + h), ACT.Abs, bias=dtb[:, h:h + 1]).then_inc(abs_done, 1)
                        act.wait_ge(abs_done, i * 4 + k + 1)
                        act.activation(l, l, ACT.Exp, scale=-1.0).then_inc(exp_done, 1)
                        act.wait_ge(exp_done, i * 4 + k + 1)
                        act.activation(l, l, ACT.Ln, bias=c.one[:, 0:1]).then_inc(ln_done, 1)
                    act.wait_ge(dtu_done, i * 4 + 4)
                    act.wait_ge(a_done, i + 1)
                    for gt in range(2):
                        with act.Fori(0, NS // 2) as t:
                            for k in range(4):
                                item = i * 4 * NS + t * 4 + gt * 2 * NS + k
                                if k % 2 == 0:
                                    act.wait_ge(b_ready, i * 2 * NS + t * 2 + gt * NS + k // 2 + 1)
                                    act.wait_ge(dbu_done, item - 2 + DBU0)
                                    act.activation(Bs[:, k // 2, :], pair(0), ACT.Copy).then_inc(bs_done, 1)
                                act.wait_ge(scan_done, item + 1)
                                d = dA[:, k, :].rearrange("p (b l) -> p b l", l=L)[:, :, 1:L]
                                act.activation(d, dt[:, k % 2, half(gt)].rearrange("p (b l) -> p b l", l=L)[:, :, 1:L],
                                               ACT.Exp, scale=A[:, k % 2, ds(t * 2 + k // 2, 1)]).then_inc(da_done, 1)

            @block.vector
            def _(dve):
                dve.sem_inc(xm_ready, XM0)
                dve.sem_inc(dt_done, DT0)
                dve.sem_inc(scan_done, SCAN0)
                dve.sem_inc(hc_done, HC0)
                dve.wait_ge(consts, 6)
                with dve.Fori(0, NBLK) as i:
                    dve.wait_ge(late_in, i * LATE + LATE)
                    for h in range(2):
                        dve.tensor_scalar(dD[:, h, :], c.ident[:, :], Dp[:, h:h + 1], None, ALU.mult).then_inc(dd_done, 1)
                    dve.wait_ge(early_in, i * EARLY + EARLY)
                    for h in range(4):
                        x = sq[:, h * CH:(h + 1) * CH]
                        dve.wait_ge(rstd_done, i * 4 + h + 1)
                        dve.tensor_tensor(x, c.ps[:, h, :], rstd[:, h * CH:(h + 1) * CH], ALU.mult).then_inc(scaled, 1)
                        dve.wait_ge(scaled, i * 4 + h + 1)
                        dve.tensor_scalar(hn[:, 2 * h:2 * h + 2, PAD:PAD + L], x.rearrange("p (b l) -> p b l", l=L),
                                          nw[:, 0:1], nw[:, 1:2], ALU.mult, ALU.add).then_inc(hn_ready, 1)
                    for gt in range(2):
                        dve.wait_ge(bc_p1, i * 2 + gt + 1)
                        dve.tensor_tensor(bcr[:, half(gt)], pair(gt, 96), bc[:, half(gt)], ALU.subtract).then_inc(bc_r, 1)
                    for gt in range(2):
                        dve.wait_ge(bc_p2, i * 2 + gt + 1)
                        dve.tensor_tensor(bcr[64:96, half(gt)], bcr[64:96, half(gt)], bc[64:96, half(gt)],
                                          ALU.subtract).then_inc(bc_r2, 1)
                    for k in range(4):
                        gt, h = divmod(k, 2)
                        d = dt[:, h, half(gt)]
                        dve.wait_ge(abs_done, i * 4 + k + 1)
                        dve.tensor_scalar(d, pair(2 - 2 * gt + h), dtb[:, h:h + 1], 0.0, ALU.add, ALU.max).then_inc(relu_done, 1)
                        dve.wait_ge(relu_done, i * 4 + k + 1)
                        dve.wait_ge(ln_done, i * 4 + k + 1)
                        dve.tensor_tensor(d, d, Bs[:, k % 2, :], ALU.add).then_inc(dt_done, 1)
                        dve.wait_ge(dt_done, i * 4 + k + 1 + DT0)
                        dve.tensor_tensor(dtu[:, h, half(gt)], d, u[:, h, half(gt)], ALU.mult).then_inc(dtu_done, 1)
                    for gt in range(2):
                        with dve.Fori(0, NS // 2) as t:
                            for p in range(2):
                                item = i * 4 * NS + t * 4 + gt * 2 * NS + 2 * p
                                for h in range(2):
                                    k = 2 * p + h
                                    dve.wait_ge(da_done, item + h + 1)
                                    dve.wait_ge(dbu_done, item + h + 1 + DBU0)
                                    dve.tensor_tensor_scan(hs[:, k, :], dA[:, k, :], hs[:, k, :], 0.0,
                                                           ALU.mult, ALU.add).then_inc(scan_done, 1)
                                dve.wait_ge(c_ready, i * 2 * NS + t * 2 + gt * NS + p + 1)
                                for h in range(2):
                                    k = 2 * p + h
                                    dve.wait_ge(scan_done, item + h + 1 + SCAN0)
                                    dve.tensor_tensor(hs[:, k, :], hs[:, k, :], pair(1), ALU.mult).then_inc(hc_done, 1)
                        dve.wait_ge(y_acc, i * 4 * NS + (gt + 1) * 2 * NS + Y0)
                        for h in range(2):
                            dve.tensor_tensor(z[:, h, half(gt)], pair(2 + h), z[:, h, half(gt)], ALU.mult).then_inc(gated, 1)
                    for gt in range(2):
                        dve.wait_ge(out_ps, i * 2 + gt + 1)
                        dve.tensor_tensor(xm[:, half(gt)], xm[:, half(gt)], pair(gt), ALU.add).then_inc(xm_ready, 1)


def expert_stage(c):
    nc = c.nc
    xn = c.xn
    with Stage(c, "moe") as s:
        pr = s.sb("pr", [P, NT, NE])
        st = s.sb("st", [P, 3, NT])
        more = s.sb("more", [P, NT, NE, NE])
        same = s.sb("same", [P, NT, NE, NE])
        before = s.sb("before", [P, NE, NE])
        rank = s.sb("rank", [P, NT, NE])
        pick = s.sb("pick", [P, NT, NE])
        pT = s.sb("pT", [NE, T])
        pTb = s.sb("pTb", [NE, T], BF16)
        sel = s.sb("sel", [NE, NE, P], BF16)
        xe = s.sb("xe", [P, 2, HALF])
        consts, logits, step, exp_done, picked, turned, pT_done, spread, masked, used, acc = (s.sem(x) for x in (
            "consts", "logits", "step", "exp_done", "picked", "turned", "pT_done", "spread", "masked", "used", "acc"))
        out_done = s.sem("out_done")
        NI = 2 * NE

        def pair(k):
            return c.ps[:, 2 * k:2 * k + 2, :].rearrange("p a l -> p (a l)")

        with nc.Block() as block:
            @block.gpsimd
            def _(pool):
                pool.memset(before[:, :, :], 1.0).then_inc(consts, 1)
                pool.memset(sel[:, :, :], 0.0).then_inc(consts, 1)
                pool.wait_ge(consts, 2)
                pool.affine_select(out=before[:, :, :], in_=before[:, :, :], compare_op=ALU.is_gt, fill=0.0, base=0,
                                   pattern=[[1, NE], [-1, NE]], channel_multiplier=0).then_inc(consts, 1)
                pool.affine_select(out=sel[:, :, :], in_=sel[:, :, :], compare_op=ALU.not_equal, fill=1.0, base=0,
                                   pattern=[[-1, NE], [0, P]], channel_multiplier=1).then_inc(consts, 1)

            @block.tensor
            def _(pe):
                for t in range(NT):
                    pe.matmul(c.ps[:, 0, t * NE:(t + 1) * NE], xn[:, t * P:(t + 1) * P], c.rwT[:, :], start=True, stop=False)
                    mm = pe.matmul(c.ps[:, 0, t * NE:(t + 1) * NE], c.ones_f[0:1, :], c.rb[:, :], start=False, stop=True)
                mm.then_inc(logits, 1)
                pe.wait_ge(picked, 1)
                for t in range(NT):
                    mm = pe.transpose(c.ps[0:NE, 4 + t // 4, (t % 4) * P:(t % 4 + 1) * P], pick[:, t, :], c.ident[:, :])
                mm.then_inc(turned, 1)
                pe.wait_ge(consts, 4)
                pe.wait_ge(pT_done, 2)
                for a in range(4):
                    pe.matmul(c.ps[:, 4 + a, :], c.eb[:, :], pT[:, a * CH:(a + 1) * CH], start=True, stop=False,
                              skip_group_check=True)
                for n in range(NI + 1):
                    if n < NI:
                        gt, e = divmod(n, NE)
                        if n >= 2:
                            pe.wait_ge(masked, n - 1)
                        for a in range(2):
                            mm = pe.matmul(c.ps[:, 2 * (n % 2) + a, :], sel[:, e, :],
                                           pTb[:, gt * HALF + a * CH:gt * HALF + (a + 1) * CH], start=True, stop=True)
                        mm.then_inc(spread, 1)
                    if n >= 1:
                        gt, e = divmod(n - 1, NE)
                        pe.wait_ge(masked, n)
                        for a in range(2):
                            mm = pe.matmul(c.ps[:, 4 + 2 * gt + a, :], c.ewT[:, e, :],
                                           xe[:, (n - 1) % 2, a * CH:(a + 1) * CH], start=False, stop=(e == NE - 1),
                                           skip_group_check=True)
                        mm.then_inc(acc, 1)

            @block.scalar
            def _(act):
                act.wait_ge(step, 2)
                act.activation(pr[:, :, :], pr[:, :, :], ACT.Exp).then_inc(exp_done, 1)
                act.wait_ge(pT_done, 1)
                act.activation(pTb[:, :], pT[:, :], ACT.Copy).then_inc(pT_done, 1)

            @block.vector
            def _(dve):
                def each(x):
                    return x.unsqueeze(2).broadcast_to([P, NT, NE])
                lg = c.ps[:, 0, 0:NT * NE].rearrange("p (t e) -> p t e", e=NE)
                dve.wait_ge(logits, 1)
                dve.tensor_reduce(st[:, 0, :], lg, AX.X, ALU.max).then_inc(step, 1)
                dve.wait_ge(step, 1)
                dve.tensor_tensor(pr[:, :, :], lg, each(st[:, 0, :]), ALU.subtract).then_inc(step, 1)
                dve.wait_ge(exp_done, 1)
                dve.tensor_reduce(st[:, 1, :], pr[:, :, :], AX.X, ALU.add).then_inc(step, 1)
                dve.wait_ge(step, 3)
                dve.reciprocal(st[:, 2, :], st[:, 1, :]).then_inc(step, 1)
                dve.wait_ge(step, 4)
                dve.tensor_tensor(pr[:, :, :], pr[:, :, :], each(st[:, 2, :]), ALU.mult).then_inc(step, 1)
                dve.wait_ge(step, 5)
                dve.wait_ge(consts, 4)
                mine = pr[:, :, :].unsqueeze(3).broadcast_to([P, NT, NE, NE])
                other = pr[:, :, :].unsqueeze(2).broadcast_to([P, NT, NE, NE])
                dve.tensor_tensor(more[:, :, :, :], other, mine, ALU.is_gt).then_inc(step, 1)
                dve.tensor_tensor(same[:, :, :, :], other, mine, ALU.is_equal).then_inc(step, 1)
                dve.wait_ge(step, 7)
                flat = same[:, :, :, :].rearrange("p t e j -> p t (e j)")
                dve.tensor_tensor(flat, flat, before[:, :, :].rearrange("p e j -> p (e j)").unsqueeze(1)
                                  .broadcast_to([P, NT, NE * NE]), ALU.mult).then_inc(step, 1)
                dve.wait_ge(step, 8)
                dve.tensor_tensor(more[:, :, :, :], more[:, :, :, :], same[:, :, :, :], ALU.add).then_inc(step, 1)
                dve.wait_ge(step, 9)
                dve.tensor_reduce(rank[:, :, :], more[:, :, :, :], AX.X, ALU.add).then_inc(step, 1)
                dve.wait_ge(step, 10)
                dve.tensor_scalar(pick[:, :, :], rank[:, :, :], 1.5, None, ALU.is_lt).then_inc(picked, 1)
                dve.wait_ge(turned, 1)
                dve.tensor_copy(pT[:, :], c.ps[0:NE, 4:8, :].rearrange("p a l -> p (a l)")).then_inc(pT_done, 1)
                for n in range(NI):
                    gt = n // NE
                    dve.wait_ge(spread, n + 1)
                    if n >= 2:
                        dve.wait_ge(acc, n - 1)
                    dve.tensor_tensor(xe[:, n % 2, :], xn[:, gt * HALF:(gt + 1) * HALF], pair(n % 2),
                                      ALU.mult).then_inc(masked, 1)
                dve.wait_ge(acc, NI)
                for gt in range(2):
                    cols = slice(gt * HALF, (gt + 1) * HALF)
                    dve.tensor_tensor(c.xT[:, cols], c.xT[:, cols], pair(2 + gt), ALU.add).then_inc(out_done, 1)


def store_stage(c, g):
    nc = c.nc
    with Stage(c, "store") as s:
        o = s.sb("o", [P, NT, P])
        turned, copied, stored = s.sem("turned"), s.sem("copied"), s.sem("stored")
        out = g["out"].rearrange("b (t p) d -> p (b t) d", p=P)
        with nc.Block() as block:
            @block.tensor
            def _(pe):
                for n in range(4):
                    for k in range(4):
                        t = 4 * n + k
                        mm = pe.transpose(c.ps[:, n, k * P:(k + 1) * P], c.xT[:, t * P:(t + 1) * P], c.ident[:, :])
                    mm.then_inc(turned, 1)

            @block.vector
            def _(dve):
                for n in range(4):
                    dve.wait_ge(turned, n + 1)
                    dve.tensor_copy(o[:, 4 * n:4 * n + 4, :], c.ps[:, n, :].rearrange("p (k d) -> p k d", k=4)).then_inc(copied, 1)

            @block.sync
            def _(sp):
                for n in range(4):
                    sp.wait_ge(copied, n + 1)
                    sp.dma_start(out[:, 4 * n:4 * n + 4, :], o[:, 4 * n:4 * n + 4, :]).then_inc(stored, 16)
                sp.wait_ge(stored, 64)


def decoder_kernel(nc, g):
    with ExitStack() as ctx:
        c = Chip(nc, ctx)
        c.ps = ctx.enter_context(nc.psum_tensor("ps", [P, 8, CH], F32))
        c.xT = c.sb("xT", [P, T])
        c.cT = c.sb("cT", [P, T])
        c.xn = c.sb("xn", [P, T])
        c.mask1 = g["m1"]
        c.norm_sems = [ctx.enter_context(nc.semaphore(f"norm_{n}")) for n in ("centred", "squared", "var_done", "lnv_done", "rstd_done",
                                                    "scaled", "done")]
        c.norms = 0
        with ExitStack() as layer0:
            c.ctx = ctx
            c.ewT = c.sb("ewT", [P, NE, P])
            c.rwT = c.sb("rwT", [P, NE])
            c.rb = c.sb("rb", [1, NE])
            c.eb = c.sb("eb", [NE, P])
            c.ones_f = c.sb("ones_f", [P, P])
            c.wmean = c.sb("wmean", [P, 3])
            constants(c)
            c.made = []
            c.ctx = layer0
            c.wpad = c.sb("wpad", [P, 4, CH])
            c.wvo = c.sb("wvo", [P, 4, P])
            c.bqp = c.sb("bqp", [P, 2, 4])
            c.bqs = c.sb("bqs", [P, 4])
            c.bv = c.sb("bv", [P, 1])
            c.bo = c.sb("bo", [P, 1])
            c.maskrow = c.sb("maskrow", [P, B, L], BF16)
            c.maskcol = c.sb("maskcol", [P, NT])
            c.wguT = c.sb("wguT", [P, 2 * F], BF16)
            c.wdT = c.sb("wdT", [P, 4, P], BF16)
            c.whole = layer0
            load_stage(c, g)
            norm_stage(c, "n1", c.xT, c.xn)
            linear_attention_stage(c)
            norm_stage(c, "n2", c.xT, c.xn)
            cross_attention_stage(c, "x0", P // NH, False, (c.wpad[:, 2, :], c.wpad[:, 3, :], c.wvo[:, 2, :], c.wvo[:, 3, :]))
            norm_stage(c, "n3", c.xT, c.xn)
            ffn_stage(c)
            clear_semaphores(c)
        c.whole = ctx
        norm_stage(c, "n4", c.xT, c.xn)
        mamba_stage(c, g)
        with ExitStack() as last:
            c.ctx = last
            fn = c.sb("fn", [P, 2])
            with Stage(c, "fn") as s:
                fn_in = s.sem("in")
                with nc.Block() as block:
                    @block.sync
                    def _(sp):
                        for k, n in enumerate(("m_fw", "m_fb")):
                            sp.dma_start(fn[:, k:k + 1], g[n].rearrange("(p a) -> p a", a=1)).then_inc(fn_in, 16)
                        sp.wait_ge(fn_in, 32)
            norm_stage(c, "n5", c.xn, None, fn[:, 0:1], fn[:, 1:2], c.xT)
        norm_stage(c, "n6", c.xT, c.xn)
        cross_attention_stage(c, "x1", 64, True, (g["x1q"], g["x1k"], g["x1v"], g["x1o"]))
        norm_stage(c, "n7", c.xT, c.xn)
        expert_stage(c)
        store_stage(c, g)


_NAMES = {
    "x": "x", "ctx_1024": "ctx", "mask_BxS2_ik0": "m0", "mask_BxSxS2_fk1": "m1",
    "L0_attn_Wq": "aq", "L0_attn_Wk": "ak", "L0_attn_Wv": "av", "L0_attn_Wo": "ao",
    "L0_xattn_Wq": "xq", "L0_xattn_bq": "xbq", "L0_xattn_Wk": "xk", "L0_xattn_bk": "xbk",
    "L0_xattn_Wv": "xv", "L0_xattn_bv": "xbv", "L0_xattn_Wo": "xo", "L0_xattn_bo": "xbo",
    "L0_ffn_w_gate": "wg", "L0_ffn_w_up": "wu", "L0_ffn_w_down": "wd",
    "L1_attn_norm_w": "m_nw", "L1_attn_norm_b": "m_nb", "L1_attn_in_proj_w": "m_in", "L1_attn_conv_w": "m_cw",
    "L1_attn_conv_b": "m_cb", "L1_attn_xproj_w": "m_xw", "L1_attn_dtproj_w": "m_dw", "L1_attn_dtproj_b": "m_db",
    "L1_attn_A_log": "m_al", "L1_attn_skip_D": "m_D", "L1_attn_out_proj_w": "m_ow", "L1_attn_fn_w": "m_fw",
    "L1_attn_fn_b": "m_fb", "L1_xattn_w_q": "x1q", "L1_xattn_w_k": "x1k", "L1_xattn_w_v": "x1v",
    "L1_xattn_w_o": "x1o", "L1_ffn_router_w": "rw", "L1_ffn_router_b": "rb", "L1_ffn_expert_w": "ew",
    "L1_ffn_expert_b": "eb",
}


def kernel(**inputs):
    import numpy as _np
    import concourse.bacc as _bacc
    from concourse import mybir as _mybir
    from concourse.bass_utils import run_bass_kernel_spmd as _run

    nc = _bacc.Bacc("TRN2", target_bir_lowering=False, num_devices=1)
    arrays, g = {}, {}
    for name, short in _NAMES.items():
        a = _np.ascontiguousarray(inputs[name])
        arrays[f"in_{name}_dram"] = a
        g[short] = nc.dram_tensor(f"in_{name}_dram", a.shape, _mybir.dt.from_np(a.dtype), kind="ExternalInput").ap()
    g["out"] = nc.dram_tensor("out_0_dram", (B, L, P), _mybir.dt.float32, kind="ExternalOutput").ap()
    decoder_kernel(nc, g)
    r = _run(nc, [arrays], core_ids=[0])
    return r.results[0]["out_0_dram"]
```

```python
from contextlib import ExitStack

import concourse.bass as bass
from concourse import mybir

ALU = mybir.AluOpType
ACT = mybir.ActivationFunctionType
AX = mybir.AxisListType
F32 = mybir.dt.float32
BF16 = mybir.dt.bfloat16
I32 = mybir.dt.int32
ds = bass.ds

P = 128
B = 8
L = 256
T = B * L
NT = T // P
CH = 512
HALF = 1024
HB = HALF // L
NH = 16
ROUND = 12582912.0
MASKED = -1.0e30
F = 512
DI = 256
NS = 16
RANK = 64
TAPS = 4
NBLK = 4
NE = 8


class Chip:

    def __init__(self, nc, ctx):
        self.nc = nc
        self.ctx = ctx
        self.whole = ctx
        self.made = []

    def sb(self, name, shape, dt=F32):
        return self.ctx.enter_context(self.nc.sbuf_tensor(name, shape, dt))

    def psb(self, bank):
        return self.ps[:, bank, :].bitcast(BF16)


class Stage:

    def __init__(self, chip, name):
        self.nc, self.name, self.ctx = chip.nc, name, ExitStack()
        self.whole, self.made = chip.whole, chip.made

    def __enter__(self):
        self.ctx.__enter__()
        return self

    def __exit__(self, *a):
        return self.ctx.__exit__(*a)

    def sb(self, name, shape, dt=F32):
        return self.ctx.enter_context(self.nc.sbuf_tensor(f"{self.name}_{name}", shape, dt))

    def sem(self, name):
        made = self.whole.enter_context(self.nc.semaphore(f"{self.name}_{name}"))
        self.made.append(made)
        return made


def clear_semaphores(c):
    with c.nc.Block() as block:
        @block.gpsimd
        def _(pool):
            for made in c.made:
                pool.sem_clear(made)
    c.made = []


def constants(c):
    nc = c.nc
    c.ident = c.sb("ident", [P, P])
    c.identb = c.sb("identb", [P, P], BF16)
    c.centre = c.sb("centre", [P, P])
    c.average = c.sb("average", [P, P])
    c.ones_row = c.sb("ones_row", [P, P], BF16)
    c.ones_sq = c.sb("ones_sq", [P, P])
    c.eps = c.sb("eps", [P, 1])
    c.one = c.sb("one", [P, 1])
    with Stage(c, "const") as s:
        made = s.sem("made")
        with nc.Block() as block:
            @block.gpsimd
            def _(pool):
                pool.memset(c.ident[:, :], 0.0).then_inc(made, 1)
                pool.memset(c.average[:, :], 1.0 / P).then_inc(made, 1)
                pool.memset(c.centre[:, :], -1.0 / P).then_inc(made, 1)
                pool.memset(c.ones_row[:, :], 1.0).then_inc(made, 1)
                pool.memset(c.ones_sq[:, :], 1.0).then_inc(made, 1)
                pool.memset(c.eps[:, :], 1e-5).then_inc(made, 1)
                pool.memset(c.one[:, :], 1.0).then_inc(made, 1)
                pool.wait_ge(made, 7)
                pool.affine_select(out=c.ident[:, :], in_=c.ident[:, :], compare_op=ALU.not_equal, fill=1.0,
                                   base=0, pattern=[[-1, P]], channel_multiplier=1).then_inc(made, 1)
                pool.affine_select(out=c.centre[:, :], in_=c.centre[:, :], compare_op=ALU.not_equal,
                                   fill=1.0 - 1.0 / P, base=0, pattern=[[-1, P]],
                                   channel_multiplier=1).then_inc(made, 1)
                pool.wait_ge(made, 9)
                pool.tensor_copy(c.identb[:, :], c.ident[:, :]).then_inc(made, 1)
                pool.wait_ge(made, 10)


def load_stage(c, g):
    nc = c.nc
    with Stage(c, "load") as s:
        xt = s.sb("xt", [P, NT, P])
        ct = s.sb("ct", [P, NT, P])
        wa = s.sb("wa", [P, 8, P])
        wg = s.sb("wg", [P, 8, P])
        wd = s.sb("wd", [P, F])
        we = s.sb("we", [P, NE, P])
        wr = s.sb("wr", [NE, P])
        wq = s.sb("wq", [P, 3, 2 * F])
        part = s.sb("part", [P, 3])
        mean = s.sb("mean", [P, 3])
        wscale = s.sb("wscale", [P, 3])
        wgq = s.sb("wgq", [P, 8, P], BF16)
        wdq = s.sb("wdq", [P, F], BF16)

        acts_in, weights_in, small_in = s.sem("acts_in"), s.sem("weights_in"), s.sem("small_in")
        turned = s.sem("turned")
        copied_act, copied_dve = s.sem("copied_act"), s.sem("copied_dve")
        sums, mean_done, step, ternary = s.sem("sums"), s.sem("mean_done"), s.sem("step"), s.sem("ternary")
        padded, mask_read, mask_done = s.sem("padded"), s.sem("mask_read"), s.sem("mask_done")
        qturned, qcopied = s.sem("qturned"), s.sem("qcopied")
        mi = s.sb("mi", [P, B, L], I32)
        absent = s.sb("absent", [P, B])

        jobs = [(ct[:, t, :], P) for t in range(NT)] + [(xt[:, t, :], P) for t in range(NT)]
        jobs += [(wa[:, i, :], P) for i in range(8)] + [(we[:, e, :], P) for e in range(NE)] + [(wr[:, :], NE)]
        banks = [jobs[i:i + 4] for i in range(0, len(jobs), 4)]

        with nc.Block() as block:
            @block.sync
            def _(sp):
                sp.dma_start(ct[:, :, :], g["ctx"].rearrange("b (t p) d -> p (b t) d", p=P)).then_inc(acts_in, 16)
                sp.dma_start(xt[:, :, :], g["x"].rearrange("b (t p) d -> p (b t) d", p=P)).then_inc(acts_in, 16)
                sp.dma_start(we[:, :, :], g["ew"].rearrange("e h d -> h e d")).then_inc(weights_in, 16)
                sp.dma_start(wr[:, :], g["rw"]).then_inc(weights_in, 16)

            @block.scalar
            def _(act):
                for i, n in enumerate(("aq", "ak", "av", "ao", "xq", "xk", "xv", "xo")):
                    act.dma_start(wa[:, i, :], g[n]).then_inc(weights_in, 16)
                act.dma_start(wg[:, 0:4, :], g["wg"].rearrange("(t p) d -> p t d", p=P)).then_inc(weights_in, 16)
                act.dma_start(wg[:, 4:8, :], g["wu"].rearrange("(t p) d -> p t d", p=P)).then_inc(weights_in, 16)
                act.dma_start(wd[:, :], g["wd"]).then_inc(weights_in, 16)
                act.dma_start(mi[:, :, :], g["m0"].rearrange("(a b) k -> a b k", a=1).broadcast_to([P, B, L])
                              ).then_inc(mask_read, 16)
                for n in range(1, 8, 2):
                    act.wait_ge(turned, n + 1)
                    dst = c.cT if n < 4 else c.xT
                    act.activation(dst[:, (n % 4) * CH:(n % 4 + 1) * CH], c.ps[:, n % 4, :], ACT.Copy).then_inc(copied_act, 1)

            @block.gpsimd
            def _(pool):
                for k, n in enumerate(("xbq", "xbk")):
                    pool.dma_start(c.bqk[:, k:k + 1], g[n].rearrange("(p a) -> p a", a=1)).then_inc(small_in, 16)
                pool.dma_start(c.bv[:, :], g["xbv"].rearrange("(p a) -> p a", a=1)).then_inc(small_in, 16)
                pool.dma_start(c.bo[:, :], g["xbo"].rearrange("(p a) -> p a", a=1)).then_inc(small_in, 16)
                pool.dma_start(c.rb[:, :], g["rb"].rearrange("(a n) -> a n", a=1)).then_inc(small_in, 16)
                pool.dma_start(c.eb[:, :], g["eb"]).then_inc(small_in, 16)
                pool.memset(c.ones_f[:, :], 1.0).then_inc(padded, 1)
                pool.wait_ge(small_in, 16 * 6)

            @block.tensor
            def _(pe):
                pe.wait_ge(acts_in, 32)
                for n, bank in enumerate(banks):
                    if n == 8:
                        pe.wait_ge(weights_in, 16 * 13)
                    if n >= 4 and n < 12 and n % 2 == 1:
                        pe.wait_ge(copied_act, (n - 4) // 2 + 1)
                    elif 4 <= n < 12:
                        pe.wait_ge(copied_dve, (n - 4) // 2 + 1)
                    elif n >= 12:
                        pe.wait_ge(copied_dve, 4 + n - 11)
                    for k, (src, rows) in enumerate(bank):
                        mm = pe.transpose(c.ps[:, n % 4, k * P:k * P + rows], src, c.ident[0:rows, 0:rows])
                    mm.then_inc(turned, 1)
                pe.wait_ge(sums, 3)
                pe.matmul(c.ps[:, 4, 0:3], c.ones_sq[:, :], part[:, :], start=True, stop=True).then_inc(mean_done, 1)
                pe.wait_ge(ternary, 3)
                for n in range(8):
                    pe.transpose(c.psb(5)[:, n * P:(n + 1) * P], wgq[:, n, :], c.identb[:, :])
                for n in range(4):
                    mm = pe.transpose(c.psb(6)[:, n * P:(n + 1) * P], wdq[:, n * P:(n + 1) * P], c.identb[:, :])
                mm.then_inc(qturned, 1)

            @block.vector
            def _(dve):
                for n in range(0, 8, 2):
                    dve.wait_ge(turned, n + 1)
                    dst = c.cT if n < 4 else c.xT
                    dve.tensor_copy(dst[:, (n % 4) * CH:(n % 4 + 1) * CH], c.ps[:, n % 4, :]).then_inc(copied_dve, 1)
                dve.wait_ge(mask_read, 16)
                dve.tensor_scalar(c.maskrow[:, :, :], mi[:, :, :], 0.0, MASKED, ALU.is_equal, ALU.mult).then_inc(mask_done, 1)
                dve.wait_ge(mask_done, 1)
                dve.tensor_reduce(c.present[:, :], c.maskrow[:, :, :], AX.X, ALU.max).then_inc(mask_done, 1)
                dve.wait_ge(mask_done, 2)
                dve.tensor_scalar(c.present[:, :], c.present[:, :], 0.0, None, ALU.is_equal).then_inc(mask_done, 1)
                dve.wait_ge(mask_done, 3)
                dve.reciprocal(absent[:, :], c.present[:, :]).then_inc(mask_done, 1)
                dve.wait_ge(mask_done, 4)
                dve.tensor_tensor(c.present[:, :], c.present[:, :], absent[:, :], ALU.mult).then_inc(mask_done, 1)
                for n in (8, 9):
                    a = n - 8
                    dve.wait_ge(turned, n + 1)
                    dve.tensor_copy(c.wqk[:, 2 * a:2 * a + 2, :], c.ps[:, n % 4, 0:2 * P]
                                    .rearrange("p (a d) -> p a d", a=2)).then_inc(step, 1)
                    dve.tensor_copy(c.wvo[:, 2 * a:2 * a + 2, :], c.ps[:, n % 4, 2 * P:4 * P]
                                    .rearrange("p (a d) -> p a d", a=2)).then_inc(copied_dve, 1)
                for n in (10, 11):
                    dve.wait_ge(turned, n + 1)
                    dve.tensor_copy(c.ewT[:, 4 * (n - 10):4 * (n - 10) + 4, :], c.ps[:, n % 4, :]
                                    .rearrange("p (a d) -> p a d", a=4)).then_inc(copied_dve, 1)
                dve.wait_ge(turned, 13)
                dve.tensor_copy(c.rwT[:, :], c.ps[:, 0, 0:NE]).then_inc(copied_dve, 1)
                dve.wait_ge(weights_in, 16 * 13)
                for k, src in enumerate((wg[:, 0:4, :], wg[:, 4:8, :], wd[:, :])):
                    dve.tensor_reduce(part[:, k:k + 1], src, AX.XY if k < 2 else AX.X, ALU.add,
                                      apply_absolute_value=True).then_inc(sums, 1)
                dve.wait_ge(mean_done, 1)
                dve.tensor_scalar(c.wmean[:, :], c.ps[:, 4, 0:3], 1.0 / (F * P), 1e-5, ALU.mult, ALU.max).then_inc(step, 1)
                dve.wait_ge(step, 3)
                dve.reciprocal(wscale[:, :], c.wmean[:, :]).then_inc(step, 1)
                dve.wait_ge(step, 4)
                for k, src in enumerate((wg[:, 0:4, :], wg[:, 4:8, :], wd[:, :])):
                    w = wq[:, k, 0:F]
                    if k < 2:
                        w = w.rearrange("p (t d) -> p t d", t=4)
                    dve.tensor_scalar(w, src, wscale[:, k:k + 1], ROUND, ALU.mult, ALU.add).then_inc(step, 1)
                dve.wait_ge(step, 7)
                dve.tensor_scalar(wq[:, :, F:2 * F], wq[:, :, 0:F], ROUND, 1.0, ALU.subtract, ALU.min).then_inc(step, 1)
                dve.wait_ge(step, 8)
                for k, dst in enumerate((wgq[:, 0:4, :], wgq[:, 4:8, :], wdq[:, :])):
                    w = wq[:, k, F:2 * F]
                    if k < 2:
                        w = w.rearrange("p (t d) -> p t d", t=4)
                    dve.tensor_scalar(dst, w, -1.0, None, ALU.max).then_inc(ternary, 1)
                dve.wait_ge(qturned, 1)
                dve.tensor_copy(c.wguT[:, :], c.psb(5)[:, 0:8 * P]).then_inc(qcopied, 1)
                dve.tensor_copy(c.wdT[:, :, :], c.psb(6)[:, 0:4 * P].rearrange("p (t d) -> p t d", t=4)).then_inc(qcopied, 1)
                dve.wait_ge(small_in, 16 * 6)
                dve.tensor_scalar(c.bqk[:, 0:1], c.bqk[:, 0:1], 8.0 ** -0.5, None, ALU.mult).then_inc(qcopied, 1)


def norm_stage(c, name, src, dst, gain=None, bias=None, add_to=None):
    nc = c.nc
    with Stage(c, name) as s:
        sq = s.sb("sq", [P, T])
        lnv = s.sb("lnv", [P, T])
        rstd = s.sb("rstd", [P, T])
        centred, squared, var_done, lnv_done, rstd_done, scaled, done = c.norm_sems
        base = 4 * c.norms
        c.norms += 1
        with nc.Block() as block:
            @block.tensor
            def _(pe):
                for h in range(4):
                    pe.matmul(c.ps[:, h, :], c.centre[:, :], src[:, h * CH:(h + 1) * CH],
                              start=True, stop=True).then_inc(centred, 1)
                for h in range(4):
                    pe.wait_ge(squared, base + h + 1)
                    pe.matmul(c.ps[:, 4 + h, :], c.average[:, :], sq[:, h * CH:(h + 1) * CH],
                              start=True, stop=True).then_inc(var_done, 1)

            @block.scalar
            def _(act):
                for h in range(4):
                    act.wait_ge(centred, base + h + 1)
                    act.activation(sq[:, h * CH:(h + 1) * CH], c.ps[:, h, :], ACT.Square).then_inc(squared, 1)
                for h in range(4):
                    act.wait_ge(var_done, base + h + 1)
                    act.activation(lnv[:, h * CH:(h + 1) * CH], c.ps[:, 4 + h, :], ACT.Ln,
                                   bias=c.eps[:, 0:1]).then_inc(lnv_done, 1)
                    act.wait_ge(lnv_done, base + h + 1)
                    act.activation(rstd[:, h * CH:(h + 1) * CH], lnv[:, h * CH:(h + 1) * CH], ACT.Exp,
                                   scale=-0.5).then_inc(rstd_done, 1)

            @block.vector
            def _(dve):
                for h in range(4):
                    cols = slice(h * CH, (h + 1) * CH)
                    dve.wait_ge(rstd_done, base + h + 1)
                    if add_to is None and gain is None:
                        dve.tensor_tensor(dst[:, cols], c.ps[:, h, :], rstd[:, cols], ALU.mult).then_inc(done, 1)
                        continue
                    dve.tensor_tensor(sq[:, cols], c.ps[:, h, :], rstd[:, cols], ALU.mult).then_inc(scaled, 1)
                    dve.wait_ge(scaled, 2 * h + 1)
                    dve.tensor_scalar(lnv[:, cols], sq[:, cols], gain, bias, ALU.mult, ALU.add).then_inc(scaled, 1)
                    dve.wait_ge(scaled, 2 * h + 2)
                    dve.tensor_tensor(add_to[:, cols], add_to[:, cols], lnv[:, cols], ALU.add).then_inc(done, 1)


def linear_attention_stage(c):
    nc = c.nc
    D = P // NH
    RS = 8
    GRP = 4
    NG = NH // GRP

    def head(n):
        return 4 * (n % 4) + n // 4

    with Stage(c, "la") as s:
        xb = s.sb("xb", [P, 2, L])
        low = s.sb("low", [P, 2 * L])
        qk = s.sb("qk", [P, 2, 2, L])
        qm = s.sb("qm", [P, 2, NH, L])
        cum = s.sb("cum", [P, L])
        qc = s.sb("qc", [P, L])
        rec = s.sb("rec", [P, 2, L])
        v = s.sb("v", [P, 2, 2, 4, 160])
        sc = s.sb("sc", [P, RS, 3 * P])
        tri = s.sb("tri", [P, 3, P])
        ones = s.sb("ones", [P, L])
        mine = s.sb("mine", [P, NH])
        group = s.sb("group", [P, NH, D])
        on = s.sb("on", [P, L])
        (made, x_in, proj, v_proj, low_done, exp_done, feat, cum_done, qc_done, den_done, rec_done, v_done, qm_done,
         scores, sc_done, pv, scaled, on_done, out_done, x_done) = (s.sem(n) for n in (
            "made x_in proj v_proj low_done exp_done feat cum_done qc_done den_done rec_done v_done qm_done "
            "scores sc_done pv scaled on_done out_done x_done").split())

        def looped(eng, body):
            body(0, 0, True, True, False)
            body(1, 1, True, False, False)
            with eng.Fori(1, B // 2 - 1) as i:
                body(i * 2, 0, False, False, False)
                body(i * 2 + 1, 1, False, False, False)
            body(B - 2, 0, False, False, False)
            body(B - 1, 1, False, False, True)

        with nc.Block() as block:
            @block.gpsimd
            def _(pool):
                pool.memset(tri[:, :, :], 1.0).then_inc(made, 1)
                pool.memset(v[:, :, :, :, :], 0.0).then_inc(made, 1)
                pool.memset(mine[:, :], 1.0).then_inc(made, 1)
                pool.memset(group[:, :, :], 1.0).then_inc(made, 1)
                pool.memset(ones[:, :], 1.0).then_inc(made, 1)
                pool.wait_ge(made, 5)
                for k in (0, 2):
                    pool.affine_select(out=tri[:, k, :], in_=tri[:, k, :], compare_op=ALU.is_ge, fill=0.0,
                                       base=0, pattern=[[1, P]], channel_multiplier=-1).then_inc(made, 1)
                for dst, rest in ((mine[:, :], []), (group[:, :, :], [[0, D]])):
                    pool.affine_select(out=dst, in_=dst, compare_op=ALU.is_ge, fill=0.0, base=0,
                                       pattern=[[-D, NH]] + rest, channel_multiplier=1).then_inc(made, 1)
                pool.wait_ge(made, 9)
                for dst, rest in ((mine[:, :], []), (group[:, :, :], [[0, D]])):
                    pool.affine_select(out=dst, in_=dst, compare_op=ALU.is_ge, fill=0.0, base=D - 1,
                                       pattern=[[D, NH]] + rest, channel_multiplier=-1).then_inc(made, 1)

            @block.tensor
            def _(pe):
                def project(b, p, first):
                    pe.wait_ge(x_in, b + 1)
                    if not first:
                        pe.wait_ge(feat, b)
                        pe.wait_ge(v_done, b)
                    for k in range(2):
                        mm = pe.matmul(c.ps[:, 6, k * L:(k + 1) * L], c.wqk[:, k, :], xb[:, p, :], start=True, stop=True)
                    mm.then_inc(proj, 1)
                    for t in range(2):
                        mm = pe.matmul(c.ps[:, 7, t * P:(t + 1) * P], xb[:, p, t * P:(t + 1) * P], c.wvo[:, 0, :],
                                       start=True, stop=True)
                    mm.then_inc(v_proj, 1)

                def denominator(b, first):
                    pe.wait_ge(qc_done, b + 1)
                    if not first:
                        pe.wait_ge(rec_done, b)
                    pe.matmul(c.ps[:, 4, 0:L], group[:, :, :].rearrange("p h d -> p (h d)"), qc[:, :],
                              start=True, stop=True).then_inc(den_done, 1)

                def score(b, p, n, first):
                    h = head(n)
                    bank = c.ps[:, n % 2, :]
                    pe.wait_ge(qm_done, b * NH + n + 1)
                    if n >= 2 or not first:
                        pe.wait_ge(sc_done, b * NH + n - 1)
                    pe.matmul(bank[:, 0:L], qk[:, p, 1, 0:P], qm[:, p, h, :], start=True, stop=True)
                    pe.matmul(bank[:, L:L + P], qk[:, p, 1, P:L], qm[:, p, h, P:L],
                              start=True, stop=True).then_inc(scores, 1)

                def weigh(b, p, g, fresh):
                    if g == 0:
                        pe.wait_ge(v_done, b + 1)
                        if not fresh:
                            pe.wait_ge(scaled, b - 1)
                    pe.wait_ge(sc_done, b * NH + (g + 1) * GRP)
                    for kt in range(2):
                        for n in range(g * GRP, (g + 1) * GRP):
                            h = head(n)
                            i, a = h // 4, h % 4
                            mm = pe.matmul(c.ps[32 * i:32 * i + 32, 2 + p, kt * P:L], v[:, p, kt, i, 32 * a:32 * a + 32],
                                           sc[:, n % RS, 0:L] if kt == 0 else sc[:, n % RS, L:L + P],
                                           start=(g == 0 and kt == 0), stop=(g == NG - 1 and kt == 1),
                                           skip_group_check=True)
                    mm.then_inc(pv, 1)

                def out_projection(b, fresh):
                    pe.wait_ge(on_done, b)
                    if not fresh:
                        pe.wait_ge(x_done, b - 1)
                    pe.matmul(c.ps[:, 5, 0:L], c.wvo[:, 1, :], on[:, :], start=True, stop=True).then_inc(out_done, 1)

                pe.wait_ge(made, 11)
                project(0, 0, True)
                denominator(0, True)

                def body(b, p, fresh, first, last):
                    for n in range(NH):
                        score(b, p, n, first)
                        if n == 1 and not first:
                            weigh(b - 1, 1 - p, NG - 1, True)
                        if n == 3 and not last:
                            project(b + 1, 1 - p, False)
                        if n == 6 and not first:
                            out_projection(b, fresh)
                        if n > GRP and n % GRP == 1:
                            weigh(b, p, n // GRP - 1, fresh)
                        if n == 12 and not last:
                            denominator(b + 1, False)
                looped(pe, body)
                weigh(B - 1, 1, NG - 1, True)
                out_projection(B, False)

            @block.scalar
            def _(act):
                def copy_x(b, p, fresh):
                    if not fresh:
                        act.wait_ge(v_proj, b - 1)
                    act.activation(xb[:, p, :], c.xn[:, ds(b * L, L)], ACT.Copy).then_inc(x_in, 1)

                def prepare(b, p, fresh):
                    act.wait_ge(low_done, b + 1)
                    act.activation(low[:, :], low[:, :], ACT.Exp).then_inc(exp_done, 1)
                    act.wait_ge(v_proj, b + 1)
                    if not fresh:
                        act.wait_ge(pv, b * NG - NG)
                    act.activation(v[:, p, :, :, :].rearrange("p t i (a c) -> p (t i) a c", c=40)[:, :, :, 0:D],
                                   c.ps[:, 7, 0:L].rearrange("p (i a d) -> p i a d", a=4, d=D), ACT.Copy).then_inc(v_done, 1)
                    act.wait_ge(feat, b + 1)
                    if not fresh:
                        act.wait_ge(scores, b * NH - NH)
                    for n in range(NH):
                        h = head(n)
                        act.activation(qm[:, p, h, :], qk[:, p, 0, :], ACT.Copy, scale=mine[:, h:h + 1]).then_inc(qm_done, 1)

                act.wait_ge(made, 11)
                copy_x(0, 0, True)
                copy_x(1, 1, True)
                prepare(0, 0, True)

                prepare(1, 1, True)
                copy_x(2, 0, False)
                prepare(2, 0, False)
                copy_x(3, 1, False)
                with act.Fori(1, B // 2 - 1) as i:
                    for p in range(2):
                        prepare(i * 2 + p + 1, 1 - p, False)
                        copy_x(i * 2 + p + 2, p, False)
                prepare(B - 1, 1, False)

            @block.vector
            def _(dve):
                def negative_part(b):
                    dve.wait_ge(proj, b + 1)
                    dve.tensor_scalar(low[:, :], c.ps[:, 6, :], 0.0, None, ALU.min).then_inc(low_done, 1)

                def features(b, p):
                    dve.wait_ge(exp_done, b + 1)
                    dve.scalar_tensor_tensor(out=qk[:, p, :, :].rearrange("p a l -> p (a l)"), in0=c.ps[:, 6, :],
                                             scalar=0.0, in1=low[:, :], op0=ALU.max, op1=ALU.add).then_inc(feat, 1)
                    dve.wait_ge(feat, b + 1)
                    dve.tensor_tensor_scan(cum[:, :], ones[:, :], qk[:, p, 1, :], 0.0, ALU.mult, ALU.add).then_inc(cum_done, 1)
                    dve.wait_ge(cum_done, b + 1)
                    dve.tensor_tensor(qc[:, :], qk[:, p, 0, :], cum[:, :], ALU.mult).then_inc(qc_done, 1)

                def invert(b, p):
                    dve.wait_ge(den_done, b + 1)
                    dve.reciprocal(rec[:, p, :], c.ps[:, 4, 0:L]).then_inc(rec_done, 1)

                def keep_causal(b, n, first):
                    dve.wait_ge(scores, b * NH + n + 1)
                    if n >= RS or not first:
                        dve.wait_ge(pv, b * NG + (n - RS) // GRP + 1)
                    dve.tensor_tensor(sc[:, n % RS, :], c.ps[:, n % 2, 0:3 * P], tri[:, :, :].rearrange("p a q -> p (a q)"),
                                      ALU.mult).then_inc(sc_done, 1)

                def divide(b, p):
                    dve.wait_ge(pv, b * NG + NG)
                    dve.wait_ge(rec_done, b + 1)
                    dve.tensor_tensor(on[:, :], c.ps[:, 2 + p, 0:L], rec[:, p, :], ALU.mult).then_inc(scaled, 1)
                    dve.wait_ge(scaled, b + 1)
                    dve.tensor_scalar(on[:, :], on[:, :], 1e-12, None, ALU.add).then_inc(on_done, 1)

                def finish(b):
                    dve.wait_ge(out_done, b + 1)
                    dve.tensor_tensor(c.xT[:, ds(b * L, L)], c.xT[:, ds(b * L, L)], c.ps[:, 5, 0:L],
                                      ALU.add).then_inc(x_done, 1)

                dve.wait_ge(made, 11)
                negative_part(0)
                features(0, 0)
                invert(0, 0)

                def body(b, p, fresh, first, last):
                    for n in range(NH):
                        keep_causal(b, n, first)
                        if n == 2 and not first:
                            divide(b - 1, 1 - p)
                        if n == 4 and not last:
                            negative_part(b + 1)
                        if n == 7 and not first:
                            finish(b - 1)
                        if n == 8 and not last:
                            features(b + 1, 1 - p)
                        if n == 13 and not last:
                            invert(b + 1, 1 - p)
                looped(dve, body)
                divide(B - 1, 1)
                finish(B - 1)


def cross_attention_stage(c, name, D, masked_rows, weights):
    nc = c.nc
    small = not masked_rows
    W = NH * D
    OG = W // P
    QB = max(1, OG // 2)
    NQK = 2 * QB
    NV = max(1, 2 * W // CH)
    NP = NQK + NV
    GRP = 4 if small else 2
    NG = NH // GRP
    NO = 1 if small else 4
    RP, RT = 8, 8
    LAG = 4
    STEPS = NH + LAG + 2
    SCALE = float(D) ** -0.5
    O0 = 4
    WO = 5 if small else 4
    if small:
        wq, wk, wv, wo = weights

    def head(n):
        return 4 * (n % 4) + n // 4 if small else n

    with Stage(c, name) as s:
        cb = s.sb("cb", [P, L])
        q = s.sb("q", [P, OG, L])
        mx = s.sb("mx", [P, 2, 2])
        den = s.sb("den", [P, RP, 2])
        rec = s.sb("rec", [P, RP, 2])
        pr = s.sb("pr", [P, RP, 2, L])
        pT = s.sb("pT", [P, RT, 2, L])
        oT = s.sb("oT", [P, OG, L])
        if masked_rows:
            k = s.sb("k", [P, NH, L])
            v = s.sb("v", [P, 2, W])
            m = s.sb("m", [P, NT, L])
            neg = s.sb("neg", [P, 2, L])
            sm = s.sb("sm", [P, 2, 2, L])
            wq, wk, wv = (s.sb(x, [P, W]) for x in ("wq", "wk", "wv"))
            wo = s.sb("wo", [P, W])
        else:
            k = s.sb("k", [P, L])
            v = s.sb("v", [P, 2, 4, 160])
            mr = s.sb("mr", [1, L], BF16)
            km = s.sb("km", [P, NH, L])
            mine = s.sb("mine", [P, NH])
        (w_in, mask_in, consts, ctx_in, proj, evac, neg_done, km_done, scores, s_free, shifted, max_done,
         exp_done, rec_done, pr_done, turned, pT_done, pv, oT_done, out_done, x_done) = (s.sem(n) for n in (
            "w_in mask_in consts ctx_in proj evac neg_done km_done scores s_free shifted max_done exp_done "
            "rec_done pr_done turned pT_done pv oT_done out_done x_done").split())

        def looped(eng, body):
            body(0, True, False)
            with eng.Fori(1, B - 1) as b:
                body(b, False, False)
            body(B - 1, False, True)

        def qk_units(n):
            return range(NQK)[(n - NH) * 4:(n - NH + 1) * 4] if n >= NH else range(0)

        def v_units(n):
            return range(NQK, NP)[(n - 1) * 2:n * 2] if n in (1, 2) else range(0)

        with nc.Block() as block:
            if masked_rows:
                @block.sync
                def _(sp):
                    for w, src in zip((wq, wk, wv), weights[0:3]):
                        sp.dma_start(w[:, :].rearrange("e (n d) -> e n d", d=D),
                                     src.rearrange("n e d -> e n d")).then_inc(w_in, 16)
                    sp.dma_start(wo[:, :].rearrange("p (g e) -> p g e", e=P),
                                 weights[3].rearrange("(g a) d e -> (a d) g e", a=2)).then_inc(w_in, 16)
                    sp.dma_start(m[:, :, :], c.mask1.rearrange("b (t p) k -> p (b t) k", p=P)).then_inc(mask_in, 16)

            @block.gpsimd
            def _(pool):
                if small:
                    pool.memset(v[:, :, :, :], 0.0).then_inc(consts, 1)
                    pool.memset(mine[:, :], 1.0).then_inc(consts, 1)
                    pool.wait_ge(consts, 2)
                    pool.affine_select(out=mine[:, :], in_=mine[:, :], compare_op=ALU.is_ge, fill=0.0, base=0,
                                       pattern=[[-D, NH]], channel_multiplier=1).then_inc(consts, 1)
                    pool.wait_ge(consts, 3)
                    pool.affine_select(out=mine[:, :], in_=mine[:, :], compare_op=ALU.is_ge, fill=0.0, base=D - 1,
                                       pattern=[[D, NH]], channel_multiplier=-1).then_inc(consts, 1)

                else:
                    pool.memset(k[:, :, :], 0.0).then_inc(consts, 1)

                def body(b, first, last):
                    for n in range(NH):
                        pool.wait_ge(rec_done, b * NH + n + 1)
                        r = n % RP
                        pool.tensor_tensor(pr[:, r, :, :], pr[:, r, :, :],
                                           rec[:, r, :].unsqueeze(2).broadcast_to([P, 2, L]), ALU.mult).then_inc(pr_done, 1)
                looped(pool, body)

            @block.tensor
            def _(pe):
                if masked_rows:
                    pe.wait_ge(w_in, 64)

                def project(b, n, first):
                    bank = c.ps[:, 6 + n % 2, :]
                    if n >= 2:
                        pe.wait_ge(evac, b * NP + n - 1)
                    elif not first:
                        pe.wait_ge(evac, b * NP)
                    if n < NQK:
                        w, src = (wq, c.xn) if n < QB else (wk, c.cT)
                        for j in range(min(2, OG)):
                            gr = 2 * (n % QB) + j
                            mm = pe.matmul(bank[:, j * L:(j + 1) * L], w[:, gr * P:(gr + 1) * P],
                                           src[:, ds(b * L, L)], start=True, stop=True)
                    else:
                        if n == NQK:
                            pe.wait_ge(ctx_in, b + 1)
                        if small:
                            for t in range(2):
                                mm = pe.matmul(bank[:, t * P:(t + 1) * P], cb[:, t * P:(t + 1) * P], wv,
                                               start=True, stop=True)
                        else:
                            t, half = divmod(n - NQK, 2)
                            mm = pe.matmul(bank, cb[:, t * P:(t + 1) * P], wv[:, half * CH:(half + 1) * CH],
                                           start=True, stop=True)
                    mm.then_inc(proj, 1)

                def score(b, n, first):
                    bank = c.ps[:, n % 2, :]
                    if n == 0:
                        pe.wait_ge(evac, b * NP + NQK)
                    if n >= 2 or not first:
                        pe.wait_ge(exp_done if small else s_free, b * NH + n - 1)
                    h = head(n)
                    if small:
                        pe.wait_ge(km_done, b * NH + n + 1)
                        pe.matmul(bank.rearrange("p (t k) -> p t k", t=2), c.ones_row[0:1, :],
                                  mr[:, :].unsqueeze(1).broadcast_to([1, 2, L]), start=True, stop=False,
                                  skip_group_check=True)
                    for t in range(2):
                        if small:
                            mm = pe.matmul(bank[:, t * L:(t + 1) * L], q[:, 0, t * P:(t + 1) * P], km[:, h, :],
                                           start=False, stop=True, skip_group_check=True)
                        else:
                            mm = pe.matmul(bank[:, t * L:(t + 1) * L], q[:, h // 2, t * P:(t + 1) * P],
                                           k[:, h, :], start=True, stop=True)
                    mm.then_inc(scores, 1)

                def turn(b, n, first):
                    pe.wait_ge(pr_done, b * NH + n + 1)
                    if n >= 2 or not first:
                        pe.wait_ge(pT_done, b * NH + n - 1)
                    for kt in range(2):
                        for t in range(2):
                            mm = pe.transpose(c.ps[:, 2 + n % 2, kt * L + t * P:kt * L + (t + 1) * P],
                                              pr[:, n % RP, t, kt * P:(kt + 1) * P], c.ident[:, :])
                    mm.then_inc(turned, 1)

                def weigh(b, g, first):
                    if g == 0:
                        pe.wait_ge(evac, b * NP + NP)
                        if not first:
                            if small:
                                pe.wait_ge(oT_done, b)
                            else:
                                pe.wait_ge(x_done, b)
                    if not small and g % 2 == 0 and (g >= 4 or not first):
                        pe.wait_ge(oT_done, b * NO + g // 2 - 1)
                    pe.wait_ge(pT_done, b * NH + (g + 1) * GRP)
                    for kt in range(2):
                        for n in range(g * GRP, (g + 1) * GRP):
                            h = head(n)
                            if small:
                                i, a = h // 4, h % 4
                                mm = pe.matmul(c.ps[32 * i:32 * i + 32, O0, 0:L], v[:, kt, i, 32 * a:32 * a + 32],
                                               pT[:, n % RT, kt, :], start=(g == 0 and kt == 0),
                                               stop=(g == NG - 1 and kt == 1), skip_group_check=True)
                            else:
                                r = h % 2
                                at = (h // 2 % 2) * L
                                mm = pe.matmul(c.ps[64 * r:64 * r + 64, O0 + h // 4 % 2, at:at + L],
                                               v[:, kt, h * D:(h + 1) * D], pT[:, n % RT, kt, :],
                                               start=(kt == 0), stop=(kt == 1))
                    mm.then_inc(pv, 1)

                def out_projection(b):
                    pe.wait_ge(oT_done, b * NO)
                    for gr in range(OG):
                        mm = pe.matmul(c.ps[:, WO, 0:L], wo[:, gr * P:(gr + 1) * P], oT[:, gr, :],
                                       start=(gr == 0), stop=(gr == OG - 1))
                    mm.then_inc(out_done, 1)

                for n in range(NQK):
                    project(0, n, True)

                def body(b, first, last):
                    for n in range(STEPS):
                        if n < NH:
                            score(b, n, first)
                        if not last:
                            for a in qk_units(n):
                                project(b + 1, a, False)
                        for a in v_units(n):
                            project(b, a, first)
                        if n == LAG and not first:
                            out_projection(b)
                        if LAG <= n < NH + LAG:
                            turn(b, n - LAG, first)
                        done = n - LAG
                        if done > 0 and done % GRP == 0 and done <= NH:
                            weigh(b, done // GRP - 1, first)
                looped(pe, body)
                out_projection(B)

            def evacuate_turned(eng, b, n, first):
                eng.wait_ge(turned, b * NH + n + 1)
                if n >= RT or not first:
                    eng.wait_ge(pv, b * NG + (n - RT) // GRP + 1)
                src = c.ps[:, 2 + n % 2, :]
                dst = pT[:, n % RT, :, :].rearrange("p t q -> p (t q)")
                if small:
                    eng.tensor_copy(dst, src).then_inc(pT_done, 1)
                else:
                    eng.activation(dst, src, ACT.Copy).then_inc(pT_done, 1)

            @block.scalar
            def _(act):
                def evacuate(b, n, first):
                    act.wait_ge(proj, b * NP + n + 1)
                    bank = c.ps[:, 6 + n % 2, :]
                    if n < NQK:
                        scale = SCALE if n < QB else 1.0
                        if small:
                            if n == 1:
                                act.activation(mr[:, :], c.maskrow[0:1, ds(b, 1), :].rearrange("p a k -> p (a k)"), ACT.Copy)
                            act.activation(q[:, 0, :] if n < QB else k[:, :], bank[:, 0:L], ACT.Identity, scale=scale,
                                           bias=c.bqk[:, n:n + 1]).then_inc(evac, 1)
                        else:
                            gr = 2 * (n % QB)
                            if n < QB:
                                a = act.activation(q[:, gr:gr + 2, :].rearrange("p j l -> p (j l)"), bank,
                                                   ACT.Copy, scale=scale)
                            for r in range(2) if n >= QB else ():
                                row = slice(64 * r, 64 * r + 64)
                                a = act.activation(k[row, 2 * gr:2 * gr + 4, :].rearrange("p (j r) l -> p j r l", r=2)[:, :, r, :],
                                                   bank[row, :].rearrange("p (j l) -> p j l", j=2), ACT.Copy)
                            a.then_inc(evac, 1)
                        return
                    if n == NQK and not first:
                        act.wait_ge(pv, b * NG)
                    if small:
                        act.activation(v[:, :, :, :].rearrange("p t i (a c) -> p (t i) a c", c=40)[:, :, :, 0:D],
                                       bank[:, 0:L].rearrange("p (i a d) -> p i a d", a=4, d=D),
                                       ACT.Copy).then_inc(evac, 1)
                    else:
                        t, half = divmod(n - NQK, 2)
                        act.activation(v[:, t, half * CH:(half + 1) * CH], bank, ACT.Copy).then_inc(evac, 1)

                act.activation(cb[:, :], c.cT[:, 0:L], ACT.Copy).then_inc(ctx_in, 1)
                act.wait_ge(consts, 4 if small else 1)
                for n in range(NQK):
                    evacuate(0, n, True)

                def body(b, first, last):
                    for n in range(STEPS):
                        if not last:
                            for a in qk_units(n):
                                evacuate(b + 1, a, False)
                        for a in v_units(n):
                            evacuate(b, a, first)
                        if masked_rows and LAG <= n < NH + LAG:
                            evacuate_turned(act, b, n - LAG, first)
                        if n < NH:
                            if n >= RP or not first:
                                act.wait_ge(turned, b * NH + n - RP + 1)
                            act.wait_ge(max_done, b * NH + n + 1)
                            for t in range(2):
                                src = sm[:, n % 2, t, :] if masked_rows else c.ps[:, n % 2, t * L:(t + 1) * L]
                                a = act.activation(pr[:, n % RP, t, :], src, ACT.Exp, bias=mx[:, n % 2, t:t + 1],
                                                   scale=-1.0 if masked_rows else 1.0,
                                                   accum_out=den[:, n % RP, t:t + 1])
                            a.then_inc(exp_done, 1)
                        if n == 4 and not last:
                            act.wait_ge(proj, b * NP + NP)
                            act.activation(cb[:, :], c.cT[:, ds(b * L + L, L)], ACT.Copy).then_inc(ctx_in, 1)
                looped(act, body)

            @block.vector
            def _(dve):
                def keys_of_head(b, n):
                    h = head(n)
                    dve.tensor_scalar(km[:, h, :], k[:, :], mine[:, h:h + 1], None, ALU.mult).then_inc(km_done, 1)

                def maximum(b, n, first):
                    dve.wait_ge(scores, b * NH + n + 1)
                    bank = c.ps[:, n % 2, :].rearrange("p (t k) -> p t k", t=2)
                    if n >= 2 or not first:
                        dve.wait_ge(exp_done, b * NH + n - 1)
                    if small:
                        dve.tensor_reduce(mx[:, n % 2, :], bank, AX.X, ALU.max, negate=True).then_inc(max_done, 1)
                        return
                    dve.tensor_tensor(sm[:, n % 2, :, :], bank, m[:, ds(b * 2, 2), :], ALU.mult).then_inc(s_free, 1)
                    dve.wait_ge(s_free, b * NH + n + 1)
                    dve.sem_inc(shifted, 1)
                    for t in range(2):
                        a = dve.tensor_tensor_reduce(sm[:, n % 2, t, :], sm[:, n % 2, t, :], neg[:, t, :], -1.0, 3.0e38,
                                                     ALU.add, ALU.min, accum_out=mx[:, n % 2, t:t + 1])
                    a.then_inc(max_done, 1)

                def invert(b, n, first):
                    dve.wait_ge(exp_done, b * NH + n + 1)
                    if n >= RP or not first:
                        dve.wait_ge(pr_done, b * NH + n - RP + 1)
                    dve.reciprocal(rec[:, n % RP, :], den[:, n % RP, :]).then_inc(rec_done, 1)

                def output_bank(b, u, first):
                    dve.wait_ge(pv, b * NG + (u + 1) * NG // NO)
                    if small:
                        dve.tensor_scalar(oT[:, 0, :], c.ps[:, O0, 0:L], c.bv[:, 0:1], c.present[:, ds(b, 1)],
                                          ALU.add, ALU.mult).then_inc(oT_done, 1)
                    else:
                        dve.tensor_copy(oT[:, 2 * u:2 * u + 2, :].rearrange("p g q -> p (g q)"),
                                        c.ps[:, O0 + u % 2, :]).then_inc(oT_done, 1)

                def finish(b):
                    dve.wait_ge(out_done, b)
                    cols = c.xT[:, ds(b * L - L, L)]
                    if small:
                        dve.scalar_tensor_tensor(out=cols, in0=c.ps[:, WO, 0:L], scalar=c.bo[:, 0:1], in1=cols,
                                                 op0=ALU.add, op1=ALU.add).then_inc(x_done, 1)
                    else:
                        dve.tensor_tensor(cols, cols, c.ps[:, WO, 0:L], ALU.add).then_inc(x_done, 1)

                if small:
                    dve.wait_ge(consts, 4)
                else:
                    dve.wait_ge(mask_in, 16)

                def body(b, first, last):
                    if small:
                        dve.wait_ge(evac, b * NP + NQK)
                        for n in range(4):
                            keys_of_head(b, n)
                    else:
                        dve.tensor_scalar(neg[:, :, :], m[:, ds(b * 2, 2), :], 1.0, 1.0e8,
                                          ALU.subtract, ALU.mult).then_inc(neg_done, 1)
                        dve.wait_ge(neg_done, b + 1)
                    for n in range(STEPS + 1):
                        if small and n + 4 < NH:
                            keys_of_head(b, n + 4)
                        if n < NH:
                            maximum(b, n, first)
                        if 1 <= n <= NH:
                            invert(b, n - 1, first)
                        if small and LAG <= n < NH + LAG:
                            evacuate_turned(dve, b, n - LAG, first)
                        if n == LAG and not first:
                            finish(b)
                        if small and n == STEPS:
                            output_bank(b, 0, first)
                        elif not small and n > LAG + 4 and (n - LAG) % 4 == 1:
                            output_bank(b, (n - LAG) // 4 - 1, first)
                looped(dve, body)
                finish(B)


def ffn_stage(c):
    nc = c.nc
    with Stage(c, "ffn") as s:
        xb = s.sb("xb", [P, P])
        ab = s.sb("ab", [P, 8])
        xr = s.sb("xr", [P, P])
        xq = s.sb("xq", [P, P], BF16)
        xqT = s.sb("xqT", [P, P], BF16)
        gate = s.sb("gate", [P, F])
        hid = s.sb("hid", [P, F])
        hr = s.sb("hr", [P, F])
        hq = s.sb("hq", [P, F], BF16)
        hqT = s.sb("hqT", [P, 4, P], BF16)
        y = s.sb("y", [P, P])
        names = "x_in turned st xq_done xqT_t xqT_done gu gate_done hq_done hqT_t hqT_done down y_done y_t x_done s_w".split()
        (x_in, turned, st, xq_done, xqT_t, xqT_done, gu, gate_done, hq_done, hqT_t, hqT_done, down, y_done, y_t,
         x_done, s_w) = (s.sem(n) for n in names)
        hq_step = s.sem("hq_step")
        with nc.Block() as block:
            @block.gpsimd
            def _(pool):
                pool.memset(xb[:, 0:1], 0.0).then_inc(x_done, 1)
                with pool.Fori(0, NT) as t:
                    pool.wait_ge(x_done, t + 1)
                    pool.wait_ge(x_done, 1)
                    pool.tensor_copy(xb[:, :], c.xn[:, ds(t * P, P)]).then_inc(x_in, 1)

            @block.tensor
            def _(pe):
                with pe.Fori(0, NT) as t:
                    pe.wait_ge(x_in, t + 1)
                    pe.transpose(c.ps[:, 0, 0:P], xb[:, :], c.ident[:, :]).then_inc(turned, 1)
                    pe.wait_ge(xq_done, t + 1)
                    pe.transpose(c.psb(1)[:, 0:P], xq[:, :], c.identb[:, :]).then_inc(xqT_t, 1)
                    pe.wait_ge(xqT_done, t + 1)
                    pe.matmul(c.ps[:, 2, :], xqT[:, :], c.wguT[:, 0:F], start=True, stop=True).then_inc(gu, 1)
                    pe.matmul(c.ps[:, 3, :], xqT[:, :], c.wguT[:, F:2 * F], start=True, stop=True).then_inc(gu, 1)
                    pe.wait_ge(hq_done, t + 1)
                    for k in range(4):
                        mm = pe.transpose(c.psb(4)[:, k * P:(k + 1) * P], hq[:, k * P:(k + 1) * P], c.identb[:, :])
                    mm.then_inc(hqT_t, 1)
                    pe.wait_ge(hqT_done, t + 1)
                    for k in range(4):
                        mm = pe.matmul(c.ps[:, 5, 0:P], hqT[:, k, :], c.wdT[:, k, :], start=(k == 0), stop=(k == 3))
                    mm.then_inc(down, 1)
                    pe.wait_ge(y_done, t + 1)
                    pe.transpose(c.ps[:, 6, 0:P], y[:, :], c.ident[:, :]).then_inc(y_t, 1)

            @block.scalar
            def _(act):
                with act.Fori(0, NT) as t:
                    act.wait_ge(xqT_t, t + 1)
                    act.activation(xqT[:, :], c.psb(1)[:, 0:P], ACT.Copy).then_inc(xqT_done, 1)
                    act.wait_ge(gu, 2 * t + 1)
                    act.wait_ge(s_w, t + 1)
                    act.activation(gate[:, :], c.ps[:, 2, :], ACT.Silu, scale=ab[:, 3:4]).then_inc(gate_done, 1)
                    act.wait_ge(hqT_t, t + 1)
                    act.activation(hqT[:, :, :].rearrange("p k q -> p (k q)"), c.psb(4)[:, 0:F], ACT.Copy).then_inc(hqT_done, 1)

            @block.vector
            def _(dve):
                STEPS = 7
                with dve.Fori(0, NT) as t:
                    dve.wait_ge(turned, t + 1)
                    dve.tensor_reduce(ab[:, 0:1], c.ps[:, 0, 0:P], AX.X, ALU.max, apply_absolute_value=True).then_inc(st, 1)
                    dve.wait_ge(st, t * STEPS + 1)
                    dve.tensor_scalar(ab[:, 1:2], ab[:, 0:1], 1e-5, 1.0 / 127.0, ALU.max, ALU.mult).then_inc(st, 1)
                    dve.wait_ge(st, t * STEPS + 2)
                    dve.reciprocal(ab[:, 2:3], ab[:, 1:2]).then_inc(st, 1)
                    dve.wait_ge(st, t * STEPS + 3)
                    dve.tensor_scalar(xr[:, :], c.ps[:, 0, 0:P], ab[:, 2:3], ROUND, ALU.mult, ALU.add).then_inc(st, 1)
                    dve.wait_ge(st, t * STEPS + 4)
                    dve.tensor_scalar(xq[:, :], xr[:, :], ROUND, None, ALU.subtract).then_inc(xq_done, 1)
                    dve.tensor_scalar(ab[:, 3:5], c.wmean[:, 0:2], ab[:, 1:2], None, ALU.mult).then_inc(s_w, 1)
                    dve.wait_ge(s_w, t + 1)
                    dve.wait_ge(gate_done, t + 1)
                    dve.wait_ge(gu, 2 * t + 2)
                    dve.scalar_tensor_tensor(out=hid[:, :], in0=c.ps[:, 3, :], scalar=ab[:, 4:5], in1=gate[:, :],
                                             op0=ALU.mult, op1=ALU.mult).then_inc(st, 1)
                    dve.wait_ge(st, t * STEPS + 5)
                    dve.tensor_reduce(ab[:, 5:6], hid[:, :], AX.X, ALU.max, apply_absolute_value=True).then_inc(st, 1)
                    dve.wait_ge(st, t * STEPS + 6)
                    dve.tensor_scalar(ab[:, 6:7], ab[:, 5:6], 1e-5, 1.0 / 127.0, ALU.max, ALU.mult).then_inc(st, 1)
                    dve.wait_ge(st, t * STEPS + 7)
                    dve.reciprocal(ab[:, 7:8], ab[:, 6:7]).then_inc(hq_step, 1)
                    dve.wait_ge(hq_step, 2 * t + 1)
                    dve.tensor_scalar(hr[:, :], hid[:, :], ab[:, 7:8], ROUND, ALU.mult, ALU.add).then_inc(hq_step, 1)
                    dve.wait_ge(hq_step, 2 * t + 2)
                    dve.tensor_scalar(hq[:, :], hr[:, :], ROUND, None, ALU.subtract).then_inc(hq_done, 1)
                    dve.wait_ge(down, t + 1)
                    dve.tensor_scalar(y[:, :], c.ps[:, 5, 0:P], ab[:, 6:7], c.wmean[:, 2:3], ALU.mult, ALU.mult).then_inc(y_done, 1)
                    dve.wait_ge(y_t, t + 1)
                    cols = c.xT[:, ds(t * P, P)]
                    dve.tensor_tensor(cols, cols, c.ps[:, 6, 0:P], ALU.add).then_inc(x_done, 1)



def mamba_stage(c, g):
    nc = c.nc
    PAD = TAPS - 1
    R = 4
    xm = c.xn
    with Stage(c, "ma") as s:
        w_in = s.sb("w_in", [P, 2 * DI])
        cw = s.sb("cw", [P, DI, TAPS])
        w_tap = s.sb("w_tap", [P, TAPS, DI])
        cb = s.sb("cb", [P, 2])
        w_x = s.sb("w_x", [P, 2, RANK + 2 * NS])
        w_bc = s.sb("w_bc", [P, 2, 3, 2 * NS])
        w_dt = s.sb("w_dt", [RANK, DI])
        dtb = s.sb("dtb", [P, 2])
        A = s.sb("A", [P, 2, NS])
        Al = s.sb("Al", [P, 2, NS])
        Dp = s.sb("Dp", [P, 2])
        dD = s.sb("dD", [P, 2, P])
        w_out = s.sb("w_out", [P, 2, P])
        nw = s.sb("nw", [P, 2])
        sel = s.sb("sel", [3 * 2 * NS, 2 * NS, P], BF16)
        hn = s.sb("hn", [P, B, PAD + L])
        u = s.sb("u", [P, 2, T])
        z = s.sb("z", [P, 2, T])
        bc = s.sb("bc", [3 * 2 * NS, T], BF16)
        dt = s.sb("dt", [P, 2, T])
        dtu = s.sb("dtu", [P, 2, T])
        dA = s.sb("dA", [P, R, HALF])
        hs = s.sb("hs", [P, R, HALF])
        Bs = s.sb("Bs", [P, 2, HALF])
        sq = hs[:, 0:2, :].rearrange("p a l -> p (a l)")
        rstd = hs[:, 2:4, :].rearrange("p a l -> p (a l)")
        dtr = hs[0:RANK, 0:2, :].rearrange("p a l -> p (a l)")
        bcr = hs[0:96, 2:4, :].rearrange("p a l -> p (a l)")

        names = ("early_in mid_in late_in consts tap_done dd_done a_step a_done xm_ready centred squared "
                 "var_done lnv_done rstd_done scaled hn_ready proj silu_done bc_ps dtr_ps bc_p1 bc_r bc_p2 bc_r2 "
                 "bc_done dtr_done dt_ps abs_done relu_done exp_done ln_done dt_done dtu_done b_ready bs_done "
                 "c_ready da_done dbu_done scan_done hc_done y_acc gated out_ps").split()
        (early_in, mid_in, late_in, consts, tap_done, dd_done, a_step, a_done, xm_ready, centred, squared,
         var_done, lnv_done, rstd_done, scaled, hn_ready, proj, silu_done, bc_ps, dtr_ps, bc_p1, bc_r, bc_p2, bc_r2,
         bc_done, dtr_done, dt_ps, abs_done, relu_done, exp_done, ln_done, dt_done, dtu_done, b_ready, bs_done,
         c_ready, da_done, dbu_done, scan_done, hc_done, y_acc, gated, out_ps) = (s.sem(n) for n in names)
        EARLY, MID, LATE = 5 * 16, 6 * 16, 3 * 16
        XM0, BS0, DBU0, HC0, SCAN0, Y0, DT0 = 2, 1, 4, 2, 4, 4, 2

        def pair(k, rows=P):
            return c.ps[0:rows, 2 * k:2 * k + 2, :].rearrange("p a l -> p (a l)")

        def half(gt):
            return slice(gt * HALF, (gt + 1) * HALF)

        def load_early(sp, i):
            sp.dma_start(w_in[:, :], g["m_in"][ds(i, 1)].rearrange("a p n -> (a p) n")).then_inc(early_in, 16)
            sp.dma_start(cw[:, :, :], g["m_cw"][ds(i, 1)].broadcast_to([P, DI, TAPS])).then_inc(early_in, 16)
            sp.dma_start(cb[:, :], g["m_cb"][ds(i, 1)].rearrange("a (h p) -> (a p) h", p=P),
                         allow_slow_non_contiguous=True).then_inc(early_in, 16)
            for k, n in enumerate(("m_nw", "m_nb")):
                sp.dma_start(nw[:, k:k + 1], g[n][ds(i, 1)].rearrange("a p -> p a"),
                             allow_slow_non_contiguous=True).then_inc(early_in, 16)

        def load_mid(sp, i):
            sp.dma_start(w_x[:, :, :], g["m_xw"][ds(i, 1)].rearrange("a (h p) n -> (a p) h n", p=P)).then_inc(mid_in, 16)
            for part in range(3):
                sp.dma_start(w_bc[:, :, part, :], g["m_xw"][ds(i, 1), :, RANK:RANK + 2 * NS]
                             .rearrange("a (h p) n -> (a p) h n", p=P)).then_inc(mid_in, 16)
            sp.dma_start(w_dt[:, :], g["m_dw"][ds(i, 1)].rearrange("a p n -> (a p) n")).then_inc(mid_in, 16)
            sp.dma_start(dtb[:, :], g["m_db"][ds(i, 1)].rearrange("a (h p) -> (a p) h", p=P),
                         allow_slow_non_contiguous=True).then_inc(mid_in, 16)

        def load_late(sp, i):
            sp.dma_start(Al[:, :, :], g["m_al"][ds(i, 1)].rearrange("a (h p) n -> (a p) h n", p=P)).then_inc(late_in, 16)
            sp.dma_start(Dp[:, :], g["m_D"][ds(i, 1)].rearrange("a (h p) -> (a p) h", p=P),
                         allow_slow_non_contiguous=True).then_inc(late_in, 16)
            sp.dma_start(w_out[:, :, :], g["m_ow"][ds(i, 1)].rearrange("a (h p) n -> (a p) h n", p=P)).then_inc(late_in, 16)

        with nc.Block() as block:
            @block.sync
            def _(sp):
                load_early(sp, 0)
                load_mid(sp, 0)
                load_late(sp, 0)
                with sp.Fori(1, NBLK) as i:
                    sp.wait_ge(silu_done, i * 8)
                    load_early(sp, i)
                    sp.wait_ge(dt_done, i * 4 + DT0)
                    load_mid(sp, i)
                    sp.wait_ge(xm_ready, i * 2 + XM0)
                    load_late(sp, i)

            @block.gpsimd
            def _(pool):
                pool.memset(hn[:, :, 0:PAD], 0.0).then_inc(consts, 1)
                pool.memset(dA[:, :, :], 0.0).then_inc(consts, 1)
                pool.memset(sel[:, :, :], 0.0).then_inc(consts, 1)
                for part in range(3):
                    pool.wait_ge(consts, 3 + part)
                    pool.affine_select(out=sel[:, :, :], in_=sel[:, :, :], compare_op=ALU.not_equal, fill=1.0,
                                       base=-2 * NS * part, pattern=[[-1, 2 * NS], [0, P]],
                                       channel_multiplier=1).then_inc(consts, 1)
                pool.sem_inc(dbu_done, DBU0)
                with pool.Fori(0, NBLK) as i:
                    pool.wait_ge(early_in, i * EARLY + EARLY)
                    for k in range(TAPS):
                        pool.tensor_tensor(w_tap[:, k, :], w_in[:, 0:DI], cw[:, :, k], ALU.mult).then_inc(tap_done, 1)
                    for gt in range(2):
                        with pool.Fori(0, NS // 2) as t:
                            for k in range(4):
                                if k % 2 == 0:
                                    pool.wait_ge(bs_done, i * 2 * NS + t * 2 + gt * NS + k // 2 + 1 + BS0)
                                pool.wait_ge(y_acc, i * 4 * NS + t * 4 + gt * 2 * NS + k + 1)
                                pool.tensor_tensor(hs[:, k, :], dtu[:, k % 2, half(gt)], Bs[:, k // 2, :],
                                                   ALU.mult).then_inc(dbu_done, 1)

            @block.tensor
            def _(pe):
                pe.sem_inc(y_acc, Y0)
                pe.wait_ge(consts, 6)
                with pe.Fori(0, NBLK) as i:
                    pe.wait_ge(xm_ready, i * 2 + XM0)
                    for h in range(4):
                        pe.matmul(c.ps[:, h, :], c.centre[:, :], xm[:, h * CH:(h + 1) * CH],
                                  start=True, stop=True).then_inc(centred, 1)
                    for h in range(4):
                        pe.wait_ge(squared, i * 4 + h + 1)
                        pe.matmul(c.ps[:, 4 + h, :], c.average[:, :], sq[:, h * CH:(h + 1) * CH],
                                  start=True, stop=True).then_inc(var_done, 1)
                    pe.wait_ge(hn_ready, i * 4 + 4)
                    pe.wait_ge(tap_done, i * TAPS + TAPS)
                    for k in range(8):
                        gt, m = divmod(k, 4)
                        if k >= 4:
                            pe.wait_ge(silu_done, i * 8 + k - 3)
                        for a in range(2):
                            b0 = gt * HB + a * 2
                            out = c.ps[:, 2 * m + a, :]
                            if m < 2:
                                mm = pe.matmul(out, w_in[:, DI + m * P:DI + (m + 1) * P], hn[:, b0:b0 + 2, PAD:PAD + L],
                                               start=True, stop=True)
                            else:
                                for t in range(TAPS):
                                    mm = pe.matmul(out, w_tap[:, t, (m - 2) * P:(m - 1) * P], hn[:, b0:b0 + 2, t:t + L],
                                                   start=(t == 0), stop=(t == TAPS - 1))
                        mm.then_inc(proj, 1)
                    pe.wait_ge(silu_done, i * 8 + 8)
                    pe.wait_ge(mid_in, i * MID + MID)
                    for gt in range(2):
                        for a in range(2):
                            cols = slice(gt * HALF + a * CH, gt * HALF + (a + 1) * CH)
                            for h in range(2):
                                mm = pe.matmul(c.ps[0:96, 2 * gt + a, :], w_bc[:, h, :, :].rearrange("p a n -> p (a n)"),
                                               u[:, h, cols], start=(h == 0), stop=(h == 1))
                        mm.then_inc(bc_ps, 1)
                        for a in range(2):
                            cols = slice(gt * HALF + a * CH, gt * HALF + (a + 1) * CH)
                            for h in range(2):
                                mm = pe.matmul(c.ps[0:RANK, 4 + 2 * gt + a, :], w_x[:, h, 0:RANK],
                                               u[:, h, cols], start=(h == 0), stop=(h == 1))
                        mm.then_inc(dtr_ps, 1)
                    pe.wait_ge(dtr_done, i * 2 + 2)
                    for gt in range(2):
                        if gt == 1:
                            pe.wait_ge(bc_r, i * 2 + 2)
                        for h in range(2):
                            for a in range(2):
                                cols = slice(gt * HALF + a * CH, gt * HALF + (a + 1) * CH)
                                mm = pe.matmul(c.ps[:, 4 - 4 * gt + 2 * h + a, :], w_dt[:, h * P:(h + 1) * P],
                                               dtr[:, cols], start=True, stop=True)
                            mm.then_inc(dt_ps, 1)
                    pe.wait_ge(relu_done, i * 4 + 4)
                    pe.wait_ge(bc_done, i * 2 + 2)
                    pe.wait_ge(dd_done, i * 2 + 2)
                    for gt in range(2):
                        if gt == 1:
                            pe.wait_ge(gated, i * 4 + 2)
                        for h in range(2):
                            for a in range(2):
                                cols = slice(gt * HALF + a * CH, gt * HALF + (a + 1) * CH)
                                pe.matmul(c.ps[:, 4 + 2 * h + a, :], dD[:, h, :], u[:, h, cols], start=True, stop=False,
                                          skip_group_check=True)

                        def spread(k, a, done):
                            for q in range(2):
                                mm = pe.matmul(c.ps[:, 2 * a + q, :], k,
                                               bc[:, gt * HALF + q * CH:gt * HALF + (q + 1) * CH],
                                               start=True, stop=True)
                            mm.then_inc(done, 1)

                        def spread_b(n, state):
                            pe.wait_ge(bs_done, state + BS0)
                            spread(sel[:, ds(n, 1), :].rearrange("p a q -> p (a q)"), 0, b_ready)

                        def spread_c(n, state):
                            pe.wait_ge(hc_done, state * 2 + HC0)
                            spread(sel[:, ds(n + NS, 1), :].rearrange("p a q -> p (a q)"), 1, c_ready)

                        def sum_y(slot, item):
                            pe.wait_ge(hc_done, item + 1 + HC0)
                            for q in range(2):
                                mm = pe.matmul(c.ps[:, 4 + 2 * (slot % 2) + q, :], c.ident[:, :],
                                               hs[:, slot, q * CH:(q + 1) * CH], start=False, stop=False,
                                               skip_group_check=True)
                            mm.then_inc(y_acc, 1)

                        first = i * 2 * NS + gt * NS
                        spread_b(0, first)
                        spread_b(1, first + 1)
                        spread_c(0, first)
                        with pe.Fori(0, NS // 2 - 1) as t:
                            for p in range(2):
                                state = i * 2 * NS + t * 2 + gt * NS + 1 + p
                                slot = 2 * p
                                spread_b(t * 2 + 2 + p, state + 1)
                                sum_y(slot, i * 4 * NS + t * 4 + gt * 2 * NS + 2 * p)
                                spread_c(t * 2 + 1 + p, state)
                                sum_y(slot + 1, i * 4 * NS + t * 4 + gt * 2 * NS + 2 * p + 1)
                        item = i * 4 * NS + gt * 2 * NS + 2 * (NS - 2)
                        sum_y(0, item)
                        spread_c(NS - 1, first + NS - 1)
                        sum_y(1, item + 1)
                        sum_y(2, item + 2)
                        sum_y(3, item + 3)
                    pe.wait_ge(gated, i * 4 + 4)
                    for gt in range(2):
                        for a in range(2):
                            cols = slice(gt * HALF + a * CH, gt * HALF + (a + 1) * CH)
                            for h in range(2):
                                mm = pe.matmul(c.ps[:, 2 * gt + a, :], w_out[:, h, :], z[:, h, cols],
                                               start=(h == 0), stop=(h == 1))
                        mm.then_inc(out_ps, 1)

            @block.scalar
            def _(act):
                act.sem_inc(bs_done, BS0)
                act.wait_ge(consts, 6)
                with act.Fori(0, NBLK) as i:
                    for h in range(4):
                        act.wait_ge(centred, i * 4 + h + 1)
                        act.activation(sq[:, h * CH:(h + 1) * CH], c.ps[:, h, :], ACT.Square).then_inc(squared, 1)
                    for h in range(4):
                        r = rstd[:, h * CH:(h + 1) * CH]
                        act.wait_ge(var_done, i * 4 + h + 1)
                        act.activation(r, c.ps[:, 4 + h, :], ACT.Ln, bias=c.eps[:, 0:1]).then_inc(lnv_done, 1)
                        act.wait_ge(lnv_done, i * 4 + h + 1)
                        act.activation(r, r, ACT.Exp, scale=-0.5).then_inc(rstd_done, 1)
                    act.wait_ge(late_in, i * LATE + LATE)
                    act.activation(A[:, :, :], Al[:, :, :], ACT.Exp).then_inc(a_step, 1)
                    act.wait_ge(a_step, i + 1)
                    act.activation(A[:, :, :], A[:, :, :], ACT.Copy, scale=-1.0).then_inc(a_done, 1)
                    for k in range(8):
                        gt, m = divmod(k, 4)
                        act.wait_ge(proj, i * 8 + k + 1)
                        if m < 2:
                            act.activation(z[:, m, half(gt)], pair(m), ACT.Silu).then_inc(silu_done, 1)
                        else:
                            act.activation(u[:, m - 2, half(gt)], pair(m), ACT.Silu,
                                           bias=cb[:, m - 2:m - 1]).then_inc(silu_done, 1)
                    for gt in range(2):
                        act.wait_ge(bc_ps, i * 2 + gt + 1)
                        act.activation(bc[:, half(gt)], pair(gt, 96), ACT.Copy).then_inc(bc_p1, 1)
                        act.wait_ge(dtr_ps, i * 2 + gt + 1)
                        act.activation(dtr[:, half(gt)], pair(2 + gt, RANK), ACT.Copy).then_inc(dtr_done, 1)
                    for gt in range(2):
                        act.wait_ge(bc_r, i * 2 + gt + 1)
                        act.activation(bc[32:64, half(gt)], bcr[32:64, half(gt)], ACT.Copy)
                        act.activation(bc[64:96, half(gt)], bcr[64:96, half(gt)], ACT.Copy).then_inc(bc_p2, 1)
                    for gt in range(2):
                        act.wait_ge(bc_r2, i * 2 + gt + 1)
                        act.activation(bc[64:96, half(gt)], bcr[64:96, half(gt)], ACT.Copy).then_inc(bc_done, 1)
                    for k in range(4):
                        gt, h = divmod(k, 2)
                        l = Bs[:, k % 2, :]
                        act.wait_ge(dt_ps, i * 4 + k + 1)
                        act.wait_ge(dt_done, i * 4 + k + 1)
                        act.activation(l, pair(2 - 2 * gt + h), ACT.Abs, bias=dtb[:, h:h + 1]).then_inc(abs_done, 1)
                        act.wait_ge(abs_done, i * 4 + k + 1)
                        act.activation(l, l, ACT.Exp, scale=-1.0).then_inc(exp_done, 1)
                        act.wait_ge(exp_done, i * 4 + k + 1)
                        act.activation(l, l, ACT.Ln, bias=c.one[:, 0:1]).then_inc(ln_done, 1)
                    act.wait_ge(dtu_done, i * 4 + 4)
                    act.wait_ge(a_done, i + 1)
                    for gt in range(2):
                        with act.Fori(0, NS // 2) as t:
                            for k in range(4):
                                item = i * 4 * NS + t * 4 + gt * 2 * NS + k
                                if k % 2 == 0:
                                    act.wait_ge(b_ready, i * 2 * NS + t * 2 + gt * NS + k // 2 + 1)
                                    act.wait_ge(dbu_done, item - 2 + DBU0)
                                    act.activation(Bs[:, k // 2, :], pair(0), ACT.Copy).then_inc(bs_done, 1)
                                act.wait_ge(scan_done, item + 1)
                                d = dA[:, k, :].rearrange("p (b l) -> p b l", l=L)[:, :, 1:L]
                                act.activation(d, dt[:, k % 2, half(gt)].rearrange("p (b l) -> p b l", l=L)[:, :, 1:L],
                                               ACT.Exp, scale=A[:, k % 2, ds(t * 2 + k // 2, 1)]).then_inc(da_done, 1)

            @block.vector
            def _(dve):
                dve.sem_inc(xm_ready, XM0)
                dve.sem_inc(dt_done, DT0)
                dve.sem_inc(scan_done, SCAN0)
                dve.sem_inc(hc_done, HC0)
                dve.wait_ge(consts, 6)
                with dve.Fori(0, NBLK) as i:
                    dve.wait_ge(late_in, i * LATE + LATE)
                    for h in range(2):
                        dve.tensor_scalar(dD[:, h, :], c.ident[:, :], Dp[:, h:h + 1], None, ALU.mult).then_inc(dd_done, 1)
                    dve.wait_ge(early_in, i * EARLY + EARLY)
                    for h in range(4):
                        x = sq[:, h * CH:(h + 1) * CH]
                        dve.wait_ge(rstd_done, i * 4 + h + 1)
                        dve.tensor_tensor(x, c.ps[:, h, :], rstd[:, h * CH:(h + 1) * CH], ALU.mult).then_inc(scaled, 1)
                        dve.wait_ge(scaled, i * 4 + h + 1)
                        dve.tensor_scalar(hn[:, 2 * h:2 * h + 2, PAD:PAD + L], x.rearrange("p (b l) -> p b l", l=L),
                                          nw[:, 0:1], nw[:, 1:2], ALU.mult, ALU.add).then_inc(hn_ready, 1)
                    for gt in range(2):
                        dve.wait_ge(bc_p1, i * 2 + gt + 1)
                        dve.tensor_tensor(bcr[:, half(gt)], pair(gt, 96), bc[:, half(gt)], ALU.subtract).then_inc(bc_r, 1)
                    for gt in range(2):
                        dve.wait_ge(bc_p2, i * 2 + gt + 1)
                        dve.tensor_tensor(bcr[64:96, half(gt)], bcr[64:96, half(gt)], bc[64:96, half(gt)],
                                          ALU.subtract).then_inc(bc_r2, 1)
                    for k in range(4):
                        gt, h = divmod(k, 2)
                        d = dt[:, h, half(gt)]
                        dve.wait_ge(abs_done, i * 4 + k + 1)
                        dve.tensor_scalar(d, pair(2 - 2 * gt + h), dtb[:, h:h + 1], 0.0, ALU.add, ALU.max).then_inc(relu_done, 1)
                        dve.wait_ge(relu_done, i * 4 + k + 1)
                        dve.wait_ge(ln_done, i * 4 + k + 1)
                        dve.tensor_tensor(d, d, Bs[:, k % 2, :], ALU.add).then_inc(dt_done, 1)
                        dve.wait_ge(dt_done, i * 4 + k + 1 + DT0)
                        dve.tensor_tensor(dtu[:, h, half(gt)], d, u[:, h, half(gt)], ALU.mult).then_inc(dtu_done, 1)
                    for gt in range(2):
                        with dve.Fori(0, NS // 2) as t:
                            for p in range(2):
                                item = i * 4 * NS + t * 4 + gt * 2 * NS + 2 * p
                                for h in range(2):
                                    k = 2 * p + h
                                    dve.wait_ge(da_done, item + h + 1)
                                    dve.wait_ge(dbu_done, item + h + 1 + DBU0)
                                    dve.tensor_tensor_scan(hs[:, k, :], dA[:, k, :], hs[:, k, :], 0.0,
                                                           ALU.mult, ALU.add).then_inc(scan_done, 1)
                                dve.wait_ge(c_ready, i * 2 * NS + t * 2 + gt * NS + p + 1)
                                for h in range(2):
                                    k = 2 * p + h
                                    dve.wait_ge(scan_done, item + h + 1 + SCAN0)
                                    dve.tensor_tensor(hs[:, k, :], hs[:, k, :], pair(1), ALU.mult).then_inc(hc_done, 1)
                        dve.wait_ge(y_acc, i * 4 * NS + (gt + 1) * 2 * NS + Y0)
                        for h in range(2):
                            dve.tensor_tensor(z[:, h, half(gt)], pair(2 + h), z[:, h, half(gt)], ALU.mult).then_inc(gated, 1)
                    for gt in range(2):
                        dve.wait_ge(out_ps, i * 2 + gt + 1)
                        dve.tensor_tensor(xm[:, half(gt)], xm[:, half(gt)], pair(gt), ALU.add).then_inc(xm_ready, 1)


def expert_stage(c):
    nc = c.nc
    xn = c.xn
    with Stage(c, "moe") as s:
        pr = s.sb("pr", [P, NT, NE])
        st = s.sb("st", [P, 3, NT])
        more = s.sb("more", [P, NT, NE, NE])
        same = s.sb("same", [P, NT, NE, NE])
        before = s.sb("before", [P, NE, NE])
        rank = s.sb("rank", [P, NT, NE])
        pick = s.sb("pick", [P, NT, NE])
        pT = s.sb("pT", [NE, T])
        pTb = s.sb("pTb", [NE, T], BF16)
        sel = s.sb("sel", [NE, NE, P], BF16)
        xe = s.sb("xe", [P, 2, HALF])
        consts, logits, step, exp_done, picked, turned, pT_done, spread, masked, used, acc = (s.sem(x) for x in (
            "consts", "logits", "step", "exp_done", "picked", "turned", "pT_done", "spread", "masked", "used", "acc"))
        out_done = s.sem("out_done")
        NI = 2 * NE

        def pair(k):
            return c.ps[:, 2 * k:2 * k + 2, :].rearrange("p a l -> p (a l)")

        with nc.Block() as block:
            @block.gpsimd
            def _(pool):
                pool.memset(before[:, :, :], 1.0).then_inc(consts, 1)
                pool.memset(sel[:, :, :], 0.0).then_inc(consts, 1)
                pool.wait_ge(consts, 2)
                pool.affine_select(out=before[:, :, :], in_=before[:, :, :], compare_op=ALU.is_gt, fill=0.0, base=0,
                                   pattern=[[1, NE], [-1, NE]], channel_multiplier=0).then_inc(consts, 1)
                pool.affine_select(out=sel[:, :, :], in_=sel[:, :, :], compare_op=ALU.not_equal, fill=1.0, base=0,
                                   pattern=[[-1, NE], [0, P]], channel_multiplier=1).then_inc(consts, 1)

            @block.tensor
            def _(pe):
                for t in range(NT):
                    pe.matmul(c.ps[:, 0, t * NE:(t + 1) * NE], xn[:, t * P:(t + 1) * P], c.rwT[:, :], start=True, stop=False)
                    mm = pe.matmul(c.ps[:, 0, t * NE:(t + 1) * NE], c.ones_f[0:1, :], c.rb[:, :], start=False, stop=True)
                mm.then_inc(logits, 1)
                pe.wait_ge(picked, 1)
                for t in range(NT):
                    mm = pe.transpose(c.ps[0:NE, 4 + t // 4, (t % 4) * P:(t % 4 + 1) * P], pick[:, t, :], c.ident[:, :])
                mm.then_inc(turned, 1)
                pe.wait_ge(consts, 4)
                pe.wait_ge(pT_done, 2)
                for a in range(4):
                    pe.matmul(c.ps[:, 4 + a, :], c.eb[:, :], pT[:, a * CH:(a + 1) * CH], start=True, stop=False,
                              skip_group_check=True)
                for n in range(NI + 1):
                    if n < NI:
                        gt, e = divmod(n, NE)
                        if n >= 2:
                            pe.wait_ge(masked, n - 1)
                        for a in range(2):
                            mm = pe.matmul(c.ps[:, 2 * (n % 2) + a, :], sel[:, e, :],
                                           pTb[:, gt * HALF + a * CH:gt * HALF + (a + 1) * CH], start=True, stop=True)
                        mm.then_inc(spread, 1)
                    if n >= 1:
                        gt, e = divmod(n - 1, NE)
                        pe.wait_ge(masked, n)
                        for a in range(2):
                            mm = pe.matmul(c.ps[:, 4 + 2 * gt + a, :], c.ewT[:, e, :],
                                           xe[:, (n - 1) % 2, a * CH:(a + 1) * CH], start=False, stop=(e == NE - 1),
                                           skip_group_check=True)
                        mm.then_inc(acc, 1)

            @block.scalar
            def _(act):
                act.wait_ge(step, 2)
                act.activation(pr[:, :, :], pr[:, :, :], ACT.Exp).then_inc(exp_done, 1)
                act.wait_ge(pT_done, 1)
                act.activation(pTb[:, :], pT[:, :], ACT.Copy).then_inc(pT_done, 1)

            @block.vector
            def _(dve):
                def each(x):
                    return x.unsqueeze(2).broadcast_to([P, NT, NE])
                lg = c.ps[:, 0, 0:NT * NE].rearrange("p (t e) -> p t e", e=NE)
                dve.wait_ge(logits, 1)
                dve.tensor_reduce(st[:, 0, :], lg, AX.X, ALU.max).then_inc(step, 1)
                dve.wait_ge(step, 1)
                dve.tensor_tensor(pr[:, :, :], lg, each(st[:, 0, :]), ALU.subtract).then_inc(step, 1)
                dve.wait_ge(exp_done, 1)
                dve.tensor_reduce(st[:, 1, :], pr[:, :, :], AX.X, ALU.add).then_inc(step, 1)
                dve.wait_ge(step, 3)
                dve.reciprocal(st[:, 2, :], st[:, 1, :]).then_inc(step, 1)
                dve.wait_ge(step, 4)
                dve.tensor_tensor(pr[:, :, :], pr[:, :, :], each(st[:, 2, :]), ALU.mult).then_inc(step, 1)
                dve.wait_ge(step, 5)
                dve.wait_ge(consts, 4)
                mine = pr[:, :, :].unsqueeze(3).broadcast_to([P, NT, NE, NE])
                other = pr[:, :, :].unsqueeze(2).broadcast_to([P, NT, NE, NE])
                dve.tensor_tensor(more[:, :, :, :], other, mine, ALU.is_gt).then_inc(step, 1)
                dve.tensor_tensor(same[:, :, :, :], other, mine, ALU.is_equal).then_inc(step, 1)
                dve.wait_ge(step, 7)
                flat = same[:, :, :, :].rearrange("p t e j -> p t (e j)")
                dve.tensor_tensor(flat, flat, before[:, :, :].rearrange("p e j -> p (e j)").unsqueeze(1)
                                  .broadcast_to([P, NT, NE * NE]), ALU.mult).then_inc(step, 1)
                dve.wait_ge(step, 8)
                dve.tensor_tensor(more[:, :, :, :], more[:, :, :, :], same[:, :, :, :], ALU.add).then_inc(step, 1)
                dve.wait_ge(step, 9)
                dve.tensor_reduce(rank[:, :, :], more[:, :, :, :], AX.X, ALU.add).then_inc(step, 1)
                dve.wait_ge(step, 10)
                dve.tensor_scalar(pick[:, :, :], rank[:, :, :], 1.5, None, ALU.is_lt).then_inc(picked, 1)
                dve.wait_ge(turned, 1)
                dve.tensor_copy(pT[:, :], c.ps[0:NE, 4:8, :].rearrange("p a l -> p (a l)")).then_inc(pT_done, 1)
                for n in range(NI):
                    gt = n // NE
                    dve.wait_ge(spread, n + 1)
                    if n >= 2:
                        dve.wait_ge(acc, n - 1)
                    dve.tensor_tensor(xe[:, n % 2, :], xn[:, gt * HALF:(gt + 1) * HALF], pair(n % 2),
                                      ALU.mult).then_inc(masked, 1)
                dve.wait_ge(acc, NI)
                for gt in range(2):
                    cols = slice(gt * HALF, (gt + 1) * HALF)
                    dve.tensor_tensor(c.xT[:, cols], c.xT[:, cols], pair(2 + gt), ALU.add).then_inc(out_done, 1)


def store_stage(c, g):
    nc = c.nc
    with Stage(c, "store") as s:
        o = s.sb("o", [P, NT, P])
        turned, copied, stored = s.sem("turned"), s.sem("copied"), s.sem("stored")
        out = g["out"].rearrange("b (t p) d -> p (b t) d", p=P)
        with nc.Block() as block:
            @block.tensor
            def _(pe):
                for n in range(4):
                    for k in range(4):
                        t = 4 * n + k
                        mm = pe.transpose(c.ps[:, n, k * P:(k + 1) * P], c.xT[:, t * P:(t + 1) * P], c.ident[:, :])
                    mm.then_inc(turned, 1)

            @block.vector
            def _(dve):
                for n in range(4):
                    dve.wait_ge(turned, n + 1)
                    dve.tensor_copy(o[:, 4 * n:4 * n + 4, :], c.ps[:, n, :].rearrange("p (k d) -> p k d", k=4)).then_inc(copied, 1)

            @block.sync
            def _(sp):
                for n in range(4):
                    sp.wait_ge(copied, n + 1)
                    sp.dma_start(out[:, 4 * n:4 * n + 4, :], o[:, 4 * n:4 * n + 4, :]).then_inc(stored, 16)
                sp.wait_ge(stored, 64)


def decoder_kernel(nc, g):
    with ExitStack() as ctx:
        c = Chip(nc, ctx)
        c.ps = ctx.enter_context(nc.psum_tensor("ps", [P, 8, CH], F32))
        c.xT = c.sb("xT", [P, T])
        c.cT = c.sb("cT", [P, T])
        c.xn = c.sb("xn", [P, T])
        c.mask1 = g["m1"]
        c.norm_sems = [ctx.enter_context(nc.semaphore(f"norm_{n}")) for n in ("centred", "squared", "var_done", "lnv_done", "rstd_done",
                                                    "scaled", "done")]
        c.norms = 0
        with ExitStack() as layer0:
            c.ctx = ctx
            c.ewT = c.sb("ewT", [P, NE, P])
            c.rwT = c.sb("rwT", [P, NE])
            c.rb = c.sb("rb", [1, NE])
            c.eb = c.sb("eb", [NE, P])
            c.ones_f = c.sb("ones_f", [P, P])
            c.wmean = c.sb("wmean", [P, 3])
            constants(c)
            c.made = []
            c.ctx = layer0
            c.wvo = c.sb("wvo", [P, 4, P])
            c.wqk = c.sb("wqk", [P, 4, P])
            c.bqk = c.sb("bqk", [P, 2])
            c.bv = c.sb("bv", [P, 1])
            c.bo = c.sb("bo", [P, 1])
            c.maskrow = c.sb("maskrow", [P, B, L], BF16)
            c.present = c.sb("present", [P, B])
            c.wguT = c.sb("wguT", [P, 2 * F], BF16)
            c.wdT = c.sb("wdT", [P, 4, P], BF16)
            c.whole = layer0
            load_stage(c, g)
            norm_stage(c, "n1", c.xT, c.xn)
            linear_attention_stage(c)
            norm_stage(c, "n2", c.xT, c.xn)
            cross_attention_stage(c, "x0", P // NH, False, (c.wqk[:, 2, :], c.wqk[:, 3, :], c.wvo[:, 2, :], c.wvo[:, 3, :]))
            norm_stage(c, "n3", c.xT, c.xn)
            ffn_stage(c)
            clear_semaphores(c)
        c.whole = ctx
        norm_stage(c, "n4", c.xT, c.xn)
        mamba_stage(c, g)
        with ExitStack() as last:
            c.ctx = last
            fn = c.sb("fn", [P, 2])
            with Stage(c, "fn") as s:
                fn_in = s.sem("in")
                with nc.Block() as block:
                    @block.sync
                    def _(sp):
                        for k, n in enumerate(("m_fw", "m_fb")):
                            sp.dma_start(fn[:, k:k + 1], g[n].rearrange("(p a) -> p a", a=1)).then_inc(fn_in, 16)
                        sp.wait_ge(fn_in, 32)
            norm_stage(c, "n5", c.xn, None, fn[:, 0:1], fn[:, 1:2], c.xT)
        norm_stage(c, "n6", c.xT, c.xn)
        cross_attention_stage(c, "x1", 64, True, (g["x1q"], g["x1k"], g["x1v"], g["x1o"]))
        norm_stage(c, "n7", c.xT, c.xn)
        expert_stage(c)
        store_stage(c, g)


_NAMES = {
    "x": "x", "ctx_1024": "ctx", "mask_BxS2_ik0": "m0", "mask_BxSxS2_fk1": "m1",
    "L0_attn_Wq": "aq", "L0_attn_Wk": "ak", "L0_attn_Wv": "av", "L0_attn_Wo": "ao",
    "L0_xattn_Wq": "xq", "L0_xattn_bq": "xbq", "L0_xattn_Wk": "xk", "L0_xattn_bk": "xbk",
    "L0_xattn_Wv": "xv", "L0_xattn_bv": "xbv", "L0_xattn_Wo": "xo", "L0_xattn_bo": "xbo",
    "L0_ffn_w_gate": "wg", "L0_ffn_w_up": "wu", "L0_ffn_w_down": "wd",
    "L1_attn_norm_w": "m_nw", "L1_attn_norm_b": "m_nb", "L1_attn_in_proj_w": "m_in", "L1_attn_conv_w": "m_cw",
    "L1_attn_conv_b": "m_cb", "L1_attn_xproj_w": "m_xw", "L1_attn_dtproj_w": "m_dw", "L1_attn_dtproj_b": "m_db",
    "L1_attn_A_log": "m_al", "L1_attn_skip_D": "m_D", "L1_attn_out_proj_w": "m_ow", "L1_attn_fn_w": "m_fw",
    "L1_attn_fn_b": "m_fb", "L1_xattn_w_q": "x1q", "L1_xattn_w_k": "x1k", "L1_xattn_w_v": "x1v",
    "L1_xattn_w_o": "x1o", "L1_ffn_router_w": "rw", "L1_ffn_router_b": "rb", "L1_ffn_expert_w": "ew",
    "L1_ffn_expert_b": "eb",
}


def kernel(**inputs):
    import numpy as _np
    import concourse.bacc as _bacc
    from concourse import mybir as _mybir
    from concourse.bass_utils import run_bass_kernel_spmd as _run

    nc = _bacc.Bacc("TRN2", target_bir_lowering=False, num_devices=1)
    arrays, g = {}, {}
    for name, short in _NAMES.items():
        a = _np.ascontiguousarray(inputs[name])
        arrays[f"in_{name}_dram"] = a
        g[short] = nc.dram_tensor(f"in_{name}_dram", a.shape, _mybir.dt.from_np(a.dtype), kind="ExternalInput").ap()
    g["out"] = nc.dram_tensor("out_0_dram", (B, L, P), _mybir.dt.float32, kind="ExternalOutput").ap()
    decoder_kernel(nc, g)
    r = _run(nc, [arrays], core_ids=[0])
    return r.results[0]["out_0_dram"]
```

```python
from contextlib import ExitStack

import concourse.bass as bass
from concourse import mybir

ALU = mybir.AluOpType
ACT = mybir.ActivationFunctionType
AX = mybir.AxisListType
F32 = mybir.dt.float32
BF16 = mybir.dt.bfloat16
I32 = mybir.dt.int32
ds = bass.ds

P = 128
B = 8
L = 256
T = B * L
NT = T // P
CH = 512
HALF = 1024
NH = 16
ROUND = 12582912.0
MASKED = -1.0e30
F = 512
DI = 256
NS = 16
RANK = 64
TAPS = 4
NBLK = 4
NE = 8


class Chip:

    def __init__(self, nc, ctx):
        self.nc = nc
        self.ctx = ctx
        self.whole = ctx
        self.made = []

    def sb(self, name, shape, dt=F32):
        return self.ctx.enter_context(self.nc.sbuf_tensor(name, shape, dt))

    def psb(self, bank):
        return self.ps[:, bank, :].bitcast(BF16)


class Stage:

    def __init__(self, chip, name):
        self.nc, self.name, self.ctx = chip.nc, name, ExitStack()
        self.whole, self.made = chip.whole, chip.made

    def __enter__(self):
        self.ctx.__enter__()
        return self

    def __exit__(self, *a):
        return self.ctx.__exit__(*a)

    def sb(self, name, shape, dt=F32):
        return self.ctx.enter_context(self.nc.sbuf_tensor(f"{self.name}_{name}", shape, dt))

    def sem(self, name):
        made = self.whole.enter_context(self.nc.semaphore(f"{self.name}_{name}"))
        self.made.append(made)
        return made


def constants(c):
    nc = c.nc
    c.ident = c.sb("ident", [P, P])
    c.identb = c.sb("identb", [P, P], BF16)
    c.centre = c.sb("centre", [P, P])
    c.average = c.sb("average", [P, P])
    c.ones_sq = c.sb("ones_sq", [P, P])
    c.eps = c.sb("eps", [P, 1])
    c.one = c.sb("one", [P, 1])
    with Stage(c, "const") as s:
        made = s.sem("made")
        with nc.Block() as block:
            @block.gpsimd
            def _(pool):
                pool.memset(c.ident[:, :], 0.0).then_inc(made, 1)
                pool.memset(c.average[:, :], 1.0 / P).then_inc(made, 1)
                pool.memset(c.centre[:, :], -1.0 / P).then_inc(made, 1)
                pool.memset(c.ones_sq[:, :], 1.0).then_inc(made, 1)
                pool.memset(c.eps[:, :], 1e-5).then_inc(made, 1)
                pool.memset(c.one[:, :], 1.0).then_inc(made, 1)
                pool.wait_ge(made, 6)
                pool.affine_select(out=c.ident[:, :], in_=c.ident[:, :], compare_op=ALU.not_equal, fill=1.0,
                                   base=0, pattern=[[-1, P]], channel_multiplier=1).then_inc(made, 1)
                pool.affine_select(out=c.centre[:, :], in_=c.centre[:, :], compare_op=ALU.not_equal,
                                   fill=1.0 - 1.0 / P, base=0, pattern=[[-1, P]],
                                   channel_multiplier=1).then_inc(made, 1)
                pool.wait_ge(made, 8)
                pool.tensor_copy(c.identb[:, :], c.ident[:, :]).then_inc(made, 1)
                pool.wait_ge(made, 9)


def load_stage(c, g):
    nc = c.nc
    with Stage(c, "load") as s:
        xt = s.sb("xt", [P, NT, P])
        ct = s.sb("ct", [P, NT, P])
        wa = s.sb("wa", [P, 8, P])
        wg = s.sb("wg", [P, 8, P])
        wd = s.sb("wd", [P, F])
        we = s.sb("we", [P, NE, P])
        wr = s.sb("wr", [NE, P])
        wq = s.sb("wq", [P, 3, 2 * F])
        part = s.sb("part", [P, 3])
        mean = s.sb("mean", [P, 3])
        wscale = s.sb("wscale", [P, 3])
        wgq = s.sb("wgq", [P, 8, P], BF16)
        wdq = s.sb("wdq", [P, F], BF16)

        acts_in, weights_in, small_in = s.sem("acts_in"), s.sem("weights_in"), c.small_in
        turned = s.sem("turned")
        copied_act, copied_dve = s.sem("copied_act"), s.sem("copied_dve")
        sums, mean_done, step, ternary = s.sem("sums"), s.sem("mean_done"), s.sem("step"), s.sem("ternary")
        mask_read, mask_done = s.sem("mask_read"), s.sem("mask_done")
        qturned, qcopied = s.sem("qturned"), s.sem("qcopied")
        mi = s.sb("mi", [P, B, L], I32)
        absent = s.sb("absent", [P, B])
        sq = s.sb("sq", [P, T])
        lnv = s.sb("lnv", [P, T])
        rstd = s.sb("rstd", [P, T])
        centred, squared, var_done, lnv_done, rstd_done, _, normed = c.norm_sems
        c.norms += 1

        jobs = [(ct[:, t, :], P) for t in range(NT)] + [(xt[:, t, :], P) for t in range(NT)]
        jobs += [(wa[:, i, :], P) for i in range(8)] + [(we[:, e, :], P) for e in range(NE)] + [(wr[:, :], NE)]
        banks = [jobs[i:i + 4] for i in range(0, len(jobs), 4)]

        with nc.Block() as block:
            @block.sync
            def _(sp):
                sp.dma_start(ct[:, :, :], g["ctx"].rearrange("b (t p) d -> p (b t) d", p=P)).then_inc(acts_in, 16)
                sp.dma_start(xt[:, :, :], g["x"].rearrange("b (t p) d -> p (b t) d", p=P)).then_inc(acts_in, 16)
                sp.dma_start(we[:, :, :], g["ew"].rearrange("e h d -> h e d")).then_inc(weights_in, 16)
                sp.dma_start(wr[:, :], g["rw"]).then_inc(weights_in, 16)

            @block.scalar
            def _(act):
                for i, n in enumerate(("aq", "ak", "av", "ao", "xq", "xk", "xv", "xo")):
                    act.dma_start(wa[:, i, :], g[n]).then_inc(weights_in, 16)
                act.dma_start(wg[:, 0:4, :], g["wg"].rearrange("(t p) d -> p t d", p=P)).then_inc(weights_in, 16)
                act.dma_start(wg[:, 4:8, :], g["wu"].rearrange("(t p) d -> p t d", p=P)).then_inc(weights_in, 16)
                act.dma_start(wd[:, :], g["wd"]).then_inc(weights_in, 16)
                act.dma_start(mi[:, :, :], g["m0"].rearrange("(a b) k -> a b k", a=1).broadcast_to([P, B, L])
                              ).then_inc(mask_read, 16)
                for n in range(1, 8, 2):
                    act.wait_ge(turned, n + 1)
                    dst = c.cT if n < 4 else c.xT
                    act.activation(dst[:, (n % 4) * CH:(n % 4 + 1) * CH], c.ps[:, n % 4, :], ACT.Copy).then_inc(copied_act, 1)
                for h in range(4):
                    act.wait_ge(centred, h + 1)
                    act.activation(sq[:, h * CH:(h + 1) * CH], c.ps[:, 4 + h, :], ACT.Square).then_inc(squared, 1)
                for h in range(4):
                    act.wait_ge(var_done, h + 1)
                    act.activation(lnv[:, h * CH:(h + 1) * CH], c.ps[:, h, :], ACT.Ln, bias=c.eps[:, 0:1]).then_inc(lnv_done, 1)
                for h in range(4):
                    act.wait_ge(lnv_done, h + 1)
                    act.activation(rstd[:, h * CH:(h + 1) * CH], lnv[:, h * CH:(h + 1) * CH], ACT.Exp,
                                   scale=-0.5).then_inc(rstd_done, 1)

            @block.gpsimd
            def _(pool):
                for k, n in enumerate(("xbq", "xbk")):
                    pool.dma_start(c.bqk[:, k:k + 1], g[n].rearrange("(p a) -> p a", a=1)).then_inc(small_in, 16)
                for k, n in enumerate(("m_fw", "m_fb")):
                    pool.dma_start(c.fn[:, k:k + 1], g[n].rearrange("(p a) -> p a", a=1)).then_inc(small_in, 16)
                pool.dma_start(c.bv[:, :], g["xbv"].rearrange("(p a) -> p a", a=1)).then_inc(small_in, 16)
                pool.dma_start(c.bo[:, :], g["xbo"].rearrange("(p a) -> p a", a=1)).then_inc(small_in, 16)
                pool.dma_start(c.rb[:, :], g["rb"].rearrange("(n a) -> n a", a=1)).then_inc(small_in, 16)
                pool.dma_start(c.eb[:, :], g["eb"]).then_inc(small_in, 16)
                pool.wait_ge(small_in, 16 * 8)

            @block.tensor
            def _(pe):
                pe.wait_ge(acts_in, 32)
                for n, bank in enumerate(banks):
                    if n == 8:
                        for h in range(4):
                            pe.wait_ge((copied_dve, copied_act)[h % 2], 3 + h // 2)
                            pe.matmul(c.ps[:, 4 + h, :], c.centre[:, :], c.xT[:, h * CH:(h + 1) * CH],
                                      start=True, stop=True).then_inc(centred, 1)
                        for h in range(4):
                            pe.wait_ge(squared, h + 1)
                            pe.matmul(c.ps[:, h, :], c.average[:, :], sq[:, h * CH:(h + 1) * CH],
                                      start=True, stop=True).then_inc(var_done, 1)
                        pe.wait_ge(lnv_done, 4)
                        pe.wait_ge(weights_in, 16 * 13)
                    if n >= 4 and n < 12 and n % 2 == 1:
                        pe.wait_ge(copied_act, (n - 4) // 2 + 1)
                    elif 4 <= n < 12:
                        pe.wait_ge(copied_dve, (n - 4) // 2 + 1)
                    elif n >= 12:
                        pe.wait_ge(copied_dve, 4 + n - 11)
                    for k, (src, rows) in enumerate(bank):
                        mm = pe.transpose(c.ps[:, n % 4, k * P:k * P + rows], src, c.ident[0:rows, 0:rows])
                    mm.then_inc(turned, 1)
                pe.wait_ge(sums, 3)
                pe.wait_ge(normed, 4)
                pe.matmul(c.ps[:, 4, 0:3], c.ones_sq[:, :], part[:, :], start=True, stop=True).then_inc(mean_done, 1)
                pe.wait_ge(ternary, 3)
                for n in range(8):
                    pe.transpose(c.psb(5)[:, n * P:(n + 1) * P], wgq[:, n, :], c.identb[:, :])
                for n in range(4):
                    mm = pe.transpose(c.psb(6)[:, n * P:(n + 1) * P], wdq[:, n * P:(n + 1) * P], c.identb[:, :])
                mm.then_inc(qturned, 1)

            @block.vector
            def _(dve):
                for n in range(0, 8, 2):
                    dve.wait_ge(turned, n + 1)
                    dst = c.cT if n < 4 else c.xT
                    dve.tensor_copy(dst[:, (n % 4) * CH:(n % 4 + 1) * CH], c.ps[:, n % 4, :]).then_inc(copied_dve, 1)
                dve.wait_ge(mask_read, 16)
                dve.tensor_scalar(c.maskrow[:, :, :], mi[:, :, :], 0.0, MASKED, ALU.is_equal, ALU.mult).then_inc(mask_done, 1)
                dve.wait_ge(mask_done, 1)
                dve.tensor_reduce(c.present[:, :], c.maskrow[:, :, :], AX.X, ALU.max).then_inc(mask_done, 1)
                dve.wait_ge(mask_done, 2)
                dve.tensor_scalar(c.present[:, :], c.present[:, :], 0.0, None, ALU.is_equal).then_inc(mask_done, 1)
                dve.wait_ge(mask_done, 3)
                dve.reciprocal(absent[:, :], c.present[:, :]).then_inc(mask_done, 1)
                dve.wait_ge(mask_done, 4)
                dve.tensor_tensor(c.present[:, :], c.present[:, :], absent[:, :], ALU.mult).then_inc(mask_done, 1)
                dve.wait_ge(weights_in, 16 * 13)
                for k, src in enumerate((wg[:, 0:4, :], wg[:, 4:8, :], wd[:, :])):
                    dve.tensor_reduce(part[:, k:k + 1], src, AX.XY if k < 2 else AX.X, ALU.add,
                                      apply_absolute_value=True).then_inc(sums, 1)
                for h in range(4):
                    dve.wait_ge(rstd_done, h + 1)
                    dve.tensor_tensor(c.xn[:, h * CH:(h + 1) * CH], c.ps[:, 4 + h, :], rstd[:, h * CH:(h + 1) * CH],
                                      ALU.mult).then_inc(normed, 1)
                for n in (8, 9):
                    a = n - 8
                    dve.wait_ge(turned, n + 1)
                    dve.tensor_copy(c.wqk[:, 2 * a:2 * a + 2, :], c.ps[:, n % 4, 0:2 * P]
                                    .rearrange("p (a d) -> p a d", a=2)).then_inc(step, 1)
                    dve.tensor_copy(c.wvo[:, 2 * a:2 * a + 2, :], c.ps[:, n % 4, 2 * P:4 * P]
                                    .rearrange("p (a d) -> p a d", a=2)).then_inc(copied_dve, 1)
                for n in (10, 11):
                    dve.wait_ge(turned, n + 1)
                    dve.tensor_copy(c.ewT[:, 4 * (n - 10):4 * (n - 10) + 4, :], c.ps[:, n % 4, :]
                                    .rearrange("p (a d) -> p a d", a=4)).then_inc(copied_dve, 1)
                dve.wait_ge(turned, 13)
                dve.tensor_copy(c.rwT[:, :], c.ps[:, 0, 0:NE]).then_inc(copied_dve, 1)
                dve.wait_ge(mean_done, 1)
                dve.tensor_scalar(c.wmean[:, :], c.ps[:, 4, 0:3], 1.0 / (F * P), 1e-5, ALU.mult, ALU.max).then_inc(step, 1)
                dve.wait_ge(step, 3)
                dve.reciprocal(wscale[:, :], c.wmean[:, :]).then_inc(step, 1)
                dve.wait_ge(step, 4)
                for k, src in enumerate((wg[:, 0:4, :], wg[:, 4:8, :], wd[:, :])):
                    w = wq[:, k, 0:F]
                    if k < 2:
                        w = w.rearrange("p (t d) -> p t d", t=4)
                    dve.tensor_scalar(w, src, wscale[:, k:k + 1], ROUND, ALU.mult, ALU.add).then_inc(step, 1)
                dve.wait_ge(step, 7)
                dve.tensor_scalar(wq[:, :, F:2 * F], wq[:, :, 0:F], ROUND, 1.0, ALU.subtract, ALU.min).then_inc(step, 1)
                dve.wait_ge(step, 8)
                for k, dst in enumerate((wgq[:, 0:4, :], wgq[:, 4:8, :], wdq[:, :])):
                    w = wq[:, k, F:2 * F]
                    if k < 2:
                        w = w.rearrange("p (t d) -> p t d", t=4)
                    dve.tensor_scalar(dst, w, -1.0, None, ALU.max).then_inc(ternary, 1)
                dve.wait_ge(qturned, 1)
                dve.tensor_copy(c.wguT[:, :], c.psb(5)[:, 0:8 * P]).then_inc(qcopied, 1)
                dve.tensor_copy(c.wdT[:, :, :], c.psb(6)[:, 0:4 * P].rearrange("p (t d) -> p t d", t=4)).then_inc(qcopied, 1)
                dve.wait_ge(small_in, 16 * 8)
                dve.tensor_scalar(c.bqk[:, 0:1], c.bqk[:, 0:1], 8.0 ** -0.5, None, ALU.mult).then_inc(qcopied, 1)


class Norm:

    def __init__(self, c, sq, lnv, rstd):
        self.c, self.sq, self.lnv, self.rstd = c, sq, lnv, rstd
        self.base = 4 * c.norms
        c.norms += 1

    def on_tensor(self, pe):
        c, base = self.c, self.base
        centred, squared, var_done, _, _, _, done = c.norm_sems
        for h in range(4):
            pe.matmul(c.ps[:, h, :], c.centre[:, :], c.xT[:, h * CH:(h + 1) * CH], start=True, stop=True).then_inc(centred, 1)
        for h in range(4):
            pe.wait_ge(squared, base + h + 1)
            pe.matmul(c.ps[:, 4 + h, :], c.average[:, :], self.sq[:, h * CH:(h + 1) * CH],
                      start=True, stop=True).then_inc(var_done, 1)
        pe.wait_ge(done, base + 4)

    def on_scalar(self, act):
        c, base = self.c, self.base
        centred, squared, var_done, lnv_done, rstd_done, _, _ = c.norm_sems
        for h in range(4):
            act.wait_ge(centred, base + h + 1)
            act.activation(self.sq[:, h * CH:(h + 1) * CH], c.ps[:, h, :], ACT.Square).then_inc(squared, 1)
        for h in range(4):
            act.wait_ge(var_done, base + h + 1)
            act.activation(self.lnv[:, h * CH:(h + 1) * CH], c.ps[:, 4 + h, :], ACT.Ln, bias=c.eps[:, 0:1]).then_inc(lnv_done, 1)
        for h in range(4):
            act.wait_ge(lnv_done, base + h + 1)
            act.activation(self.rstd[:, h * CH:(h + 1) * CH], self.lnv[:, h * CH:(h + 1) * CH], ACT.Exp,
                           scale=-0.5).then_inc(rstd_done, 1)

    def on_vector(self, dve):
        c, base = self.c, self.base
        _, _, _, _, rstd_done, _, done = c.norm_sems
        for h in range(4):
            dve.wait_ge(rstd_done, base + h + 1)
            dve.tensor_tensor(c.xn[:, h * CH:(h + 1) * CH], c.ps[:, h, :], self.rstd[:, h * CH:(h + 1) * CH],
                              ALU.mult).then_inc(done, 1)
        dve.wait_ge(done, base + 4)


def norm_stage(c, name, src, dst, gain=None, bias=None, add_to=None, prefetch=None, cleared=()):
    nc = c.nc
    with Stage(c, name) as s:
        sq = s.sb("sq", [P, T])
        lnv = s.sb("lnv", [P, T])
        rstd = s.sb("rstd", [P, T])
        centred, squared, var_done, lnv_done, rstd_done, scaled, done = c.norm_sems
        base = 4 * c.norms
        c.norms += 1
        with nc.Block() as block:
            if prefetch:
                @block.sync
                def _(sp):
                    prefetch(sp)

                @block.gpsimd
                def _(pool):
                    for made in cleared:
                        pool.sem_clear(made)

            @block.tensor
            def _(pe):
                for h in range(4):
                    pe.matmul(c.ps[:, h, :], c.centre[:, :], src[:, h * CH:(h + 1) * CH],
                              start=True, stop=True).then_inc(centred, 1)
                for h in range(4):
                    pe.wait_ge(squared, base + h + 1)
                    pe.matmul(c.ps[:, 4 + h, :], c.average[:, :], sq[:, h * CH:(h + 1) * CH],
                              start=True, stop=True).then_inc(var_done, 1)

            @block.scalar
            def _(act):
                for h in range(4):
                    act.wait_ge(centred, base + h + 1)
                    act.activation(sq[:, h * CH:(h + 1) * CH], c.ps[:, h, :], ACT.Square).then_inc(squared, 1)
                for h in range(4):
                    act.wait_ge(var_done, base + h + 1)
                    act.activation(lnv[:, h * CH:(h + 1) * CH], c.ps[:, 4 + h, :], ACT.Ln,
                                   bias=c.eps[:, 0:1]).then_inc(lnv_done, 1)
                for h in range(4):
                    act.wait_ge(lnv_done, base + h + 1)
                    act.activation(rstd[:, h * CH:(h + 1) * CH], lnv[:, h * CH:(h + 1) * CH], ACT.Exp,
                                   scale=-0.5).then_inc(rstd_done, 1)

            @block.vector
            def _(dve):
                for h in range(4):
                    cols = slice(h * CH, (h + 1) * CH)
                    dve.wait_ge(rstd_done, base + h + 1)
                    if add_to is None and gain is None:
                        dve.tensor_tensor(dst[:, cols], c.ps[:, h, :], rstd[:, cols], ALU.mult).then_inc(done, 1)
                        continue
                    dve.tensor_tensor(sq[:, cols], c.ps[:, h, :], rstd[:, cols], ALU.mult).then_inc(scaled, 1)
                    dve.wait_ge(scaled, 2 * h + 1)
                    dve.tensor_scalar(lnv[:, cols], sq[:, cols], gain, bias, ALU.mult, ALU.add).then_inc(scaled, 1)
                    dve.wait_ge(scaled, 2 * h + 2)
                    dve.tensor_tensor(add_to[:, cols], add_to[:, cols], lnv[:, cols], ALU.add).then_inc(done, 1)


def linear_attention_stage(c):
    nc = c.nc
    D = P // NH
    RS = 8
    GRP = 4
    NG = NH // GRP

    def head(n):
        return 4 * (n % 4) + n // 4

    with Stage(c, "la") as s:
        xb = s.sb("xb", [P, 2, L])
        low = s.sb("low", [P, 2 * L])
        qk = s.sb("qk", [P, 2, 2, L])
        qm = s.sb("qm", [P, 2, NH, L])
        cum = s.sb("cum", [P, L])
        qc = s.sb("qc", [P, L])
        rec = s.sb("rec", [P, 2, L])
        v = s.sb("v", [P, 2, 2, 4, 160])
        sc = s.sb("sc", [P, RS, 3 * P])
        tri = s.sb("tri", [P, 3, P])
        ones = s.sb("ones", [P, L])
        mine = s.sb("mine", [P, NH])
        group = s.sb("group", [P, NH, D])
        on = s.sb("on", [P, L])
        (made, x_in, proj, v_proj, low_done, exp_done, feat, cum_done, qc_done, den_done, rec_done, v_done, qm_done,
         scores, sc_done, pv, scaled, on_done, out_done, x_done) = (s.sem(n) for n in (
            "made x_in proj v_proj low_done exp_done feat cum_done qc_done den_done rec_done v_done qm_done "
            "scores sc_done pv scaled on_done out_done x_done").split())

        def looped(eng, body):
            body(0, 0, True, True, False)
            body(1, 1, True, False, False)
            with eng.Fori(1, B // 2 - 1) as i:
                body(i * 2, 0, False, False, False)
                body(i * 2 + 1, 1, False, False, False)
            body(B - 2, 0, False, False, False)
            body(B - 1, 1, False, False, True)

        with nc.Block() as block:
            @block.gpsimd
            def _(pool):
                pool.memset(tri[:, :, :], 1.0).then_inc(made, 1)
                pool.memset(v[:, :, :, :, :], 0.0).then_inc(made, 1)
                pool.memset(mine[:, :], 1.0).then_inc(made, 1)
                pool.memset(group[:, :, :], 1.0).then_inc(made, 1)
                pool.memset(ones[:, :], 1.0).then_inc(made, 1)
                pool.wait_ge(made, 5)
                for k in (0, 2):
                    pool.affine_select(out=tri[:, k, :], in_=tri[:, k, :], compare_op=ALU.is_ge, fill=0.0,
                                       base=0, pattern=[[1, P]], channel_multiplier=-1).then_inc(made, 1)
                for dst, rest in ((mine[:, :], []), (group[:, :, :], [[0, D]])):
                    pool.affine_select(out=dst, in_=dst, compare_op=ALU.is_ge, fill=0.0, base=0,
                                       pattern=[[-D, NH]] + rest, channel_multiplier=1).then_inc(made, 1)
                pool.wait_ge(made, 9)
                for dst, rest in ((mine[:, :], []), (group[:, :, :], [[0, D]])):
                    pool.affine_select(out=dst, in_=dst, compare_op=ALU.is_ge, fill=0.0, base=D - 1,
                                       pattern=[[D, NH]] + rest, channel_multiplier=-1).then_inc(made, 1)

            @block.tensor
            def _(pe):
                def project(b, p, first):
                    pe.wait_ge(x_in, b + 1)
                    if not first:
                        pe.wait_ge(feat, b)
                        pe.wait_ge(v_done, b)
                    for k in range(2):
                        mm = pe.matmul(c.ps[:, 6, k * L:(k + 1) * L], c.wqk[:, k, :], xb[:, p, :], start=True, stop=True)
                    mm.then_inc(proj, 1)
                    for t in range(2):
                        mm = pe.matmul(c.ps[:, 7, t * P:(t + 1) * P], xb[:, p, t * P:(t + 1) * P], c.wvo[:, 0, :],
                                       start=True, stop=True)
                    mm.then_inc(v_proj, 1)

                def denominator(b, first):
                    pe.wait_ge(qc_done, b + 1)
                    if not first:
                        pe.wait_ge(rec_done, b)
                    pe.matmul(c.ps[:, 4, 0:L], group[:, :, :].rearrange("p h d -> p (h d)"), qc[:, :],
                              start=True, stop=True).then_inc(den_done, 1)

                def score(b, p, n, first):
                    h = head(n)
                    bank = c.ps[:, n % 2, :]
                    pe.wait_ge(qm_done, b * NH + n + 1)
                    if n >= 2 or not first:
                        pe.wait_ge(sc_done, b * NH + n - 1)
                    pe.matmul(bank[:, 0:L], qk[:, p, 1, 0:P], qm[:, p, h, :], start=True, stop=True)
                    pe.matmul(bank[:, L:L + P], qk[:, p, 1, P:L], qm[:, p, h, P:L],
                              start=True, stop=True).then_inc(scores, 1)

                def weigh(b, p, g, fresh):
                    if g == 0:
                        pe.wait_ge(v_done, b + 1)
                        if not fresh:
                            pe.wait_ge(scaled, b - 1)
                    pe.wait_ge(sc_done, b * NH + (g + 1) * GRP)
                    for kt in range(2):
                        for n in range(g * GRP, (g + 1) * GRP):
                            h = head(n)
                            i, a = h // 4, h % 4
                            mm = pe.matmul(c.ps[32 * i:32 * i + 32, 2 + p, kt * P:L], v[:, p, kt, i, 32 * a:32 * a + 32],
                                           sc[:, n % RS, 0:L] if kt == 0 else sc[:, n % RS, L:L + P],
                                           start=(g == 0 and kt == 0), stop=(g == NG - 1 and kt == 1),
                                           skip_group_check=True)
                    mm.then_inc(pv, 1)

                def out_projection(b, fresh):
                    pe.wait_ge(on_done, b)
                    if not fresh:
                        pe.wait_ge(x_done, b - 1)
                    pe.matmul(c.ps[:, 5, 0:L], c.wvo[:, 1, :], on[:, :], start=True, stop=True).then_inc(out_done, 1)

                pe.wait_ge(made, 11)
                project(0, 0, True)
                denominator(0, True)

                def body(b, p, fresh, first, last):
                    for n in range(NH):
                        score(b, p, n, first)
                        if n == 1 and not first:
                            weigh(b - 1, 1 - p, NG - 1, True)
                        if n == 3 and not last:
                            project(b + 1, 1 - p, False)
                        if n == 6 and not first:
                            out_projection(b, fresh)
                        if n > GRP and n % GRP == 1:
                            weigh(b, p, n // GRP - 1, fresh)
                        if n == 12 and not last:
                            denominator(b + 1, False)
                looped(pe, body)
                weigh(B - 1, 1, NG - 1, True)
                out_projection(B, False)

            @block.scalar
            def _(act):
                def copy_x(b, p, fresh):
                    if not fresh:
                        act.wait_ge(v_proj, b - 1)
                    act.activation(xb[:, p, :], c.xn[:, ds(b * L, L)], ACT.Copy).then_inc(x_in, 1)

                def prepare(b, p, fresh):
                    act.wait_ge(proj, b + 1)
                    act.activation(low[:, :], c.ps[:, 6, :], ACT.Relu, scale=-1.0).then_inc(low_done, 1)
                    act.wait_ge(low_done, b + 1)
                    act.activation(low[:, :], low[:, :], ACT.Exp, scale=-1.0).then_inc(exp_done, 1)
                    act.wait_ge(v_proj, b + 1)
                    if not fresh:
                        act.wait_ge(pv, b * NG - NG)
                    act.activation(v[:, p, :, :, :].rearrange("p t i (a c) -> p (t i) a c", c=40)[:, :, :, 0:D],
                                   c.ps[:, 7, 0:L].rearrange("p (i a d) -> p i a d", a=4, d=D), ACT.Copy).then_inc(v_done, 1)
                    act.wait_ge(feat, b + 1)
                    if not fresh:
                        act.wait_ge(scores, b * NH - NH)
                    for n in range(NH):
                        h = head(n)
                        act.activation(qm[:, p, h, :], qk[:, p, 0, :], ACT.Copy, scale=mine[:, h:h + 1]).then_inc(qm_done, 1)

                act.wait_ge(made, 11)
                copy_x(0, 0, True)
                copy_x(1, 1, True)
                prepare(0, 0, True)

                prepare(1, 1, True)
                copy_x(2, 0, False)
                prepare(2, 0, False)
                copy_x(3, 1, False)
                with act.Fori(1, B // 2 - 1) as i:
                    for p in range(2):
                        prepare(i * 2 + p + 1, 1 - p, False)
                        copy_x(i * 2 + p + 2, p, False)
                prepare(B - 1, 1, False)

            @block.vector
            def _(dve):
                def features(b, p):
                    dve.wait_ge(exp_done, b + 1)
                    dve.scalar_tensor_tensor(out=qk[:, p, :, :].rearrange("p a l -> p (a l)"), in0=c.ps[:, 6, :],
                                             scalar=0.0, in1=low[:, :], op0=ALU.max, op1=ALU.add).then_inc(feat, 1)
                    dve.wait_ge(feat, b + 1)
                    dve.tensor_tensor_scan(cum[:, :], ones[:, :], qk[:, p, 1, :], 0.0, ALU.mult, ALU.add).then_inc(cum_done, 1)
                    dve.wait_ge(cum_done, b + 1)
                    dve.tensor_tensor(qc[:, :], qk[:, p, 0, :], cum[:, :], ALU.mult).then_inc(qc_done, 1)

                def invert(b, p):
                    dve.wait_ge(den_done, b + 1)
                    dve.reciprocal(rec[:, p, :], c.ps[:, 4, 0:L]).then_inc(rec_done, 1)

                def keep_causal(b, n, first):
                    dve.wait_ge(scores, b * NH + n + 1)
                    if n >= RS or not first:
                        dve.wait_ge(pv, b * NG + (n - RS) // GRP + 1)
                    dve.tensor_tensor(sc[:, n % RS, :], c.ps[:, n % 2, 0:3 * P], tri[:, :, :].rearrange("p a q -> p (a q)"),
                                      ALU.mult).then_inc(sc_done, 1)

                def divide(b, p):
                    dve.wait_ge(pv, b * NG + NG)
                    dve.wait_ge(rec_done, b + 1)
                    dve.tensor_tensor(on[:, :], c.ps[:, 2 + p, 0:L], rec[:, p, :], ALU.mult).then_inc(scaled, 1)
                    dve.wait_ge(scaled, b + 1)
                    dve.tensor_scalar(on[:, :], on[:, :], 1e-12, None, ALU.add).then_inc(on_done, 1)

                def finish(b):
                    dve.wait_ge(out_done, b + 1)
                    dve.tensor_tensor(c.xT[:, ds(b * L, L)], c.xT[:, ds(b * L, L)], c.ps[:, 5, 0:L],
                                      ALU.add).then_inc(x_done, 1)

                dve.wait_ge(made, 11)
                features(0, 0)
                invert(0, 0)

                def body(b, p, fresh, first, last):
                    for n in range(NH):
                        keep_causal(b, n, first)
                        if n == 2 and not first:
                            divide(b - 1, 1 - p)
                        if n == 7 and not first:
                            finish(b - 1)
                        if n == 8 and not last:
                            features(b + 1, 1 - p)
                        if n == 13 and not last:
                            invert(b + 1, 1 - p)
                looped(dve, body)
                divide(B - 1, 1)
                finish(B - 1)


def cross_attention_stage(c, name, D, masked_rows, weights):
    nc = c.nc
    small = not masked_rows
    W = NH * D
    OG = W // P
    QB = max(1, OG // 2)
    NQK = 2 * QB
    NV = max(1, 2 * W // CH)
    NP = NQK + NV
    GRP = 4 if small else 2
    NG = NH // GRP
    NO = 1 if small else 4
    RP, RT = 8, 8
    LAG = 4
    FIRST_UNIT = NH // 2
    SCALE = float(D) ** -0.5
    O0 = 4
    WO = 5 if small else 7
    wq, wk, wv, wo = weights
    m = None if small else c.mask1

    def head(n):
        return 4 * (n % 4) + n // 4 if small else n

    with Stage(c, name) as s:
        cb = s.sb("cb", [P, L])
        q = s.sb("q", [P, 2, OG, L])
        mx = s.sb("mx", [P, 2, 2])
        den = s.sb("den", [P, RP, 2])
        rec = s.sb("rec", [P, RP, 2])
        pr = s.sb("pr", [P, RP, 2, L])
        pT = s.sb("pT", [P, RT, 2, L])
        oT = s.sb("oT", [P, OG, L])
        sm = s.sb("sm", [P, 2, 2, L])
        if masked_rows:
            k = s.sb("k", [P, 2, NH, L])
            v = s.sb("v", [P, 2, 2, W])
            neg = s.sb("neg", [P, 2, L])
        else:
            k = s.sb("k", [P, 2, L])
            v = s.sb("v", [P, 2, 2, 4, 160])
            mr = s.sb("mr", [P, 2, L])
            km = s.sb("km", [P, 2, NH, L])
            mine = s.sb("mine", [P, NH])
        (consts, ctx_in, proj, evac, neg_done, km_done, scores, s_free, shifted, max_done,
         exp_done, rec_done, pr_done, turned, pT_done, pv, oT_done, out_done, x_done) = (s.sem(n) for n in (
            "consts ctx_in proj evac neg_done km_done scores s_free shifted max_done exp_done "
            "rec_done pr_done turned pT_done pv oT_done out_done x_done").split())

        flat = pr[:, :, :, :].rearrange("p a t k -> p (a t k)")
        norm = Norm(c, flat[:, 0:T], flat[:, T:2 * T], pT[:, 0:RT // 2, :, :].rearrange("p a t q -> p (a t q)"))

        def looped(eng, body):
            body(0, 0, True, True, False)
            body(1, 1, True, False, False)
            with eng.Fori(1, B // 2 - 1) as i:
                body(i * 2, 0, False, False, False)
                body(i * 2 + 1, 1, False, False, False)
            body(B - 2, 0, False, False, False)
            body(B - 1, 1, False, False, True)

        def units(n):
            a = n - FIRST_UNIT
            return range(min(NP, a * 3 // 2), min(NP, (a + 1) * 3 // 2)) if a >= 0 else range(0)

        def late(n, lag, b, p, first):
            if n >= lag:
                return [(n - lag, b, p, first)] if n - lag < NH else []
            return [] if first else [(n - lag + NH, b - 1, 1 - p, False)]

        def groups(n, b, p, first):
            done = n - LAG
            if done <= 0:
                if first or done % GRP or done + NH <= 0:
                    return []
                return [((done + NH) // GRP - 1, b - 1, 1 - p, False)]
            return [(done // GRP - 1, b, p, first)] if done % GRP == 0 and done <= NH else []

        with nc.Block() as block:
            @block.gpsimd
            def _(pool):
                if small:
                    pool.memset(v[:, :, :, :], 0.0).then_inc(consts, 1)
                    pool.memset(mine[:, :], 1.0).then_inc(consts, 1)
                    pool.wait_ge(consts, 2)
                    pool.affine_select(out=mine[:, :], in_=mine[:, :], compare_op=ALU.is_ge, fill=0.0, base=0,
                                       pattern=[[-D, NH]], channel_multiplier=1).then_inc(consts, 1)
                    pool.wait_ge(consts, 3)
                    pool.affine_select(out=mine[:, :], in_=mine[:, :], compare_op=ALU.is_ge, fill=0.0, base=D - 1,
                                       pattern=[[D, NH]], channel_multiplier=-1).then_inc(consts, 1)

                else:
                    pool.memset(k[:, :, :], 0.0).then_inc(consts, 1)

                def body(b, p, fresh, first, last):
                    for n in range(NH):
                        pool.wait_ge(rec_done, b * NH + n + 1)
                        r = n % RP
                        pool.tensor_tensor(pr[:, r, :, :], pr[:, r, :, :],
                                           rec[:, r, :].unsqueeze(2).broadcast_to([P, 2, L]), ALU.mult).then_inc(pr_done, 1)
                looped(pool, body)

            @block.tensor
            def _(pe):
                norm.on_tensor(pe)
                if masked_rows:
                    pe.wait_ge(c.w1_in, 64)

                def project(b, n, first, second):
                    bank = c.ps[:, 6 + n % 2, :]
                    if n >= 2:
                        pe.wait_ge(evac, b * NP + n - 1)
                    elif not first:
                        pe.wait_ge(evac, b * NP)
                    if 6 + n == WO and not first and not second:
                        pe.wait_ge(x_done, b - 1)
                    if n < NQK:
                        w, src = (wq, c.xn) if n < QB else (wk, c.cT)
                        for j in range(min(2, OG)):
                            gr = 2 * (n % QB) + j
                            mm = pe.matmul(bank[:, j * L:(j + 1) * L], w[:, gr * P:(gr + 1) * P],
                                           src[:, ds(b * L, L)], start=True, stop=True)
                    else:
                        if n == NQK:
                            pe.wait_ge(ctx_in, b + 1)
                        if small:
                            for t in range(2):
                                mm = pe.matmul(bank[:, t * P:(t + 1) * P], cb[:, t * P:(t + 1) * P], wv,
                                               start=True, stop=True)
                        else:
                            t, half = divmod(n - NQK, 2)
                            mm = pe.matmul(bank, cb[:, t * P:(t + 1) * P], wv[:, half * CH:(half + 1) * CH],
                                           start=True, stop=True)
                    mm.then_inc(proj, 1)

                def score(b, p, n, first):
                    bank = c.ps[:, n % 2, :]
                    if n == 0:
                        pe.wait_ge(evac, b * NP + NQK)
                    if n >= 2 or not first:
                        pe.wait_ge(max_done if small else s_free, b * NH + n - 1)
                    h = head(n)
                    if small:
                        pe.wait_ge(km_done, b * NH + n + 1)
                    for t in range(2):
                        if small:
                            mm = pe.matmul(bank[:, t * L:(t + 1) * L], q[:, p, 0, t * P:(t + 1) * P], km[:, p, h, :],
                                           start=True, stop=True)
                        else:
                            mm = pe.matmul(bank[:, t * L:(t + 1) * L], q[:, p, h // 2, t * P:(t + 1) * P],
                                           k[:, p, h, :], start=True, stop=True)
                    mm.then_inc(scores, 1)

                def turn(b, n, first):
                    pe.wait_ge(pr_done, b * NH + n + 1)
                    if n >= 2 or not first:
                        pe.wait_ge(pT_done, b * NH + n - 1)
                    for kt in range(2):
                        for t in range(2):
                            mm = pe.transpose(c.ps[:, 2 + n % 2, kt * L + t * P:kt * L + (t + 1) * P],
                                              pr[:, n % RP, t, kt * P:(kt + 1) * P], c.ident[:, :])
                    mm.then_inc(turned, 1)

                def weigh(b, p, g, first):
                    if g == 0:
                        pe.wait_ge(evac, b * NP + NP)
                        if small and not first:
                            pe.wait_ge(oT_done, b)
                    if not small and g % 2 == 0 and (g >= 4 or not first):
                        pe.wait_ge(oT_done, b * NO + g // 2 - 1)
                    pe.wait_ge(pT_done, b * NH + (g + 1) * GRP)
                    for kt in range(2):
                        for n in range(g * GRP, (g + 1) * GRP):
                            h = head(n)
                            if small:
                                i, a = h // 4, h % 4
                                mm = pe.matmul(c.ps[32 * i:32 * i + 32, O0, 0:L], v[:, p, kt, i, 32 * a:32 * a + 32],
                                               pT[:, n % RT, kt, :], start=(g == 0 and kt == 0),
                                               stop=(g == NG - 1 and kt == 1), skip_group_check=True)
                            else:
                                r = h % 2
                                at = (h // 2 % 2) * L
                                mm = pe.matmul(c.ps[64 * r:64 * r + 64, O0 + h // 4 % 2, at:at + L],
                                               v[:, p, kt, h * D:(h + 1) * D], pT[:, n % RT, kt, :],
                                               start=(kt == 0), stop=(kt == 1))
                    mm.then_inc(pv, 1)

                def out_projection(b, fresh, last):
                    pe.wait_ge(oT_done, b * NO)
                    if not fresh:
                        pe.wait_ge(x_done, b - 1)
                    if not small and not last:
                        pe.wait_ge(evac, b * NP + NP)
                    for gr in range(OG):
                        mm = pe.matmul(c.ps[:, WO, 0:L], wo[:, gr * P:(gr + 1) * P], oT[:, gr, :],
                                       start=(gr == 0), stop=(gr == OG - 1))
                    mm.then_inc(out_done, 1)

                for n in range(NP):
                    project(0, n, True, False)

                def step(b, p, n, first):
                    for a, b_, p_, f in late(n, LAG, b, p, first):
                        turn(b_, a, f)
                    for g, b_, p_, f in groups(n, b, p, first):
                        weigh(b_, p_, g, f)

                def body(b, p, fresh, first, last):
                    for n in range(NH):
                        score(b, p, n, first)
                        if not last:
                            for a in units(n):
                                project(b + 1, a, False, first)
                        if n == LAG + 3 and not first:
                            out_projection(b, fresh, False)
                        step(b, p, n, first)
                looped(pe, body)
                for n in range(NH, NH + LAG + 1):
                    step(B - 1, 1, n, False)
                out_projection(B, False, True)

            def evacuate_turned(eng, b, n, first):
                eng.wait_ge(turned, b * NH + n + 1)
                if n >= RT or not first:
                    eng.wait_ge(pv, b * NG + (n - RT) // GRP + 1)
                src = c.ps[:, 2 + n % 2, :]
                dst = pT[:, n % RT, :, :].rearrange("p t q -> p (t q)")
                if small:
                    eng.tensor_copy(dst, src).then_inc(pT_done, 1)
                else:
                    eng.activation(dst, src, ACT.Copy).then_inc(pT_done, 1)

            @block.scalar
            def _(act):
                norm.on_scalar(act)
                def evacuate(b, p, n, first, second):
                    act.wait_ge(proj, b * NP + n + 1)
                    bank = c.ps[:, 6 + n % 2, :]
                    if n < NQK:
                        scale = SCALE if n < QB else 1.0
                        if n == 0 and not first and not second:
                            act.wait_ge(pv, b * NG - NG)
                        if small:
                            if n == 1:
                                act.activation(mr[:, p, :], c.maskrow[:, ds(b, 1), :].rearrange("p a k -> p (a k)"), ACT.Copy)
                            act.activation(q[:, p, 0, :] if n < QB else k[:, p, :], bank[:, 0:L], ACT.Identity, scale=scale,
                                           bias=c.bqk[:, n:n + 1]).then_inc(evac, 1)
                        else:
                            gr = 2 * (n % QB)
                            if n < QB:
                                a = act.activation(q[:, p, gr:gr + 2, :].rearrange("p j l -> p (j l)"), bank,
                                                   ACT.Copy, scale=scale)
                            for r in range(2) if n >= QB else ():
                                row = slice(64 * r, 64 * r + 64)
                                a = act.activation(k[row, p, 2 * gr:2 * gr + 4, :].rearrange("p (j r) l -> p j r l", r=2)[:, :, r, :],
                                                   bank[row, :].rearrange("p (j l) -> p j l", j=2), ACT.Copy)
                            a.then_inc(evac, 1)
                        return
                    if small:
                        act.activation(v[:, p, :, :, :].rearrange("p t i (a c) -> p (t i) a c", c=40)[:, :, :, 0:D],
                                       bank[:, 0:L].rearrange("p (i a d) -> p i a d", a=4, d=D),
                                       ACT.Copy).then_inc(evac, 1)
                    else:
                        t, half = divmod(n - NQK, 2)
                        act.activation(v[:, p, t, half * CH:(half + 1) * CH], bank, ACT.Copy).then_inc(evac, 1)

                act.activation(cb[:, :], c.cT[:, 0:L], ACT.Copy).then_inc(ctx_in, 1)
                act.wait_ge(consts, 4 if small else 1)
                def keys_of_head(b, p, n):
                    h = head(n)
                    act.activation(km[:, p, h, :], k[:, p, :], ACT.Copy, scale=mine[:, h:h + 1]).then_inc(km_done, 1)

                for n in range(NP):
                    evacuate(0, 0, n, True, False)
                if small:
                    act.wait_ge(evac, NQK)
                    for n in range(4):
                        keys_of_head(0, 0, n)

                def step(b, p, n, first):
                    if masked_rows:
                        for a, b_, p_, f in late(n, LAG, b, p, first):
                            evacuate_turned(act, b_, a, f)

                def body(b, p, fresh, first, last):
                    for n in range(NH):
                        if not last:
                            for a in units(n):
                                evacuate(b + 1, 1 - p, a, False, first)
                        if small and n + 4 < NH:
                            keys_of_head(b, p, n + 4)
                        elif small and not last:
                            if n + 4 == NH:
                                act.wait_ge(evac, b * NP + NP + NQK)
                            keys_of_head(b + 1, 1 - p, n + 4 - NH)
                        step(b, p, n, first)
                        if n >= RP or not first:
                            act.wait_ge(turned, b * NH + n - RP + 1)
                        act.wait_ge(max_done, b * NH + n + 1)
                        for t in range(2):
                            a = act.activation(pr[:, n % RP, t, :], sm[:, n % 2, t, :], ACT.Exp,
                                               bias=mx[:, n % 2, t:t + 1], scale=-1.0,
                                               accum_out=den[:, n % RP, t:t + 1])
                        a.then_inc(exp_done, 1)
                        if n == 4 and not last:
                            act.wait_ge(proj, b * NP + NP)
                            act.activation(cb[:, :], c.cT[:, ds(b * L + L, L)], ACT.Copy).then_inc(ctx_in, 1)
                looped(act, body)
                for n in range(NH, NH + LAG):
                    step(B - 1, 1, n, False)

            @block.vector
            def _(dve):
                norm.on_vector(dve)
                def maximum(b, p, n, first):
                    dve.wait_ge(scores, b * NH + n + 1)
                    bank = c.ps[:, n % 2, :].rearrange("p (t k) -> p t k", t=2)
                    if n >= 2 or not first:
                        dve.wait_ge(exp_done, b * NH + n - 1)
                    if not small:
                        dve.tensor_tensor(sm[:, n % 2, :, :], bank, m[:, ds(b * 2, 2), :], ALU.mult).then_inc(s_free, 1)
                        dve.wait_ge(s_free, b * NH + n + 1)
                    dve.sem_inc(shifted, 1)
                    for t in range(2):
                        a = dve.tensor_tensor_reduce(sm[:, n % 2, t, :], bank[:, t, :] if small else sm[:, n % 2, t, :],
                                                     mr[:, p, :] if small else neg[:, t, :], -1.0, 3.0e38,
                                                     ALU.add, ALU.min, accum_out=mx[:, n % 2, t:t + 1])
                    a.then_inc(max_done, 1)

                def invert(b, n, first):
                    dve.wait_ge(exp_done, b * NH + n + 1)
                    if n >= RP or not first:
                        dve.wait_ge(pr_done, b * NH + n - RP + 1)
                    dve.reciprocal(rec[:, n % RP, :], den[:, n % RP, :]).then_inc(rec_done, 1)

                def output_bank(b, u, first):
                    dve.wait_ge(pv, b * NG + (u + 1) * NG // NO)
                    if small:
                        dve.tensor_scalar(oT[:, 0, :], c.ps[:, O0, 0:L], c.bv[:, 0:1], c.present[:, ds(b, 1)],
                                          ALU.add, ALU.mult).then_inc(oT_done, 1)
                    else:
                        dve.tensor_copy(oT[:, 2 * u:2 * u + 2, :].rearrange("p g q -> p (g q)"),
                                        c.ps[:, O0 + u % 2, :]).then_inc(oT_done, 1)

                def finish(b):
                    dve.wait_ge(out_done, b)
                    cols = c.xT[:, ds(b * L - L, L)]
                    if small:
                        dve.scalar_tensor_tensor(out=cols, in0=c.ps[:, WO, 0:L], scalar=c.bo[:, 0:1], in1=cols,
                                                 op0=ALU.add, op1=ALU.add).then_inc(x_done, 1)
                    else:
                        dve.tensor_tensor(cols, cols, c.ps[:, WO, 0:L], ALU.add).then_inc(x_done, 1)

                if small:
                    dve.wait_ge(consts, 4)
                else:
                    dve.wait_ge(c.mask1_in, 16)

                def step(b, p, n, first):
                    for a, b_, p_, f in late(n, 1, b, p, first):
                        invert(b_, a, f)
                    if small:
                        for a, b_, p_, f in late(n, LAG, b, p, first):
                            evacuate_turned(dve, b_, a, f)
                    for g, b_, p_, f in groups(n - 1, b, p, first):
                        if (g + 1) % (NG // NO) == 0:
                            output_bank(b_, (g + 1) // (NG // NO) - 1, f)

                def body(b, p, fresh, first, last):
                    if masked_rows:
                        if not first:
                            dve.wait_ge(max_done, b * NH)
                        dve.tensor_scalar(neg[:, :, :], m[:, ds(b * 2, 2), :], 1.0, 1.0e8,
                                          ALU.subtract, ALU.mult).then_inc(neg_done, 1)
                        dve.wait_ge(neg_done, b + 1)
                    for n in range(NH):
                        maximum(b, p, n, first)
                        step(b, p, n, first)
                        if n == LAG + 4 and not first:
                            finish(b)
                looped(dve, body)
                for n in range(NH, NH + LAG + 2):
                    step(B - 1, 1, n, False)
                finish(B)


def ffn_stage(c):
    nc = c.nc
    TB = CH // P
    NB = NT // TB
    with Stage(c, "ffn") as s:
        top = s.sb("top", [P, NT])
        unit = s.sb("unit", [P, NT])
        inv = s.sb("inv", [P, NT])
        s_gate = s.sb("s_gate", [P, NT])
        s_up = s.sb("s_up", [P, NT])
        xr = s.sb("xr", [P, NT, P])
        xq = s.sb("xq", [P, NT, P], BF16)
        xqT = s.sb("xqT", [P, T], BF16)
        gate = s.sb("gate", [P, 2, F])
        hid = s.sb("hid", [P, 2, F])
        ht = s.sb("ht", [P, 2, 4])
        hr = s.sb("hr", [P, 2, F])
        hq = s.sb("hq", [P, 2, F], BF16)
        hqT = s.sb("hqT", [P, 2, 4, P], BF16)
        y = s.sb("y", [P, 2, P])
        less = s.sb("less", [P, 1])
        (turned, top_done, unit_done, xr_done, xq_done, xq_turned, xqT_done, gu, gate_done, hid_done, ht_top, ht_unit,
         ht_inv, hr_done, hq_done, hq_turned, hqT_done, down, y_done, y_turned, x_done, less_set) = (s.sem(n) for n in (
            "turned top_done unit_done xr_done xq_done xq_turned xqT_done gu gate_done hid_done ht_top ht_unit "
            "ht_inv hr_done hq_done hq_turned hqT_done down y_done y_turned x_done less_set").split())
        norm = Norm(c, *(s.sb(n, [P, T]) for n in ("sq", "lnv", "rstd")))
        FIRST, LAST = 4, NT

        def looped(eng, step):
            for t in range(FIRST):
                step(t, t % 2, t)
            with eng.Fori(FIRST // 2, LAST // 2) as i:
                for p in range(2):
                    step(i * 2 + p, p, FIRST)
            for t in range(LAST, LAST + 3):
                step(t, t % 2, t)

        def has(n, lag):
            return n >= lag and n - lag < NT

        with nc.Block() as block:
            @block.tensor
            def _(pe):
                norm.on_tensor(pe)
                for a in range(NB):
                    for k in range(TB):
                        t = a * TB + k
                        mm = pe.transpose(c.ps[:, a, k * P:(k + 1) * P], c.xn[:, t * P:(t + 1) * P], c.ident[:, :])
                    mm.then_inc(turned, 1)
                for a in range(NB):
                    pe.wait_ge(xq_done, a + 1)
                    for k in range(TB):
                        t = a * TB + k
                        mm = pe.transpose(c.psb(4 + a)[:, k * P:(k + 1) * P], xq[:, t, :], c.identb[:, :])
                    mm.then_inc(xq_turned, 1)
                pe.wait_ge(xqT_done, NB)

                def step(t, p, n):
                    if has(n, 0):
                        if n >= 2:
                            pe.wait_ge(hid_done, t - 1)
                        pe.matmul(c.ps[:, p, :], xqT[:, ds(t * P, P)], c.wguT[:, 0:F], start=True, stop=True).then_inc(gu, 1)
                        pe.matmul(c.ps[:, 2 + p, :], xqT[:, ds(t * P, P)], c.wguT[:, F:2 * F],
                                  start=True, stop=True).then_inc(gu, 1)
                    if has(n, 2):
                        pe.wait_ge(hqT_done, t - 1)
                        if n >= 3:
                            pe.wait_ge(y_done, t - 2)
                        for k in range(4):
                            mm = pe.matmul(c.ps[:, 5, 0:P], hqT[:, p, k, :], c.wdT[:, k, :], start=(k == 0), stop=(k == 3))
                        mm.then_inc(down, 1)
                    if has(n, 3):
                        pe.wait_ge(y_done, t - 2)
                        if n >= 4:
                            pe.wait_ge(x_done, t - 3)
                        pe.transpose(c.ps[:, 6, 0:P], y[:, 1 - p, :], c.ident[:, :]).then_inc(y_turned, 1)
                    if has(n, 1):
                        pe.wait_ge(hq_done, t)
                        if n >= 2:
                            pe.wait_ge(hqT_done, t - 1)
                        for k in range(4):
                            mm = pe.transpose(c.psb(4)[:, k * P:(k + 1) * P], hq[:, 1 - p, k * P:(k + 1) * P], c.identb[:, :])
                        mm.then_inc(hq_turned, 1)
                looped(pe, step)

            @block.scalar
            def _(act):
                norm.on_scalar(act)
                for a in range(NB):
                    act.wait_ge(xq_turned, a + 1)
                    act.activation(xqT[:, a * CH:(a + 1) * CH], c.psb(4 + a)[:, 0:CH], ACT.Copy).then_inc(xqT_done, 1)
                act.wait_ge(less_set, 1)

                def step(t, p, n):
                    if has(n, 0):
                        act.wait_ge(gu, t * 2 + 1)
                        if n >= 2:
                            act.wait_ge(hid_done, t - 1)
                        act.activation(gate[:, p, :], c.ps[:, p, :], ACT.Silu, scale=s_gate[:, ds(t, 1)]).then_inc(gate_done, 1)
                    if has(n, 1):
                        act.wait_ge(hr_done, t)
                        if n >= 3:
                            act.wait_ge(hq_turned, t - 2)
                        act.activation(hq[:, 1 - p, :], hr[:, 1 - p, :], ACT.Identity, bias=less[:, 0:1]).then_inc(hq_done, 1)
                    if has(n, 1):
                        act.wait_ge(hq_turned, t)
                        if n >= 3:
                            act.wait_ge(down, t - 2)
                        act.activation(hqT[:, 1 - p, :, :].rearrange("p k q -> p (k q)"), c.psb(4)[:, 0:F],
                                       ACT.Copy).then_inc(hqT_done, 1)
                    if has(n, 2):
                        act.wait_ge(down, t - 1)
                        if n >= 4:
                            act.wait_ge(y_turned, t - 3)
                        act.activation(y[:, p, :], c.ps[:, 5, 0:P], ACT.Copy, scale=ht[:, p, 3:4]).then_inc(y_done, 1)
                looped(act, step)

            @block.vector
            def _(dve):
                norm.on_vector(dve)
                dve.memset(less[:, :], -ROUND).then_inc(less_set, 1)
                for a in range(NB):
                    dve.wait_ge(turned, a + 1)
                    dve.tensor_reduce(top[:, a * TB:(a + 1) * TB], c.ps[:, a, :].rearrange("p (t d) -> p t d", t=TB),
                                      AX.X, ALU.max, apply_absolute_value=True).then_inc(top_done, 1)
                dve.wait_ge(top_done, NB)
                dve.tensor_scalar(unit[:, :], top[:, :], 1e-5, 1.0 / 127.0, ALU.max, ALU.mult).then_inc(unit_done, 1)
                dve.wait_ge(unit_done, 1)
                dve.reciprocal(inv[:, :], unit[:, :]).then_inc(unit_done, 1)
                dve.tensor_scalar(s_gate[:, :], unit[:, :], c.wmean[:, 0:1], None, ALU.mult).then_inc(unit_done, 1)
                dve.tensor_scalar(s_up[:, :], unit[:, :], c.wmean[:, 1:2], None, ALU.mult).then_inc(unit_done, 1)
                dve.wait_ge(unit_done, 4)
                for a in range(NB):
                    tiles = slice(a * TB, (a + 1) * TB)
                    dve.tensor_tensor(xr[:, tiles, :], c.ps[:, a, :].rearrange("p (t d) -> p t d", t=TB),
                                      inv[:, tiles].unsqueeze(2).broadcast_to([P, TB, P]), ALU.mult).then_inc(xr_done, 1)
                for a in range(NB):
                    tiles = slice(a * TB, (a + 1) * TB)
                    dve.wait_ge(xr_done, a + 1)
                    dve.tensor_scalar(xq[:, tiles, :], xr[:, tiles, :], ROUND, ROUND, ALU.add, ALU.subtract).then_inc(xq_done, 1)

                def step(t, p, n):
                    if has(n, 0):
                        dve.wait_ge(gate_done, t + 1)
                        dve.wait_ge(gu, t * 2 + 2)
                        dve.scalar_tensor_tensor(out=hid[:, p, :], in0=c.ps[:, 2 + p, :], scalar=s_up[:, ds(t, 1)],
                                                 in1=gate[:, p, :], op0=ALU.mult, op1=ALU.mult).then_inc(hid_done, 1)
                    if has(n, 3):
                        dve.wait_ge(y_turned, t - 2)
                        cols = c.xT[:, ds(t * P - 3 * P, P)]
                        dve.tensor_tensor(cols, cols, c.ps[:, 6, 0:P], ALU.add).then_inc(x_done, 1)
                    if has(n, 0):
                        dve.wait_ge(hid_done, t + 1)
                        dve.tensor_reduce(ht[:, p, 0:1], hid[:, p, :], AX.X, ALU.max, apply_absolute_value=True).then_inc(ht_top, 1)
                        dve.wait_ge(ht_top, t + 1)
                        dve.tensor_scalar(ht[:, p, 1:2], ht[:, p, 0:1], 1e-5, 1.0 / 127.0, ALU.max, ALU.mult).then_inc(ht_unit, 1)
                        dve.wait_ge(ht_unit, t + 1)
                        dve.reciprocal(ht[:, p, 2:3], ht[:, p, 1:2]).then_inc(ht_inv, 1)
                        if n >= 2:
                            dve.wait_ge(y_done, t - 1)
                        dve.tensor_scalar(ht[:, p, 3:4], ht[:, p, 1:2], c.wmean[:, 2:3], None, ALU.mult)
                        dve.wait_ge(ht_inv, t + 1)
                        if n >= 2:
                            dve.wait_ge(hq_done, t - 1)
                        dve.tensor_scalar(hr[:, p, :], hid[:, p, :], ht[:, p, 2:3], ROUND, ALU.mult, ALU.add).then_inc(hr_done, 1)
                looped(dve, step)


def mamba_stage(c, g):
    nc = c.nc
    XR = RANK + 2 * NS
    R = 4
    xm = c.xn
    with Stage(c, "ma") as s:
        w_in = s.sb("w_in", [P, 2 * DI])
        cw = s.sb("cw", [P, 2, TAPS])
        cb = s.sb("cb", [P, 2])
        w_x = s.sb("w_x", [P, 2, RANK + 2 * NS])
        w_dt = s.sb("w_dt", [XR, DI])
        dtb = s.sb("dtb", [P, 2])
        A = s.sb("A", [P, 2, NS])
        Al = s.sb("Al", [P, 2, NS])
        Dp = s.sb("Dp", [P, 2])
        dD = s.sb("dD", [P, 2, P])
        w_out = s.sb("w_out", [P, 2, P])
        nw = s.sb("nw", [P, 2])
        sel = s.sb("sel", [3 * 2 * NS, 2 * NS, P], BF16)
        hn = s.sb("hn", [P, T])
        u = s.sb("u", [P, 2, T])
        z = s.sb("z", [P, 2, T])
        bc = s.sb("bc", [3 * 2 * NS, T], BF16)
        dt = s.sb("dt", [P, 2, T])
        dtu = s.sb("dtu", [P, 2, T])
        dA = s.sb("dA", [P, R, HALF])
        hs = s.sb("hs", [P, R, HALF])
        Bs = s.sb("Bs", [P, 2, HALF])
        sq = hs[:, 0:2, :].rearrange("p a l -> p (a l)")
        rstd = hs[:, 2:4, :].rearrange("p a l -> p (a l)")
        xp = hs[0:XR, 0:2, :].rearrange("p a l -> p (a l)")
        left = hs[0:2 * NS, 2:4, :].rearrange("p a l -> p (a l)")

        names = ("early_in mid_in late_in consts zero_rows dd_done a_step a_done xm_ready centred squared "
                 "var_done lnv_done rstd_done scaled hn_ready u_ps z_ps tap_done conv_step conv_done u_done z_done x_ps xp_done "
                 "first_part left_done second_part bc_done dt_ps abs_done relu_done exp_done ln_done dt_done dtu_done "
                 "b_ready bs_done c_ready da_done dbu_done scan_done hc_done y_acc gated out_ps").split()
        (early_in, mid_in, late_in, consts, zero_rows, dd_done, a_step, a_done, xm_ready, centred, squared,
         var_done, lnv_done, rstd_done, scaled, hn_ready, u_ps, z_ps, tap_done, conv_step, conv_done, u_done, z_done, x_ps, xp_done,
         first_part, left_done, second_part, bc_done, dt_ps, abs_done, relu_done, exp_done, ln_done, dt_done, dtu_done,
         b_ready, bs_done, c_ready, da_done, dbu_done, scan_done, hc_done, y_acc, gated, out_ps) = (s.sem(n) for n in names)
        EARLY, MID, LATE = 5 * 16, 3 * 16, 3 * 16
        XM0, BS0, DBU0, HC0, SCAN0, Y0 = 2, 1, 4, 2, 4, 4

        def pair(k, rows=P):
            return c.ps[0:rows, 2 * k:2 * k + 2, :].rearrange("p a l -> p (a l)")

        def half(gt):
            return slice(gt * HALF, (gt + 1) * HALF)

        def load_early(sp, i):
            sp.dma_start(w_in[:, :], g["m_in"][ds(i, 1)].rearrange("a p n -> (a p) n")).then_inc(early_in, 16)
            sp.dma_start(cw[:, :, :], g["m_cw"][ds(i, 1)].rearrange("a (h p) t -> (a p) h t", p=P)).then_inc(early_in, 16)
            sp.dma_start(cb[:, :], g["m_cb"][ds(i, 1)].rearrange("a (h p) -> (a p) h", p=P),
                         allow_slow_non_contiguous=True).then_inc(early_in, 16)
            for k, n in enumerate(("m_nw", "m_nb")):
                sp.dma_start(nw[:, k:k + 1], g[n][ds(i, 1)].rearrange("a p -> p a"),
                             allow_slow_non_contiguous=True).then_inc(early_in, 16)

        def load_mid(sp, i):
            sp.dma_start(w_x[:, :, :], g["m_xw"][ds(i, 1)].rearrange("a (h p) n -> (a p) h n", p=P)).then_inc(mid_in, 16)
            sp.dma_start(w_dt[0:RANK, :], g["m_dw"][ds(i, 1)].rearrange("a p n -> (a p) n")).then_inc(mid_in, 16)
            sp.dma_start(dtb[:, :], g["m_db"][ds(i, 1)].rearrange("a (h p) -> (a p) h", p=P),
                         allow_slow_non_contiguous=True).then_inc(mid_in, 16)

        def load_late(sp, i):
            sp.dma_start(Al[:, :, :], g["m_al"][ds(i, 1)].rearrange("a (h p) n -> (a p) h n", p=P)).then_inc(late_in, 16)
            sp.dma_start(Dp[:, :], g["m_D"][ds(i, 1)].rearrange("a (h p) -> (a p) h", p=P),
                         allow_slow_non_contiguous=True).then_inc(late_in, 16)
            sp.dma_start(w_out[:, :, :], g["m_ow"][ds(i, 1)].rearrange("a (h p) n -> (a p) h n", p=P)).then_inc(late_in, 16)

        with nc.Block() as block:
            @block.sync
            def _(sp):
                load_early(sp, 0)
                load_mid(sp, 0)
                load_late(sp, 0)
                with sp.Fori(1, NBLK) as i:
                    sp.wait_ge(u_done, i * 4)
                    load_early(sp, i)
                    sp.wait_ge(dt_done, i * 4)
                    load_mid(sp, i)
                    sp.wait_ge(xm_ready, i * 2 + XM0)
                    load_late(sp, i)

            @block.gpsimd
            def _(pool):
                pool.memset(dA[:, :, :], 0.0).then_inc(consts, 1)
                pool.memset(sel[:, :, :], 0.0).then_inc(consts, 1)
                for part in range(3):
                    pool.wait_ge(consts, 2 + part)
                    pool.affine_select(out=sel[:, :, :], in_=sel[:, :, :], compare_op=ALU.not_equal, fill=1.0,
                                       base=-2 * NS * part, pattern=[[-1, 2 * NS], [0, P]],
                                       channel_multiplier=1).then_inc(consts, 1)
                pool.sem_inc(dbu_done, DBU0)
                with pool.Fori(0, NBLK) as i:
                    for gt in range(2):
                        if gt == 1:
                            pool.wait_ge(bc_done, i * 2 + 1)
                        pool.wait_ge(first_part, i * 2 + gt + 1)
                        pool.tensor_tensor(left[:, half(gt)], xp[RANK:XR, half(gt)], bc[RANK:XR, half(gt)],
                                           ALU.subtract).then_inc(left_done, 1)
                        pool.wait_ge(second_part, i * 2 + gt + 1)
                        pool.tensor_tensor(bc[2 * NS:4 * NS, half(gt)], left[:, half(gt)], bc[0:2 * NS, half(gt)],
                                           ALU.subtract).then_inc(bc_done, 1)
                    for gt in range(2):
                        with pool.Fori(0, NS // 2) as t:
                            for k in range(4):
                                if k == 0:
                                    pool.wait_ge(bc_done, i * 2 + 2)
                                if k % 2 == 0:
                                    pool.wait_ge(bs_done, i * 2 * NS + t * 2 + gt * NS + k // 2 + 1 + BS0)
                                pool.wait_ge(y_acc, i * 4 * NS + t * 4 + gt * 2 * NS + k + 1)
                                pool.tensor_tensor(hs[:, k, :], dtu[:, k % 2, half(gt)], Bs[:, k // 2, :],
                                                   ALU.mult).then_inc(dbu_done, 1)

            @block.tensor
            def _(pe):
                pe.sem_inc(y_acc, Y0)
                with pe.Fori(0, NBLK) as i:
                    for h in range(4):
                        if h % 2 == 0:
                            pe.wait_ge(xm_ready, i * 2 + XM0 - 1 + h // 2)
                        pe.matmul(c.ps[:, 4 + h, :], c.centre[:, :], xm[:, h * CH:(h + 1) * CH],
                                  start=True, stop=True).then_inc(centred, 1)
                    for h in range(4):
                        pe.wait_ge(squared, i * 4 + h + 1)
                        pe.matmul(c.ps[:, h, :], c.average[:, :], sq[:, h * CH:(h + 1) * CH],
                                  start=True, stop=True).then_inc(var_done, 1)

                    def in_projection(gt, m, col, done):
                        for a in range(2):
                            cols = slice(gt * HALF + a * CH, gt * HALF + (a + 1) * CH)
                            mm = pe.matmul(c.ps[:, 2 * m + a, :], w_in[:, col:col + P], hn[:, cols], start=True, stop=True)
                        mm.then_inc(done, 1)

                    pe.wait_ge(lnv_done, i * 4 + 4)
                    pe.wait_ge(hn_ready, i * 4 + 2)
                    for h in range(2):
                        in_projection(0, h, h * P, u_ps)
                    pe.wait_ge(hn_ready, i * 4 + 4)
                    for h in range(2):
                        in_projection(0, 2 + h, DI + h * P, z_ps)
                    for h in range(2):
                        pe.wait_ge(conv_done, i * 4 + h + 1)
                        in_projection(1, h, h * P, u_ps)
                        pe.wait_ge(z_done, i * 4 + h + 1)
                        in_projection(1, 2 + h, DI + h * P, z_ps)

                    def x_projection(gt):
                        pe.wait_ge(z_done, i * 4 + 3 + gt)
                        for h in range(2):
                            pe.wait_ge(u_done, i * 4 + 2 * gt + h + 1)
                            for a in range(2):
                                cols = slice(gt * HALF + a * CH, gt * HALF + (a + 1) * CH)
                                mm = pe.matmul(c.ps[0:XR, 4 + 2 * gt + a, :], w_x[:, h, :], u[:, h, cols],
                                               start=(h == 0), stop=(h == 1))
                        mm.then_inc(x_ps, 1)

                    def dt_projection(gt, h):
                        pe.wait_ge(xp_done, i * 2 + gt + 1)
                        if gt == 0:
                            pe.wait_ge(conv_done, i * 4 + 3 + h)
                        for a in range(2):
                            cols = slice(gt * HALF + a * CH, gt * HALF + (a + 1) * CH)
                            mm = pe.matmul(c.ps[:, 4 * gt + 2 * h + a, :], w_dt[:, h * P:(h + 1) * P],
                                           xp[:, cols], start=True, stop=True)
                        mm.then_inc(dt_ps, 1)

                    pe.wait_ge(consts, 5)
                    pe.wait_ge(zero_rows, 1)
                    pe.wait_ge(mid_in, i * MID + MID)
                    for gt in range(2):
                        x_projection(gt)
                        for h in range(2):
                            dt_projection(gt, h)
                    pe.wait_ge(relu_done, i * 4 + 2)
                    pe.wait_ge(bc_done, i * 2 + 2)
                    for gt in range(2):
                        def spread(k, a, done):
                            for q in range(2):
                                mm = pe.matmul(c.ps[:, 2 * a + q, :], k,
                                               bc[:, gt * HALF + q * CH:gt * HALF + (q + 1) * CH],
                                               start=True, stop=True)
                            mm.then_inc(done, 1)

                        def spread_b(n, state):
                            pe.wait_ge(bs_done, state + BS0)
                            spread(sel[:, ds(n, 1), :].rearrange("p a q -> p (a q)"), 0, b_ready)

                        def spread_c(n, state):
                            pe.wait_ge(hc_done, state * 2 + HC0)
                            spread(sel[:, ds(n + NS, 1), :].rearrange("p a q -> p (a q)"), 1, c_ready)

                        def sum_y(slot, item):
                            pe.wait_ge(hc_done, item + 1 + HC0)
                            for q in range(2):
                                mm = pe.matmul(c.ps[:, 4 + 2 * (slot % 2) + q, :], c.ident[:, :],
                                               hs[:, slot, q * CH:(q + 1) * CH], start=False, stop=False,
                                               skip_group_check=True)
                            mm.then_inc(y_acc, 1)

                        first = i * 2 * NS + gt * NS
                        spread_b(0, first)
                        spread_b(1, first + 1)
                        spread_c(0, first)
                        if gt == 0:
                            pe.wait_ge(relu_done, i * 4 + 4)
                            pe.wait_ge(dd_done, i * 2 + 2)
                        else:
                            pe.wait_ge(gated, i * 4 + 2)
                        for h in range(2):
                            for a in range(2):
                                cols = slice(gt * HALF + a * CH, gt * HALF + (a + 1) * CH)
                                pe.matmul(c.ps[:, 4 + 2 * h + a, :], dD[:, h, :], u[:, h, cols], start=True, stop=False,
                                          skip_group_check=True)
                        with pe.Fori(0, NS // 2 - 1) as t:
                            for p in range(2):
                                state = i * 2 * NS + t * 2 + gt * NS + 1 + p
                                slot = 2 * p
                                spread_b(t * 2 + 2 + p, state + 1)
                                sum_y(slot, i * 4 * NS + t * 4 + gt * 2 * NS + 2 * p)
                                spread_c(t * 2 + 1 + p, state)
                                sum_y(slot + 1, i * 4 * NS + t * 4 + gt * 2 * NS + 2 * p + 1)
                        item = i * 4 * NS + gt * 2 * NS + 2 * (NS - 2)
                        sum_y(0, item)
                        spread_c(NS - 1, first + NS - 1)
                        sum_y(1, item + 1)
                        sum_y(2, item + 2)
                        sum_y(3, item + 3)
                    for gt in range(2):
                        if gt == 0:
                            pe.wait_ge(hc_done, i * 4 * NS + 4 * NS + HC0)
                        else:
                            pe.wait_ge(gated, i * 4 + 4)
                        for a in range(2):
                            cols = slice(gt * HALF + a * CH, gt * HALF + (a + 1) * CH)
                            for h in range(2):
                                mm = pe.matmul(c.ps[:, 2 * gt + a, :], w_out[:, h, :], z[:, h, cols],
                                               start=(h == 0), stop=(h == 1))
                        mm.then_inc(out_ps, 1)

            @block.scalar
            def _(act):
                act.sem_inc(bs_done, BS0)
                with act.Fori(0, NBLK) as i:
                    for h in range(4):
                        act.wait_ge(centred, i * 4 + h + 1)
                        act.activation(sq[:, h * CH:(h + 1) * CH], c.ps[:, 4 + h, :], ACT.Square).then_inc(squared, 1)
                    for h in range(4):
                        act.wait_ge(var_done, i * 4 + h + 1)
                        act.activation(rstd[:, h * CH:(h + 1) * CH], c.ps[:, h, :], ACT.Ln,
                                       bias=c.eps[:, 0:1]).then_inc(lnv_done, 1)
                    for h in range(4):
                        act.wait_ge(lnv_done, i * 4 + h + 1)
                        act.activation(rstd[:, h * CH:(h + 1) * CH], rstd[:, h * CH:(h + 1) * CH], ACT.Exp,
                                       scale=-0.5).then_inc(rstd_done, 1)
                    act.wait_ge(late_in, i * LATE + LATE)
                    act.activation(A[:, :, :], Al[:, :, :], ACT.Exp).then_inc(a_step, 1)
                    act.wait_ge(a_step, i + 1)
                    act.activation(A[:, :, :], A[:, :, :], ACT.Copy, scale=-1.0).then_inc(a_done, 1)
                    def gates(gt, h):
                        act.wait_ge(z_ps, i * 4 + 2 * gt + h + 1)
                        act.activation(z[:, h, half(gt)], pair(2 + h), ACT.Silu).then_inc(z_done, 1)

                    def last_tap(gt, h):
                        act.wait_ge(u_ps, i * 4 + 2 * gt + h + 1)
                        act.activation(u[:, h, half(gt)], pair(h), ACT.Copy, scale=cw[:, h, TAPS - 1:TAPS]).then_inc(tap_done, 1)

                    def channels(gt, h):
                        act.wait_ge(conv_done, i * 4 + 2 * gt + h + 1)
                        act.activation(u[:, h, half(gt)], u[:, h, half(gt)], ACT.Silu, bias=cb[:, h:h + 1]).then_inc(u_done, 1)

                    def x_rows(gt):
                        act.wait_ge(x_ps, i * 2 + gt + 1)
                        act.activation(xp[:, half(gt)], pair(2 + gt, XR), ACT.Copy).then_inc(xp_done, 1)
                        act.wait_ge(xp_done, i * 2 + gt + 1)
                        act.activation(bc[RANK:XR, half(gt)], xp[RANK:XR, half(gt)], ACT.Copy).then_inc(first_part, 1)

                    def part_2(gt):
                        act.wait_ge(left_done, i * 2 + gt + 1)
                        act.activation(bc[0:2 * NS, half(gt)], left[:, half(gt)], ACT.Copy).then_inc(second_part, 1)

                    def magnitude(gt, h):
                        act.wait_ge(dt_ps, i * 4 + 2 * gt + h + 1)
                        act.activation(dtu[:, h, half(gt)], pair(2 * gt + h), ACT.Abs, bias=dtb[:, h:h + 1]).then_inc(abs_done, 1)

                    act.wait_ge(early_in, i * EARLY + EARLY)
                    for h in range(2):
                        last_tap(0, h)
                    def exponential(gt, h):
                        act.wait_ge(abs_done, i * 4 + 2 * gt + h + 1)
                        act.activation(dtu[:, h, half(gt)], dtu[:, h, half(gt)], ACT.Exp, scale=-1.0).then_inc(exp_done, 1)

                    for h in range(2):
                        gates(0, h)
                    for h in range(2):
                        last_tap(1, h)
                        channels(0, h)
                        gates(1, h)
                    x_rows(0)
                    for h in range(2):
                        channels(1, h)
                    part_2(0)
                    for h in range(2):
                        magnitude(0, h)
                    x_rows(1)
                    for h in range(2):
                        exponential(0, h)
                    for h in range(2):
                        magnitude(1, h)
                    part_2(1)
                    for h in range(2):
                        exponential(1, h)
                    for k in range(4):
                        gt, h = divmod(k, 2)
                        act.wait_ge(exp_done, i * 4 + k + 1)
                        act.activation(dtu[:, h, half(gt)], dtu[:, h, half(gt)], ACT.Ln, bias=c.one[:, 0:1]).then_inc(ln_done, 1)
                    act.wait_ge(consts, 5)
                    act.wait_ge(a_done, i + 1)
                    for gt in range(2):
                        act.wait_ge(dtu_done, i * 4 + 2 * gt + 2)
                        with act.Fori(0, NS // 2) as t:
                            for k in range(4):
                                item = i * 4 * NS + t * 4 + gt * 2 * NS + k
                                if k % 2 == 0:
                                    act.wait_ge(b_ready, i * 2 * NS + t * 2 + gt * NS + k // 2 + 1)
                                    act.wait_ge(dbu_done, item - 2 + DBU0)
                                    act.activation(Bs[:, k // 2, :], pair(0), ACT.Copy).then_inc(bs_done, 1)
                                act.wait_ge(scan_done, item + 1)
                                d = dA[:, k, :].rearrange("p (b l) -> p b l", l=L)[:, :, 1:L]
                                act.activation(d, dt[:, k % 2, half(gt)].rearrange("p (b l) -> p b l", l=L)[:, :, 1:L],
                                               ACT.Exp, scale=A[:, k % 2, ds(t * 2 + k // 2, 1)]).then_inc(da_done, 1)

            @block.vector
            def _(dve):
                dve.sem_inc(xm_ready, XM0)
                dve.sem_inc(scan_done, SCAN0)
                dve.sem_inc(hc_done, HC0)
                dve.memset(w_dt[RANK:XR, :], 0.0).then_inc(zero_rows, 1)
                with dve.Fori(0, NBLK) as i:
                    dve.wait_ge(late_in, i * LATE + LATE)
                    for h in range(2):
                        dve.tensor_scalar(dD[:, h, :], c.ident[:, :], Dp[:, h:h + 1], None, ALU.mult).then_inc(dd_done, 1)
                    dve.wait_ge(early_in, i * EARLY + EARLY)
                    for h in range(4):
                        x = sq[:, h * CH:(h + 1) * CH]
                        dve.wait_ge(rstd_done, i * 4 + h + 1)
                        dve.tensor_tensor(x, c.ps[:, 4 + h, :], rstd[:, h * CH:(h + 1) * CH], ALU.mult).then_inc(scaled, 1)
                        dve.wait_ge(scaled, i * 4 + h + 1)
                        dve.tensor_scalar(hn[:, h * CH:(h + 1) * CH], x, nw[:, 0:1], nw[:, 1:2],
                                          ALU.mult, ALU.add).then_inc(hn_ready, 1)
                    for k in range(4):
                        gt, h = divmod(k, 2)
                        src = pair(h).rearrange("p (b l) -> p b l", l=L)
                        acc = u[:, h, half(gt)].rearrange("p (b l) -> p b l", l=L)
                        dve.wait_ge(tap_done, i * 4 + k + 1)
                        for e in range(1, TAPS):
                            if e > 1:
                                dve.wait_ge(conv_step, (i * 4 + k) * (TAPS - 2) + e - 1)
                            dve.scalar_tensor_tensor(out=acc[:, :, e:L], in0=src[:, :, 0:L - e],
                                                     scalar=cw[:, h, TAPS - 1 - e:TAPS - e], in1=acc[:, :, e:L],
                                                     op0=ALU.mult, op1=ALU.add).then_inc(
                                                         conv_step if e < TAPS - 1 else conv_done, 1)
                    for k in range(4):
                        gt, h = divmod(k, 2)
                        dve.wait_ge(abs_done, i * 4 + k + 1)
                        dve.tensor_scalar(dt[:, h, half(gt)], pair(k), dtb[:, h:h + 1], 0.0, ALU.add, ALU.max).then_inc(relu_done, 1)
                    for k in range(4):
                        gt, h = divmod(k, 2)
                        d = dt[:, h, half(gt)]
                        dve.wait_ge(relu_done, i * 4 + k + 1)
                        dve.wait_ge(ln_done, i * 4 + k + 1)
                        dve.tensor_tensor(d, d, dtu[:, h, half(gt)], ALU.add).then_inc(dt_done, 1)
                        dve.wait_ge(dt_done, i * 4 + k + 1)
                        dve.tensor_tensor(dtu[:, h, half(gt)], d, u[:, h, half(gt)], ALU.mult).then_inc(dtu_done, 1)
                    for gt in range(2):
                        with dve.Fori(0, NS // 2) as t:
                            for p in range(2):
                                item = i * 4 * NS + t * 4 + gt * 2 * NS + 2 * p
                                for h in range(2):
                                    k = 2 * p + h
                                    dve.wait_ge(da_done, item + h + 1)
                                    dve.wait_ge(dbu_done, item + h + 1 + DBU0)
                                    dve.tensor_tensor_scan(hs[:, k, :], dA[:, k, :], hs[:, k, :], 0.0,
                                                           ALU.mult, ALU.add).then_inc(scan_done, 1)
                                dve.wait_ge(c_ready, i * 2 * NS + t * 2 + gt * NS + p + 1)
                                for h in range(2):
                                    k = 2 * p + h
                                    dve.wait_ge(scan_done, item + h + 1 + SCAN0)
                                    dve.tensor_tensor(hs[:, k, :], hs[:, k, :], pair(1), ALU.mult).then_inc(hc_done, 1)
                        dve.wait_ge(y_acc, i * 4 * NS + (gt + 1) * 2 * NS + Y0)
                        for h in range(2):
                            dve.tensor_tensor(z[:, h, half(gt)], pair(2 + h), z[:, h, half(gt)], ALU.mult).then_inc(gated, 1)
                    for gt in range(2):
                        dve.wait_ge(out_ps, i * 2 + gt + 1)
                        dve.tensor_tensor(xm[:, half(gt)], xm[:, half(gt)], pair(gt), ALU.add).then_inc(xm_ready, 1)


def expert_stage(c):
    nc = c.nc
    xn = c.xn
    with Stage(c, "moe") as s:
        pr = s.sb("pr", [P, NT, NE])
        st = s.sb("st", [P, 3, NT])
        more = s.sb("more", [P, NT, NE, NE])
        same = s.sb("same", [P, NT, NE, NE])
        before = s.sb("before", [P, NE, NE])
        rank = s.sb("rank", [P, NT, NE])
        pick = s.sb("pick", [P, NT, NE])
        pT = s.sb("pT", [NE, T])
        pTb = s.sb("pTb", [NE, T], BF16)
        ebp = s.sb("ebp", [NE, 3, P], BF16)
        ebr = s.sb("ebr", [NE, P])
        sel = s.sb("sel", [NE, NE, P], BF16)
        xe = s.sb("xe", [P, 2, HALF])
        consts, logits, step, exp_done, picked, turned, pT_done, spread, masked, used, acc = (s.sem(x) for x in (
            "consts", "logits", "step", "exp_done", "picked", "turned", "pT_done", "spread", "masked", "used", "acc"))
        out_done, routed, biased = s.sem("out_done"), s.sem("routed"), s.sem("biased")
        part_1, left, part_2, part_3 = s.sem("part_1"), s.sem("left"), s.sem("part_2"), s.sem("part_3")
        NI = 2 * NE
        norm = Norm(c, *(s.sb(n, [P, T]) for n in ("sq", "lnv", "rstd")))

        def pair(k):
            return c.ps[:, 2 * k:2 * k + 2, :].rearrange("p a l -> p (a l)")

        with nc.Block() as block:
            @block.gpsimd
            def _(pool):
                pool.memset(before[:, :, :], 1.0).then_inc(consts, 1)
                pool.memset(sel[:, :, :], 0.0).then_inc(consts, 1)
                pool.wait_ge(consts, 2)
                pool.affine_select(out=before[:, :, :], in_=before[:, :, :], compare_op=ALU.is_gt, fill=0.0, base=0,
                                   pattern=[[1, NE], [-1, NE]], channel_multiplier=0).then_inc(consts, 1)
                pool.affine_select(out=sel[:, :, :], in_=sel[:, :, :], compare_op=ALU.not_equal, fill=1.0, base=0,
                                   pattern=[[-1, NE], [0, P]], channel_multiplier=1).then_inc(consts, 1)
                pool.wait_ge(part_1, 1)
                pool.tensor_tensor(ebr[:, :], c.eb[:, :], ebp[:, 0, :], ALU.subtract).then_inc(left, 1)
                pool.wait_ge(part_2, 1)
                pool.tensor_tensor(ebp[:, 2, :], ebr[:, :], ebp[:, 1, :], ALU.subtract).then_inc(part_3, 1)

            @block.tensor
            def _(pe):
                norm.on_tensor(pe)
                for a in range(4):
                    pe.matmul(c.ps[0:NE, 4 + a, :], c.rwT[:, :], xn[:, a * CH:(a + 1) * CH],
                              start=True, stop=True).then_inc(routed, 1)
                for t in range(NT):
                    if t % 4 == 0:
                        pe.wait_ge(biased, t // 4 + 1)
                    mm = pe.transpose(c.ps[:, 0, t * NE:(t + 1) * NE], pT[:, t * P:(t + 1) * P], c.ident[0:NE, 0:NE])
                mm.then_inc(logits, 1)
                pe.wait_ge(picked, 1)
                for t in range(NT):
                    mm = pe.transpose(c.ps[0:NE, 4 + t // 4, (t % 4) * P:(t % 4 + 1) * P], pick[:, t, :], c.ident[:, :])
                mm.then_inc(turned, 1)
                pe.wait_ge(consts, 4)
                pe.wait_ge(pT_done, 2)
                pe.wait_ge(part_3, 1)
                for a in range(4):
                    for k in range(3):
                        pe.matmul(c.ps[:, 4 + a, :], ebp[:, k, :], pTb[:, a * CH:(a + 1) * CH], start=(k == 0), stop=False,
                                  skip_group_check=True)
                for n in range(NI + 1):
                    if n < NI:
                        gt, e = divmod(n, NE)
                        if n >= 2:
                            pe.wait_ge(masked, n - 1)
                        for a in range(2):
                            mm = pe.matmul(c.ps[:, 2 * (n % 2) + a, :], sel[:, e, :],
                                           pTb[:, gt * HALF + a * CH:gt * HALF + (a + 1) * CH], start=True, stop=True)
                        mm.then_inc(spread, 1)
                    if n >= 1:
                        gt, e = divmod(n - 1, NE)
                        pe.wait_ge(masked, n)
                        for a in range(2):
                            mm = pe.matmul(c.ps[:, 4 + 2 * gt + a, :], c.ewT[:, e, :],
                                           xe[:, (n - 1) % 2, a * CH:(a + 1) * CH], start=False, stop=(e == NE - 1),
                                           skip_group_check=True)
                        mm.then_inc(acc, 1)

            @block.scalar
            def _(act):
                norm.on_scalar(act)
                for a in range(4):
                    act.wait_ge(routed, a + 1)
                    act.activation(pT[:, a * CH:(a + 1) * CH], c.ps[0:NE, 4 + a, :], ACT.Identity,
                                   bias=c.rb[:, 0:1]).then_inc(biased, 1)
                act.wait_ge(step, 2)
                act.activation(pr[:, :, :], pr[:, :, :], ACT.Exp).then_inc(exp_done, 1)
                act.activation(ebp[:, 0, :], c.eb[:, :], ACT.Copy).then_inc(part_1, 1)
                act.wait_ge(left, 1)
                act.activation(ebp[:, 1, :], ebr[:, :], ACT.Copy).then_inc(part_2, 1)
                act.wait_ge(turned, 1)
                act.activation(pTb[:, HALF:T], c.ps[0:NE, 6:8, :].rearrange("p a l -> p (a l)"), ACT.Copy).then_inc(pT_done, 1)

            @block.vector
            def _(dve):
                norm.on_vector(dve)
                def each(x):
                    return x.unsqueeze(2).broadcast_to([P, NT, NE])
                lg = c.ps[:, 0, 0:NT * NE].rearrange("p (t e) -> p t e", e=NE)
                dve.wait_ge(logits, 1)
                dve.tensor_reduce(st[:, 0, :], lg, AX.X, ALU.max).then_inc(step, 1)
                dve.wait_ge(step, 1)
                dve.tensor_tensor(pr[:, :, :], lg, each(st[:, 0, :]), ALU.subtract).then_inc(step, 1)
                dve.wait_ge(exp_done, 1)
                dve.tensor_reduce(st[:, 1, :], pr[:, :, :], AX.X, ALU.add).then_inc(step, 1)
                dve.wait_ge(step, 3)
                dve.reciprocal(st[:, 2, :], st[:, 1, :]).then_inc(step, 1)
                dve.wait_ge(step, 4)
                dve.tensor_tensor(pr[:, :, :], pr[:, :, :], each(st[:, 2, :]), ALU.mult).then_inc(step, 1)
                dve.wait_ge(step, 5)
                dve.wait_ge(consts, 4)
                mine = pr[:, :, :].unsqueeze(3).broadcast_to([P, NT, NE, NE])
                other = pr[:, :, :].unsqueeze(2).broadcast_to([P, NT, NE, NE])
                dve.tensor_tensor(more[:, :, :, :], other, mine, ALU.is_gt).then_inc(step, 1)
                dve.tensor_tensor(same[:, :, :, :], other, mine, ALU.is_equal).then_inc(step, 1)
                dve.wait_ge(step, 7)
                flat = same[:, :, :, :].rearrange("p t e j -> p t (e j)")
                dve.tensor_tensor(flat, flat, before[:, :, :].rearrange("p e j -> p (e j)").unsqueeze(1)
                                  .broadcast_to([P, NT, NE * NE]), ALU.mult).then_inc(step, 1)
                dve.wait_ge(step, 8)
                dve.tensor_tensor(more[:, :, :, :], more[:, :, :, :], same[:, :, :, :], ALU.add).then_inc(step, 1)
                dve.wait_ge(step, 9)
                dve.tensor_reduce(rank[:, :, :], more[:, :, :, :], AX.X, ALU.add).then_inc(step, 1)
                dve.wait_ge(step, 10)
                dve.tensor_scalar(pick[:, :, :], rank[:, :, :], 1.5, None, ALU.is_lt).then_inc(picked, 1)
                dve.wait_ge(turned, 1)
                dve.tensor_copy(pTb[:, 0:HALF], c.ps[0:NE, 4:6, :].rearrange("p a l -> p (a l)")).then_inc(pT_done, 1)
                for n in range(NI):
                    gt = n // NE
                    dve.wait_ge(spread, n + 1)
                    if n >= 2:
                        dve.wait_ge(acc, n - 1)
                    dve.tensor_tensor(xe[:, n % 2, :], xn[:, gt * HALF:(gt + 1) * HALF], pair(n % 2),
                                      ALU.mult).then_inc(masked, 1)
                dve.wait_ge(acc, NI)
                for gt in range(2):
                    cols = slice(gt * HALF, (gt + 1) * HALF)
                    dve.tensor_tensor(c.xT[:, cols], c.xT[:, cols], pair(2 + gt), ALU.add).then_inc(out_done, 1)


def store_stage(c, g):
    nc = c.nc
    with Stage(c, "store") as s:
        o = s.sb("o", [P, NT, P])
        turned, copied, stored = s.sem("turned"), s.sem("copied"), s.sem("stored")
        out = g["out"].rearrange("b (t p) d -> p (b t) d", p=P)
        with nc.Block() as block:
            @block.tensor
            def _(pe):
                for n in range(4):
                    for k in range(4):
                        t = 4 * n + k
                        mm = pe.transpose(c.ps[:, n, k * P:(k + 1) * P], c.xT[:, t * P:(t + 1) * P], c.ident[:, :])
                    mm.then_inc(turned, 1)

            @block.vector
            def _(dve):
                for n in range(4):
                    dve.wait_ge(turned, n + 1)
                    dve.tensor_copy(o[:, 4 * n:4 * n + 4, :], c.ps[:, n, :].rearrange("p (k d) -> p k d", k=4)).then_inc(copied, 1)

            @block.sync
            def _(sp):
                for n in range(4):
                    sp.wait_ge(copied, n + 1)
                    sp.dma_start(out[:, 4 * n:4 * n + 4, :], o[:, 4 * n:4 * n + 4, :]).then_inc(stored, 16)
                sp.wait_ge(stored, 64)


def decoder_kernel(nc, g):
    with ExitStack() as ctx:
        c = Chip(nc, ctx)
        c.ps = ctx.enter_context(nc.psum_tensor("ps", [P, 8, CH], F32))
        c.xT = c.sb("xT", [P, T])
        c.cT = c.sb("cT", [P, T])
        c.xn = c.sb("xn", [P, T])
        c.norm_sems = [ctx.enter_context(nc.semaphore(f"norm_{n}")) for n in ("centred", "squared", "var_done", "lnv_done", "rstd_done",
                                                    "scaled", "done")]
        c.norms = 0
        c.small_in = ctx.enter_context(nc.semaphore("small_in"))
        with ExitStack() as layer0:
            c.ctx = ctx
            c.ewT = c.sb("ewT", [P, NE, P])
            c.rwT = c.sb("rwT", [P, NE])
            c.rb = c.sb("rb", [NE, 1])
            c.eb = c.sb("eb", [NE, P])
            c.wmean = c.sb("wmean", [P, 3])
            c.fn = c.sb("fn", [P, 2])
            constants(c)
            c.ctx = layer0
            c.wvo = c.sb("wvo", [P, 4, P])
            c.wqk = c.sb("wqk", [P, 4, P])
            c.bqk = c.sb("bqk", [P, 2])
            c.bv = c.sb("bv", [P, 1])
            c.bo = c.sb("bo", [P, 1])
            c.maskrow = c.sb("maskrow", [P, B, L], BF16)
            c.present = c.sb("present", [P, B])
            c.wguT = c.sb("wguT", [P, 2 * F], BF16)
            c.wdT = c.sb("wdT", [P, 4, P], BF16)
            borrowed = ExitStack()
            c.whole = borrowed
            load_stage(c, g)
            linear_attention_stage(c)
            c.whole = ctx
            cleared = list(c.made)
            cross_attention_stage(c, "x0", P // NH, False, (c.wqk[:, 2, :], c.wqk[:, 3, :], c.wvo[:, 2, :], c.wvo[:, 3, :]))
            ffn_stage(c)
        norm_stage(c, "n4", c.xT, c.xn)
        mamba_stage(c, g)
        c.ctx = ctx
        W = NH * 64
        x1w = [c.sb(f"x1_{n}", [P, W]) for n in ("wq", "wk", "wv", "wo")]
        c.mask1 = c.sb("x1_m", [P, NT, L])
        c.w1_in, c.mask1_in = (ctx.enter_context(nc.semaphore(n)) for n in ("x1_w_in", "x1_mask_in"))

        def prefetch(sp):
            for w, n in zip(x1w, ("x1q", "x1k", "x1v")):
                sp.dma_start(w[:, :].rearrange("e (n d) -> e n d", d=64), g[n].rearrange("n e d -> e n d")).then_inc(c.w1_in, 16)
            sp.dma_start(x1w[3][:, :].rearrange("p (g e) -> p g e", e=P),
                         g["x1o"].rearrange("(g a) d e -> (a d) g e", a=2)).then_inc(c.w1_in, 16)
            sp.dma_start(c.mask1[:, :, :], g["m1"].rearrange("b (t p) k -> p (b t) k", p=P)).then_inc(c.mask1_in, 16)

        norm_stage(c, "n5", c.xn, None, c.fn[:, 0:1], c.fn[:, 1:2], c.xT, prefetch, cleared)
        borrowed.close()
        cross_attention_stage(c, "x1", 64, True, x1w)
        expert_stage(c)
        store_stage(c, g)


_NAMES = {
    "x": "x", "ctx_1024": "ctx", "mask_BxS2_ik0": "m0", "mask_BxSxS2_fk1": "m1",
    "L0_attn_Wq": "aq", "L0_attn_Wk": "ak", "L0_attn_Wv": "av", "L0_attn_Wo": "ao",
    "L0_xattn_Wq": "xq", "L0_xattn_bq": "xbq", "L0_xattn_Wk": "xk", "L0_xattn_bk": "xbk",
    "L0_xattn_Wv": "xv", "L0_xattn_bv": "xbv", "L0_xattn_Wo": "xo", "L0_xattn_bo": "xbo",
    "L0_ffn_w_gate": "wg", "L0_ffn_w_up": "wu", "L0_ffn_w_down": "wd",
    "L1_attn_norm_w": "m_nw", "L1_attn_norm_b": "m_nb", "L1_attn_in_proj_w": "m_in", "L1_attn_conv_w": "m_cw",
    "L1_attn_conv_b": "m_cb", "L1_attn_xproj_w": "m_xw", "L1_attn_dtproj_w": "m_dw", "L1_attn_dtproj_b": "m_db",
    "L1_attn_A_log": "m_al", "L1_attn_skip_D": "m_D", "L1_attn_out_proj_w": "m_ow", "L1_attn_fn_w": "m_fw",
    "L1_attn_fn_b": "m_fb", "L1_xattn_w_q": "x1q", "L1_xattn_w_k": "x1k", "L1_xattn_w_v": "x1v",
    "L1_xattn_w_o": "x1o", "L1_ffn_router_w": "rw", "L1_ffn_router_b": "rb", "L1_ffn_expert_w": "ew",
    "L1_ffn_expert_b": "eb",
}


def kernel(**inputs):
    import numpy as _np
    import concourse.bacc as _bacc
    from concourse import mybir as _mybir
    from concourse.bass_utils import run_bass_kernel_spmd as _run

    nc = _bacc.Bacc("TRN2", target_bir_lowering=False, num_devices=1)
    arrays, g = {}, {}
    for name, short in _NAMES.items():
        a = _np.ascontiguousarray(inputs[name])
        arrays[f"in_{name}_dram"] = a
        g[short] = nc.dram_tensor(f"in_{name}_dram", a.shape, _mybir.dt.from_np(a.dtype), kind="ExternalInput").ap()
    g["out"] = nc.dram_tensor("out_0_dram", (B, L, P), _mybir.dt.float32, kind="ExternalOutput").ap()
    decoder_kernel(nc, g)
    r = _run(nc, [arrays], core_ids=[0])
    return r.results[0]["out_0_dram"]
```
